# Optimizing a Trainium2 kernel written in Bass

```python
import numpy as np
import jax
import jax.numpy as jnp

def _softmax(x, axis=-1):
    return jax.nn.softmax(x, axis=axis)

def _gelu(x):
    return jax.nn.gelu(x, approximate=True)

def _silu(x):
    return jax.nn.silu(x)

def _sigmoid(x):
    return jax.nn.sigmoid(x)

def _layernorm(x, axis=-1, eps=1e-05):
    m = jnp.mean(x, axis=axis, keepdims=True)
    v = jnp.var(x, axis=axis, keepdims=True)
    return (x - m) / jnp.sqrt(v + eps)

def _scatter_add(tgt, idx, src, axis=0):
    return tgt.at[idx].add(src)

def _segment_sum(src, seg, n):
    return jax.ops.segment_sum(src, seg, n)
kernel_name = 'mk_gnn_ffn_d1_gnn_r8_2c04f7'

def setup_inputs(seed: int=0):
    np.random.seed(seed)
    _w = jnp.asarray

    def _rec_inputs():
        import jax
        import jax.numpy as jnp
        _gk = jax.random.key(seed)
        x = -0.0002117 + 1 * jax.random.normal(jax.random.fold_in(_gk, 1), (6250, 256), jnp.float32)
        src = jax.random.randint(jax.random.fold_in(_gk, 2), (200000,), 0, 6250, jnp.int32)
        dst = jax.random.randint(jax.random.fold_in(_gk, 3), (200000,), 0, 6250, jnp.int32)
        _o = jnp.argsort(dst, stable=True)
        src = src[_o]
        dst = dst[_o]
        return (x, src, dst)
    x, src, dst = _rec_inputs()

    def _L0_gnn_setup():
        import jax, jax.numpy as jnp
        import numpy as np
        N_NODES = 12500
        N_EDGES = 200000
        HIDDEN = 256
        N_LAYERS = 2
        key = jax.random.key(seed)
        k = jax.random.split(key, 7)
        x = jax.random.normal(k[0], (N_NODES, HIDDEN), dtype=jnp.float32)
        edge_index = jax.random.randint(k[1], (2, N_EDGES), 0, N_NODES, dtype=jnp.int64)
        s = 1.0 / np.sqrt(HIDDEN)
        W = jax.random.uniform(k[2], (N_LAYERS, HIDDEN, HIDDEN), jnp.float32, -s, s)
        b = jax.random.uniform(k[3], (N_LAYERS, HIDDEN), jnp.float32, -s, s)
        resW = jax.random.uniform(k[4], (HIDDEN, HIDDEN), jnp.float32, -s, s)
        resb = jax.random.uniform(k[5], (HIDDEN,), jnp.float32, -s, s)
        return {'x': x, 'edge_index': edge_index, 'W': W, 'b': b, 'resW': resW, 'resb': resb}
    _L0_gnn_all = _L0_gnn_setup()
    _L0_gnn_in = {k: v for k, v in _L0_gnn_all.items() if k in ('W', 'b', 'resW', 'resb')}
    del _L0_gnn_all

    def _L0_ffn_setup():
        import jax, jax.numpy as jnp
        import numpy as np
        E, D, H, TOP_K = (6, 256, 256, 2)
        ROUTER_H = D // 2
        key = jax.random.key(seed)
        ks = jax.random.split(key, 12)
        s = 1.0 / np.sqrt(D)
        sh = 1.0 / np.sqrt(H)
        sr = 1.0 / np.sqrt(ROUTER_H)
        return {'features': jax.random.normal(ks[0], (8, 512, D), dtype=jnp.float32), 'router_w1': jax.random.uniform(ks[1], (D, ROUTER_H), jnp.float32, -s, s), 'router_b1': jnp.zeros((ROUTER_H,), jnp.float32), 'router_w2': jax.random.uniform(ks[2], (ROUTER_H, E), jnp.float32, -sr, sr), 'router_b2': jnp.zeros((E,), jnp.float32), 'expert_w1': jax.random.uniform(ks[3], (E, D, H), jnp.float32, -s, s), 'expert_b1': jnp.zeros((E, H), jnp.float32), 'expert_w2': jax.random.uniform(ks[4], (E, H, H), jnp.float32, -sh, sh), 'expert_b2': jnp.zeros((E, H), jnp.float32), 'expert_w3': jax.random.uniform(ks[5], (E, H, D), jnp.float32, -sh, sh), 'expert_b3': jnp.zeros((E, D), jnp.float32)}
    _L0_ffn_all = _L0_ffn_setup()
    _L0_ffn_in = {k: v for k, v in _L0_ffn_all.items() if k in ('router_w1', 'router_b1', 'router_w2', 'router_b2', 'expert_w1', 'expert_b1', 'expert_w2', 'expert_b2', 'expert_w3', 'expert_b3')}
    del _L0_ffn_all
    return {'x': x, 'src': src, 'dst': dst, 'L0_gnn_W': _L0_gnn_in['W'], 'L0_gnn_b': _L0_gnn_in['b'], 'L0_gnn_resW': _L0_gnn_in['resW'], 'L0_gnn_resb': _L0_gnn_in['resb'], 'L0_ffn_router_w1': _L0_ffn_in['router_w1'], 'L0_ffn_router_b1': _L0_ffn_in['router_b1'], 'L0_ffn_router_w2': _L0_ffn_in['router_w2'], 'L0_ffn_router_b2': _L0_ffn_in['router_b2'], 'L0_ffn_expert_w1': _L0_ffn_in['expert_w1'], 'L0_ffn_expert_b1': _L0_ffn_in['expert_b1'], 'L0_ffn_expert_w2': _L0_ffn_in['expert_w2'], 'L0_ffn_expert_b2': _L0_ffn_in['expert_b2'], 'L0_ffn_expert_w3': _L0_ffn_in['expert_w3'], 'L0_ffn_expert_b3': _L0_ffn_in['expert_b3']}

def reference(x, src, dst, L0_gnn_W, L0_gnn_b, L0_gnn_resW, L0_gnn_resb, L0_ffn_router_w1, L0_ffn_router_b1, L0_ffn_router_w2, L0_ffn_router_b2, L0_ffn_expert_w1, L0_ffn_expert_b1, L0_ffn_expert_w2, L0_ffn_expert_b2, L0_ffn_expert_w3, L0_ffn_expert_b3):
    import jax
    import jax.numpy as jnp

    def _L0_gnn_ref(x, edge_index, W, b, resW, resb):
        import jax, jax.numpy as jnp
        import numpy as np
        N_NODES = 12500
        N_EDGES = 200000
        HIDDEN = 256
        N_LAYERS = 2
        N = x.shape[0]
        loop = jnp.arange(N, dtype=edge_index.dtype)
        src = jnp.concatenate([edge_index[0], loop])
        dst = jnp.concatenate([edge_index[1], loop])
        ew = jnp.ones(src.shape[0], dtype=x.dtype)
        deg = jax.ops.segment_sum(ew, dst, num_segments=N)
        dis = jnp.where(deg > 0, jax.lax.rsqrt(jnp.where(deg > 0, deg, 1.0)), 0.0)
        norm = dis[src] * ew * dis[dst]
        for l in range(W.shape[0]):
            x_res = x
            h = x @ W[l]
            msg = norm[:, None] * h[src]
            agg = jax.ops.segment_sum(msg, dst, num_segments=N) + b[l]
            x = jax.nn.relu(agg + x_res @ resW + resb)
        return x

    def _L0_ffn_ref(features, router_w1, router_b1, router_w2, router_b2, expert_w1, expert_b1, expert_w2, expert_b2, expert_w3, expert_b3):
        import jax, jax.numpy as jnp
        import numpy as np
        E, D, H, TOP_K = (6, 256, 256, 2)
        ROUTER_H = D // 2
        rh = jax.nn.relu(features @ router_w1 + router_b1)
        expert_logits = jax.nn.softmax(rh @ router_w2 + router_b2, axis=-1)
        top_w, top_i = jax.lax.top_k(expert_logits, TOP_K)
        routing_weights = jax.nn.softmax(top_w, axis=-1)
        h1 = jax.nn.relu(jnp.einsum('bsd,edh->bseh', features, expert_w1) + expert_b1)
        h2 = jax.nn.relu(jnp.einsum('bseh,ehf->bsef', h1, expert_w2) + expert_b2)
        expert_out = jnp.einsum('bsef,efo->bseo', h2, expert_w3) + expert_b3
        sel = jnp.take_along_axis(expert_out, top_i[:, :, :, None], axis=2)
        combined = jnp.sum(sel * routing_weights[..., None], axis=2)
        return combined
    edge_index = jnp.stack([src, dst])
    x = x + _L0_gnn_ref(_layernorm(x, axis=-1), edge_index, L0_gnn_W, L0_gnn_b, L0_gnn_resW, L0_gnn_resb)
    x = x + _L0_ffn_ref(_layernorm(x, axis=-1)[None], L0_ffn_router_w1, L0_ffn_router_b1, L0_ffn_router_w2, L0_ffn_router_b2, L0_ffn_expert_w1, L0_ffn_expert_b1, L0_ffn_expert_w2, L0_ffn_expert_b2, L0_ffn_expert_w3, L0_ffn_expert_b3)[0]
    return x

_drawn_inputs = setup_inputs


def setup_inputs(seed=0):
    import zlib

    import numpy as np

    out = dict(_drawn_inputs(seed))
    spreads = {'L0_ffn_router_b1': (0.0, 0.1),
     'L0_ffn_router_b2': (0.0, 0.1),
     'L0_ffn_expert_b1': (0.0, 0.692),
     'L0_ffn_expert_b2': (0.0, 0.294),
     'L0_ffn_expert_b3': (0.0, 0.1)}
    factors = {}
    for name, (base, spread) in spreads.items():
        noise = np.random.default_rng([zlib.crc32(name.encode()), seed]).standard_normal(out[name].shape)
        drawn = base * np.exp(spread * noise) if base else spread * noise
        out[name] = jnp.asarray(drawn.astype(out[name].dtype))
    for name, factor in factors.items():
        out[name] = (out[name] * factor).astype(out[name].dtype)
    return out
```

```python
from contextlib import ExitStack

import concourse.bass as bass
from concourse import mybir

P = 128
F32 = mybir.dt.float32
BF16 = mybir.dt.bfloat16
I32 = mybir.dt.int32
U32 = mybir.dt.uint32
ALU = mybir.AluOpType
ACT = mybir.ActivationFunctionType
AX = mybir.AxisListType.X
EPS = 1e-5
FAR = 16384


class Link:

    def __init__(self, engine, sem):
        self.engine, self.sem, self.count, self.trip = engine, sem, 0, None

    def loop(self, i, per):
        self.trip, self.per, self.start = i, per, self.count

    def end(self, trips):
        assert self.count - self.start == self.per, (self.count - self.start)
        self.count = self.start + self.per * trips
        self.trip = None

    def __call__(self, ins):
        ins.then_inc(self.sem, 1)
        self.count += 1
        self.engine.wait_ge(self.sem, self.count + self.trip * self.per if self.trip is not None else self.count)


def gnn_moe_kernel(nc, x, src, dst, gnn_w, gnn_b, res_w, res_b, router_w1, router_b1, router_w2, router_b2,
                   expert_w1, expert_b1, expert_w2, expert_b2, expert_w3, expert_b3, out):
    nodes, dim = x.shape
    edges = src.shape[0]
    layers = gnn_w.shape[0]
    experts = expert_w1.shape[0]
    router_h = router_w1.shape[1]
    tiles = -(-nodes // P)
    padded = tiles * P
    last_rows = nodes - (tiles - 1) * P
    cols = -(-edges // P)
    last_cols = edges - (P - 1) * cols
    K2 = dim // P
    GROUP = 7
    groups = tiles // GROUP
    HALF = GROUP * P // 2
    assert tiles % GROUP == 0 and router_h == P and dim == 2 * P and cols % 3 == 0

    ctx = ExitStack()
    with ctx:
        scopes = [ctx]

        def sb(name, shape, dt):
            return scopes[-1].enter_context(nc.sbuf_tensor(name, shape, dt))

        def open_scope():
            scopes.append(ExitStack())

        def close_scope():
            scopes.pop().close()

        def psum(name):
            return ctx.enter_context(nc.psum_tensor(name, [P, 512], F32))

        def sem(name):
            return ctx.enter_context(nc.semaphore(name))

        feat = sb("feat", [P, tiles, dim], F32)
        iota_row = sb("iota_row", [P, P], BF16)
        ident = sb("ident", [P, P], F32)
        lower = sb("lower", [P, P], F32)
        ones_row = sb("ones_row", [1, P], F32)
        stats = sb("stats", [P, tiles, 6], F32)
        ln_a = sb("ln_a", [P, tiles], F32)
        ln_d = sb("ln_d", [P, tiles], F32)
        ln_s = sb("ln_s", [P, tiles], F32)
        mean = sb("mean", [P, tiles], F32)
        rstd = sb("rstd", [P, tiles], F32)
        eps_col = sb("eps_col", [P, 1], F32)
        dis = sb("dis", [P, tiles], F32)
        scaled = sb("scaled", [P, 2, dim], F32)
        gnn_w_sb = sb("gnn_w_sb", [P, layers, K2, dim], F32)
        res_w_sb = sb("res_w_sb", [P, K2, dim], F32)
        bias_rows = sb("bias_rows", [1, layers + 1, dim], F32)
        bias_sum = sb("bias_sum", [1, layers, dim], F32)
        router_w1_sb = sb("router_w1_sb", [P, K2, router_h], F32)
        router_b1_sb = sb("router_b1_sb", [P, 1], F32)
        router_w2_sb = sb("router_w2_sb", [P, experts], F32)
        router_b2_sb = sb("router_b2_sb", [1, experts], F32)
        w1_sb = sb("w1_sb", [P, experts, K2, dim], F32)
        w2_sb = sb("w2_sb", [P, experts, K2, dim], F32)
        w3_sb = sb("w3_sb", [P, experts, K2, dim], F32)
        b1_sb = sb("b1_sb", [P, experts, K2], F32)
        b2_sb = sb("b2_sb", [P, experts, K2], F32)
        b3_sb = sb("b3_sb", [1, experts, dim], F32)

        hs_table = [nc.dram_tensor(f"hs_table{l}", (padded, dim), F32).ap() for l in range(layers)]
        feat_table = [nc.dram_tensor(f"feat_table{l}", (padded, dim), F32).ap() for l in range(layers)]
        agg_table = [nc.dram_tensor(f"agg_table{l}", (padded, dim), F32).ap() for l in range(layers)]

        bank = [psum(f"bank{i}") for i in range(8)]

        def rows_of(table, n):
            return table.rearrange("(t p) d -> p t d", p=P)

        open_scope()
        src_sb = sb("src_sb", [P, cols], I32)
        dst_sb = sb("dst_sb", [P, cols], I32)
        open_scope()
        key_i = sb("key_i", [P, cols], I32)
        dst_lo = sb("dst_lo", [P, cols], F32)
        dst_hi = sb("dst_hi", [P, cols], F32)
        onehot_lo = sb("onehot_lo", [P, 6, P], BF16)
        onehot_hi = sb("onehot_hi", [P, 6, tiles], BF16)

        x_loaded = sem("x_loaded")
        edges_loaded = sem("edges_loaded")
        gnn_w_loaded = sem("gnn_w_loaded")
        ffn_w_loaded = sem("ffn_w_loaded")
        edges_cleared = sem("edges_cleared")
        feat_cleared = sem("feat_cleared")
        consts_made = sem("consts_made")
        prep_link = sem("prep_link")
        pool_link = sem("pool_link")
        var_ready = sem("var_ready")
        std_ready = sem("std_ready")
        onehots_ready = sem("onehots_ready")
        hist_used = sem("hist_used")
        deg_ready = sem("deg_ready")
        root_ready = sem("root_ready")
        scaled_ready = sem("scaled_ready")
        feat_stored = sem("feat_stored")
        scaled_stored = [sem(f"scaled_stored{b}") for b in range(2)]

        full = (tiles - 1) * P
        with nc.Block() as block:
            @block.sync
            def _(sp):
                sp.wait_ge(edges_cleared, 2)
                for table, tile in ((dst, dst_sb), (src, src_sb)):
                    for a, b in ((0, 112), (112, P - 1)):
                        sp.dma_start(tile[a:b, :], table[a * cols:b * cols].rearrange("(p c) -> p c", c=cols)).then_inc(edges_loaded, 16)
                    sp.dma_start(tile[P - 1:P, 0:last_cols], table[(P - 1) * cols:edges].rearrange("(p c) -> p c", p=1)).then_inc(edges_loaded, 16)
                sp.wait_ge(feat_cleared, 1)
                for t0 in range(0, tiles - 1, 8):
                    sp.dma_start(feat[:, t0:t0 + 8, :], x[t0 * P:(t0 + 8) * P, :].rearrange("(t p) d -> p t d", p=P)).then_inc(x_loaded, 16)
                sp.dma_start(feat[0:last_rows, tiles - 1, :], x[full:nodes, :]).then_inc(x_loaded, 16)
                tab = hs_table[0]
                with sp.Fori(0, tiles) as t:
                    sp.wait_ge(scaled_ready, t + 1)
                    sp.dma_start(tab[bass.ds(t * P, P), :], scaled[:, 0, :]).then_inc(scaled_stored[0], 16)
                sp.dma_start(feat_table[0].rearrange("(t p) d -> p t d", p=P), feat[:, :, :]).then_inc(feat_stored, 16)
                sp.wait_ge(scaled_stored[0], 16 * tiles)
                sp.wait_ge(feat_stored, 16)

            @block.gpsimd
            def _(pool):
                link = Link(pool, pool_link)
                nc.gpsimd.iota(iota_row[:, :], [[1, P]], 0, 0, allow_small_or_imprecise_dtypes=True).then_inc(consts_made, 1)
                link(nc.gpsimd.memset(ident[:, :], 0.0))
                nc.gpsimd.affine_select(out=ident[:, :], in_=ident[:, :], compare_op=ALU.not_equal, fill=1.0,
                                        base=0, pattern=[[-1, P]], channel_multiplier=1).then_inc(consts_made, 1)
                link(nc.gpsimd.memset(lower[:, :], 1.0))
                nc.gpsimd.affine_select(out=lower[:, :], in_=lower[:, :], compare_op=ALU.is_gt, fill=0.0,
                                        base=0, pattern=[[-1, P]], channel_multiplier=1).then_inc(consts_made, 1)

            @block.scalar
            def _(act):
                act.dma_start(gnn_w_sb[:, :, :, :].rearrange("p l k d -> p (l k) d"), gnn_w.rearrange("l (k p) d -> p (l k) d", p=P)).then_inc(gnn_w_loaded, 16)
                act.dma_start(res_w_sb[:, :, :], res_w.rearrange("(k p) d -> p k d", p=P)).then_inc(gnn_w_loaded, 16)
                act.dma_start(bias_rows[:, 0:layers, :], gnn_b.rearrange("(a l) d -> a l d", a=1)).then_inc(gnn_w_loaded, 16)
                act.dma_start(bias_rows[:, layers, :], res_b.rearrange("(a d) -> a d", a=1)).then_inc(gnn_w_loaded, 16)
                for tile, w in ((w1_sb, expert_w1), (w2_sb, expert_w2), (w3_sb, expert_w3)):
                    act.dma_start(tile[:, :, :, :].rearrange("p e k d -> p (e k) d"), w.rearrange("e (k p) d -> p (e k) d", p=P)).then_inc(ffn_w_loaded, 16)
                act.dma_start(router_w1_sb[:, :, :], router_w1.rearrange("(k p) d -> p k d", p=P)).then_inc(ffn_w_loaded, 16)
                act.dma_start(router_w2_sb[:, :], router_w2).then_inc(ffn_w_loaded, 16)
                act.dma_start(router_b1_sb[:, :], router_b1.rearrange("(p a) -> p a", a=1)).then_inc(ffn_w_loaded, 16)
                act.dma_start(router_b2_sb[:, :], router_b2.rearrange("(a d) -> a d", a=1)).then_inc(ffn_w_loaded, 16)
                act.dma_start(b3_sb[:, :, :], expert_b3.rearrange("(a e) d -> a e d", a=1)).then_inc(ffn_w_loaded, 16)
                for e in range(experts):
                    for k in range(K2):
                        act.dma_start(b1_sb[:, e, k:k + 1], expert_b1[e, k * P:(k + 1) * P].rearrange("(p a) -> p a", a=1)).then_inc(ffn_w_loaded, 16)
                        act.dma_start(b2_sb[:, e, k:k + 1], expert_b2[e, k * P:(k + 1) * P].rearrange("(p a) -> p a", a=1)).then_inc(ffn_w_loaded, 16)
                act.wait_ge(var_ready, 1)
                nc.scalar.activation(rstd[:, :], ln_s[:, :], ACT.Sqrt, bias=eps_col[:, 0:1], scale=1.0 / dim).then_inc(std_ready, 1)
                act.wait_ge(deg_ready, 1)
                nc.scalar.activation(dis[:, :], bank[0][:, 0:tiles], ACT.Sqrt, bias=1.0).then_inc(root_ready, 1)
                act.wait_ge(gnn_w_loaded, 16 * 4)
                act.wait_ge(ffn_w_loaded, 16 * (8 + 2 * experts * K2))

            @block.tensor
            def _(pe):
                def count(i, base, start, stop):
                    for u in range(3):
                        mm = nc.tensor.matmul(bank[0][:, 0:tiles], onehot_lo[:, base + u, :], onehot_hi[:, base + u, :],
                                              start=start and u == 0, stop=stop and u == 2)
                    mm.then_inc(hist_used, 1)

                pe.wait_ge(onehots_ready, 1)
                count(0, 0, True, False)
                pairs = (cols // 3 - 1) // 2
                with pe.Fori(0, pairs - 1) as i:
                    pe.wait_ge(onehots_ready, 2 * i + 2)
                    count(i, 3, False, False)
                    pe.wait_ge(onehots_ready, 2 * i + 3)
                    count(i, 0, False, False)
                pe.wait_ge(onehots_ready, 2 * pairs)
                count(0, 3, False, False)
                pe.wait_ge(onehots_ready, 2 * pairs + 1)
                for u in range(3):
                    mm = nc.tensor.matmul(bank[0][:, 0:tiles], onehot_lo[:, u, :], onehot_hi[:, u, :], start=False, stop=u == 2)
                mm.then_inc(deg_ready, 1)

            @block.vector
            def _(dve):
                link = Link(dve, prep_link)
                pad = padded - 1
                nc.vector.memset(src_sb[:, :], pad).then_inc(edges_cleared, 1)
                nc.vector.memset(dst_sb[:, :], pad).then_inc(edges_cleared, 1)
                nc.vector.memset(feat[:, tiles - 1, :], 0.0).then_inc(feat_cleared, 1)
                nc.vector.memset(ones_row[:, :], 1.0)
                link(nc.vector.memset(eps_col[:, :], EPS))
                dve.wait_ge(gnn_w_loaded, 16 * 4)
                for l in range(layers):
                    link(nc.vector.tensor_tensor(bias_sum[:, l, :], bias_rows[:, l, :], bias_rows[:, layers, :], ALU.add))
                dve.wait_ge(edges_loaded, 16 * 6)
                link(nc.vector.tensor_scalar(key_i[:, :], dst_sb[:, :], P - 1, None, ALU.bitwise_and))
                link(nc.vector.tensor_copy(dst_lo[:, :], key_i[:, :]))
                link(nc.vector.tensor_scalar(key_i[:, :], dst_sb[:, :], 7, None, ALU.logical_shift_right))
                link(nc.vector.tensor_copy(dst_hi[:, :], key_i[:, :]))
                dve.wait_ge(consts_made, 3)

                def onehots(c, base):
                    for u in range(3):
                        nc.vector.tensor_scalar(onehot_lo[:, base + u, :], iota_row[:, :], dst_lo[:, bass.ds(c + u, 1)], None, ALU.is_equal)
                        last = nc.vector.tensor_scalar(onehot_hi[:, base + u, :], iota_row[:, 0:tiles], dst_hi[:, bass.ds(c + u, 1)], None, ALU.is_equal)
                    last.then_inc(onehots_ready, 1)

                onehots(0, 0)
                onehots(3, 3)
                pairs = (cols // 3 - 1) // 2
                with dve.Fori(0, pairs - 1) as i:
                    dve.wait_ge(hist_used, 2 * i + 1)
                    onehots(i * 6 + 6, 0)
                    dve.wait_ge(hist_used, 2 * i + 2)
                    onehots(i * 6 + 9, 3)
                dve.wait_ge(hist_used, 2 * pairs - 1)
                onehots(cols - 3, 0)

                dve.wait_ge(x_loaded, 16 * ((tiles - 1) // 8 + 1))
                with dve.Fori(0, tiles) as t:
                    nc.vector.bn_stats(stats[:, bass.ds(t, 1), :].rearrange("p a s -> p (a s)"), feat[:, bass.ds(t, 1), :].rearrange("p a d -> p (a d)")).then_inc(prep_link, 1)
                link.count += tiles
                dve.wait_ge(prep_link, link.count)
                st = stats[:, :, :]
                link(nc.vector.tensor_tensor(ln_a[:, :], st[:, :, 1], st[:, :, 4], ALU.add))
                link(nc.vector.tensor_tensor(ln_d[:, :], st[:, :, 1], st[:, :, 4], ALU.subtract))
                link(nc.vector.tensor_tensor(ln_s[:, :], st[:, :, 2], st[:, :, 5], ALU.add))
                link(nc.vector.tensor_tensor(ln_d[:, :], ln_d[:, :], ln_d[:, :], ALU.mult))
                link(nc.vector.tensor_scalar(mean[:, :], ln_a[:, :], 0.5, None, ALU.mult))
                nc.vector.scalar_tensor_tensor(ln_s[:, :], ln_d[:, :], dim / 4.0, ln_s[:, :], ALU.mult, ALU.add).then_inc(var_ready, 1)
                dve.wait_ge(std_ready, 1)
                link(nc.vector.reciprocal(rstd[:, :], rstd[:, :]))
                dve.wait_ge(root_ready, 1)
                link(nc.vector.reciprocal(dis[:, :], dis[:, :]))
                base = link.count

                def normalise(t):
                    ft = feat[:, bass.ds(t, 1), :].rearrange("p a d -> p (a d)")
                    nc.vector.tensor_scalar(ft, ft, mean[:, bass.ds(t, 1)], rstd[:, bass.ds(t, 1)], ALU.subtract, ALU.mult).then_inc(prep_link, 1)
                    dve.wait_ge(prep_link, base + 1 + t)
                    if t is not first:
                        dve.wait_ge(scaled_stored[0], 16 * t)
                    nc.vector.tensor_scalar(scaled[:, 0, :], ft, dis[:, bass.ds(t, 1)], None, ALU.mult).then_inc(scaled_ready, 1)

                first = 0
                normalise(first)
                with dve.Fori(1, tiles) as t:
                    normalise(t)
        close_scope()

        def gather_sum(l):
            index_ready = sem(f"index_ready{l}")
            rows_t_ready = sem(f"rows_t_ready{l}")
            same_ready = sem(f"same_ready{l}")
            count_ready = sem(f"count_ready{l}")
            target_ready = sem(f"target_ready{l}")
            hs_gathered = sem(f"hs_gathered{l}")
            agg_gathered = sem(f"agg_gathered{l}")
            summed = sem(f"summed{l}")
            added = sem(f"added{l}")
            scattered = sem(f"scattered{l}")
            passed = sem(f"passed{l}")
            index = gs_index
            with nc.Block() as block:
                @block.gpsimd
                def _(pool):
                    pool.dma_start(agg_table[l], hs_table[l]).then_inc(scattered, 16)
                    with pool.Fori(0, cols) as c:
                        pool.wait_ge(index_ready, 3 * c + 3)
                        pool.wait_ge(scattered, 16 * c + 16)
                        pool.sem_inc(passed, 1)
                        pool.indirect_dma_start(gs_hs[:, :], None, hs_table[l], bass.IndirectOffsetOnAxis(ap=index[:, 0:1], axis=0)).then_inc(hs_gathered, 16)
                        pool.indirect_dma_start(gs_agg[:, :], None, agg_table[l], bass.IndirectOffsetOnAxis(ap=index[:, 1:2], axis=0)).then_inc(agg_gathered, 16)
                        pool.wait_ge(target_ready, c + 1)
                        pool.wait_ge(added, c + 1)
                        pool.sem_inc(passed, 1)
                        pool.indirect_dma_start(agg_table[l], bass.IndirectOffsetOnAxis(ap=index[:, 2:3], axis=0), gs_agg[:, :], None,
                                                bounds_check=padded - 1, oob_is_err=False).then_inc(scattered, 16)
                    pool.wait_ge(scattered, 16 * (cols + 1))

                @block.tensor
                def _(pe):
                    with pe.Fori(0, cols) as c:
                        pe.wait_ge(index_ready, 3 * c + 3)
                        nc.tensor.transpose(bank[0][:, 0:P], gs_dst[:, 0:1].to_broadcast([P, P]), ident[:, :]).then_inc(rows_t_ready, 1)
                        pe.wait_ge(same_ready, c + 1)
                        pe.wait_ge(hs_gathered, 16 * c + 16)
                        nc.tensor.matmul(bank[1][:, 0:dim], gs_same[:, :], gs_hs[:, :], start=True, stop=True).then_inc(summed, 1)

                @block.vector
                def _(dve):
                    with dve.Fori(0, cols) as c:
                        dve.wait_ge(scattered, 16 * c + 16)
                        nc.vector.tensor_copy(index[:, 0:1], src_sb[:, bass.ds(c, 1)]).then_inc(index_ready, 1)
                        nc.vector.tensor_copy(index[:, 1:2], dst_sb[:, bass.ds(c, 1)]).then_inc(index_ready, 1)
                        nc.vector.tensor_copy(gs_dst[:, :], dst_sb[:, bass.ds(c, 1)]).then_inc(index_ready, 1)
                        dve.wait_ge(rows_t_ready, c + 1)
                        nc.vector.tensor_scalar(gs_same[:, :], bank[0][:, 0:P], gs_dst[:, 0:1], None, ALU.is_equal).then_inc(same_ready, 1)
                        dve.wait_ge(same_ready, c + 1)
                        nc.vector.tensor_tensor(gs_before[:, :], gs_same[:, :], lower[:, :], ALU.mult).then_inc(count_ready, 1)
                        dve.wait_ge(count_ready, 3 * c + 1)
                        nc.vector.tensor_reduce(gs_count[:, :], gs_before[:, :], AX, ALU.add).then_inc(count_ready, 1)
                        dve.wait_ge(count_ready, 3 * c + 2)
                        nc.vector.scalar_tensor_tensor(gs_count[:, :], gs_count[:, :], float(FAR), gs_dst[:, :], ALU.mult, ALU.add).then_inc(count_ready, 1)
                        dve.wait_ge(count_ready, 3 * c + 3)
                        nc.vector.tensor_copy(index[:, 2:3], gs_count[:, :]).then_inc(target_ready, 1)
                        dve.wait_ge(summed, c + 1)
                        dve.wait_ge(agg_gathered, 16 * c + 16)
                        nc.vector.tensor_tensor(gs_agg[:, :], gs_agg[:, :], bank[1][:, 0:dim], ALU.add).then_inc(added, 1)

        gs_index = sb("gs_index", [P, 3], I32)
        gs_dst = sb("gs_dst", [P, 1], F32)
        gs_count = sb("gs_count", [P, 1], F32)
        gs_same = sb("gs_same", [P, P], F32)
        gs_before = sb("gs_before", [P, P], F32)
        gs_hs = sb("gs_hs", [P, dim], F32)
        gs_agg = sb("gs_agg", [P, dim], F32)

        agg_tile = sb("agg_tile", [P, 2, dim], F32)
        feat_tile = sb("feat_tile", [P, 2, dim], F32)
        feat_out = sb("feat_out", [P, 2, dim], F32)
        turned = sb("turned", [P, 2, 4, P], F32)
        res_part = sb("res_part", [P, 2, dim], F32)
        layer_sum = sb("layer_sum", [P, 2, dim], F32)
        x_tile = sb("x_tile", [P, 2, dim], F32)

        def update_nodes(l):
            last = l == layers - 1
            agg_loaded = [sem(f"agg_loaded{l}_{b}") for b in range(2)]
            x_back = [sem(f"x_back{l}_{b}") for b in range(2)]
            turned_ready = sem(f"turned_ready{l}")
            turned_out = sem(f"turned_out{l}")
            products_ready = sem(f"products_ready{l}")
            res_out = sem(f"res_out{l}")
            sum_ready = sem(f"sum_ready{l}")
            feat_ready = sem(f"feat_ready{l}")
            hs_ready = sem(f"hs_ready{l}")
            hs_stored = [sem(f"hs_stored{l}_{b}") for b in range(2)]
            x_cleared = sem(f"x_cleared{l}")

            def each(eng, body):
                with eng.Fori(0, tiles // 2) as u:
                    body(u * 2, u, 0)
                    body(u * 2 + 1, u, 1)
                body(tiles - 1, tiles // 2, 0)

            def featc(t):
                return feat[:, bass.ds(t, 1), :].rearrange("p a d -> p (a d)")

            with nc.Block() as block:
                @block.sync
                def _(sp):
                    def first(t):
                        sp.dma_start(agg_tile[:, t, :], agg_table[l][t * P:(t + 1) * P, :]).then_inc(agg_loaded[t], 16)
                        sp.dma_start(feat_tile[:, t, :], feat_table[l][t * P:(t + 1) * P, :]).then_inc(agg_loaded[t], 16)
                        if last:
                            sp.dma_start(x_tile[:, t, :], x[t * P:(t + 1) * P, :]).then_inc(x_back[t], 16)

                    def later(t, b):
                        sp.wait_ge(turned_ready, t - 1)
                        sp.dma_start(agg_tile[:, b, :], agg_table[l][bass.ds(t * P, P), :]).then_inc(agg_loaded[b], 16)
                        sp.dma_start(feat_tile[:, b, :], feat_table[l][bass.ds(t * P, P), :]).then_inc(agg_loaded[b], 16)
                        if last:
                            sp.wait_ge(feat_ready, t - 1)
                            sp.dma_start(x_tile[:, b, :], x[bass.ds(t * P, P), :]).then_inc(x_back[b], 16)

                    first(0)
                    first(1)
                    with sp.Fori(1, tiles // 2) as u:
                        later(u * 2, 0)
                        later(u * 2 + 1, 1)
                    t = tiles - 1
                    sp.wait_ge(turned_ready, t - 1)
                    sp.dma_start(agg_tile[:, 0, :], agg_table[l][t * P:padded, :]).then_inc(agg_loaded[0], 16)
                    sp.dma_start(feat_tile[:, 0, :], feat_table[l][t * P:padded, :]).then_inc(agg_loaded[0], 16)
                    if last:
                        sp.wait_ge(feat_ready, t - 1)
                        sp.wait_ge(x_cleared, 1)
                        sp.dma_start(x_tile[0:last_rows, 0, :], x[full:nodes, :]).then_inc(x_back[0], 16)

                @block.tensor
                def _(pe):
                    def body(t, u, b):
                        turn, prod = bank[b], (bank[2 + b], bank[4 + b])
                        pe.wait_ge(agg_loaded[b], u * 32 + 32)
                        pe.wait_ge(turned_out, t + 1)
                        for k in range(K2):
                            nc.tensor.transpose(turn[:, k * P:(k + 1) * P], agg_tile[:, b, k * P:(k + 1) * P], ident[:, :])
                            mm = nc.tensor.transpose(turn[:, (2 + k) * P:(3 + k) * P], feat_tile[:, b, k * P:(k + 1) * P], ident[:, :])
                        mm.then_inc(turned_ready, 1)
                        pe.wait_ge(turned_out, t + 2)
                        pe.wait_ge(sum_ready, t + 1)
                        for k in range(K2):
                            nc.tensor.matmul(prod[0][:, 0:dim], turned[:, b, k, :], gnn_w_sb[:, l, k, :], start=k == 0, stop=k == K2 - 1)
                        for k in range(K2):
                            nc.tensor.matmul(prod[1][:, 0:dim], turned[:, b, 2 + k, :], res_w_sb[:, k, :], start=k == 0, stop=False)
                        nc.tensor.matmul(prod[1][:, 0:dim], ones_row[:, :], bias_sum[:, l, :], start=False, stop=True).then_inc(products_ready, 1)
                    each(pe, body)

                @block.scalar
                def _(act):
                    act.sem_inc(turned_out, 1)

                    def body(t, u, b):
                        act.wait_ge(turned_ready, t + 1)
                        nc.scalar.activation(turned[:, b, :, :].rearrange("p k d -> p (k d)"), bank[b][:, :], ACT.Copy).then_inc(turned_out, 1)
                        act.wait_ge(products_ready, t + 1)
                        act.wait_ge(sum_ready, t + 1)
                        nc.scalar.activation(res_part[:, b, :], bank[4 + b][:, 0:dim], ACT.Copy).then_inc(res_out, 1)
                    each(act, body)

                @block.vector
                def _(dve):
                    dve.sem_inc(sum_ready, 1)

                    def body(t, u, b):
                        dve.wait_ge(res_out, t + 1)
                        nc.vector.scalar_tensor_tensor(layer_sum[:, b, :], bank[2 + b][:, 0:dim], dis[:, bass.ds(t, 1)], res_part[:, b, :],
                                                       ALU.mult, ALU.add).then_inc(sum_ready, 1)
                        dve.wait_ge(sum_ready, t + 2)
                        if last:
                            dve.wait_ge(x_back[b], 16 if u is None else u * 16 + 16)
                            nc.vector.scalar_tensor_tensor(featc(t), layer_sum[:, b, :], 0.0, x_tile[:, b, :], ALU.max, ALU.add).then_inc(feat_ready, 1)
                        else:
                            if u is not None:
                                dve.wait_ge(hs_stored[b], u * 32)
                            nc.vector.tensor_scalar(feat_out[:, b, :], layer_sum[:, b, :], 0.0, None, ALU.max).then_inc(feat_ready, 1)
                            dve.wait_ge(feat_ready, t + 1)
                            nc.vector.tensor_scalar(scaled[:, b, :], feat_out[:, b, :], dis[:, bass.ds(t, 1)], None, ALU.mult).then_inc(hs_ready, 1)
                    body(0, None, 0)
                    body(1, None, 1)
                    with dve.Fori(1, tiles // 2) as u:
                        body(u * 2, u, 0)
                        body(u * 2 + 1, u, 1)
                    if last:
                        dve.wait_ge(feat_ready, tiles - 1)
                        nc.vector.memset(x_tile[:, 0, :], 0.0).then_inc(x_cleared, 1)
                    body(tiles - 1, tiles // 2, 0)

                @block.gpsimd
                def _(pool):
                    if not last:
                        def body(t, u, b):
                            pool.wait_ge(hs_ready, t + 1)
                            pool.dma_start(hs_table[l + 1][bass.ds(t * P, P), :], scaled[:, b, :]).then_inc(hs_stored[b], 16)
                            pool.dma_start(feat_table[l + 1][bass.ds(t * P, P), :], feat_out[:, b, :]).then_inc(hs_stored[b], 16)
                        each(pool, body)
                        pool.wait_ge(hs_stored[0], 32 * (tiles - tiles // 2))
                        pool.wait_ge(hs_stored[1], 32 * (tiles // 2))

        for l in range(layers):
            gather_sum(l)
            update_nodes(l)
        close_scope()

        y = sb("y", [P, GROUP, dim], F32)
        y_t = sb("y_t", [P, K2, GROUP * P], F32)
        router_t = sb("router_t", [P, GROUP * P], F32)
        h1_t = sb("h1_t", [P, 2, K2, GROUP * P], F32)
        h2_t = sb("h2_t", [P, 2, K2, GROUP * P], F32)
        acc = sb("acc", [P, GROUP, dim], F32)
        g_stats = sb("g_stats", [P, GROUP, 6], F32)
        g_a = sb("g_a", [P, GROUP], F32)
        g_d = sb("g_d", [P, GROUP], F32)
        g_s = sb("g_s", [P, GROUP], F32)
        g_mean = sb("g_mean", [P, GROUP], F32)
        g_rstd = sb("g_rstd", [P, GROUP], F32)
        rank = sb("rank", [P, experts], F32)
        top = sb("top", [P, 6, GROUP], F32)
        prob = sb("prob", [P, GROUP, experts], F32)
        pick = sb("pick", [P, 3, GROUP, experts], F32)
        gate = sb("gate", [P, GROUP, experts], F32)

        ffn_link = sem("ffn_link")
        ffn_var = sem("ffn_var")
        ffn_std = sem("ffn_std")
        y_ready = sem("y_ready")
        item_ready = sem("item_ready")
        act_out = sem("act_out")
        dve_out = sem("dve_out")
        logits_ready = sem("logits_ready")
        logits_used = sem("logits_used")
        shifted = sem("shifted")
        exped = sem("exped")
        gap_ready = sem("gap_ready")
        gap_exped = sem("gap_exped")
        outs_ready = sem("outs_ready")
        outs_used = sem("outs_used")
        acc_stored = sem("acc_stored")
        acc_free = sem("acc_free")
        rank_made = sem("rank_made")

        RING = 3
        ring, out_bank, logit_bank = bank[0:3], bank[3:7], bank[7]
        items = [("turn", k, n) for k in range(K2) for n in range(2)]
        items += [("route", 0, n) for n in range(2)]
        items += [("h1", 0, m, n) for m in range(K2) for n in range(2)]
        for e in range(experts):
            items += [("h2", e, m, n) for m in range(K2) for n in range(2)]
            if e + 1 < experts:
                items += [("h1", e + 1, m, n) for m in range(K2) for n in range(2)]
        ITEMS = len(items)
        EACH = ITEMS // 2
        FREE = 2
        assert ITEMS % RING == 0 and ITEMS % 2 == 0
        OUTS = experts * 4

        def wait_emptied(eng, g, k):
            s = (act_out, dve_out)[k % 2]
            eng.wait_ge(s, g * EACH + (FREE + k // 2 + 1))

        def wait_all_emptied(eng, g, k):
            wait_emptied(eng, g, k)
            wait_emptied(eng, g, k - 1)

        def index_of(kind, e):
            return max(k for k, it in enumerate(items) if it[0] == kind and it[1] == e)

        def cols_of(n):
            return slice(n * HALF, (n + 1) * HALF)

        with nc.Block() as block:
            @block.tensor
            def _(pe):
                def item(g, k):
                    it = items[k]
                    dstb = ring[k % RING]
                    wait_emptied(pe, g, k - RING)
                    if it[0] == "turn":
                        _, kf, n = it
                        ts = range(4) if n == 0 else range(4, GROUP)
                        for j, t in enumerate(ts):
                            mm = nc.tensor.transpose(dstb[:, j * P:(j + 1) * P], y[:, t, kf * P:(kf + 1) * P], ident[:, :])
                    elif it[0] == "route":
                        for kf in range(K2):
                            mm = nc.tensor.matmul(dstb[:, 0:HALF], router_w1_sb[:, kf, :], y_t[:, kf, cols_of(it[2])], start=kf == 0, stop=kf == K2 - 1)
                    else:
                        kind, e, m, n = it
                        w, source = (w1_sb, y_t[:, :, :]) if kind == "h1" else (w2_sb, h1_t[:, e % 2, :, :])
                        for kf in range(K2):
                            mm = nc.tensor.matmul(dstb[:, 0:HALF], w[:, e, kf, m * P:(m + 1) * P], source[:, kf, cols_of(n)], start=kf == 0, stop=kf == K2 - 1)
                    mm.then_inc(item_ready, 1)

                def outs(g, e):
                    wait_all_emptied(pe, g, index_of("h2", e))
                    for q in range(4):
                        pe.wait_ge(outs_used, g * OUTS + (e * 4 + q + 1))
                        for t in range(2 * q, min(2 * q + 2, GROUP)):
                            o = out_bank[q][:, (t % 2) * dim:(t % 2 + 1) * dim]
                            for kf in range(K2):
                                nc.tensor.matmul(o, h2_t[:, e % 2, kf, t * P:(t + 1) * P], w3_sb[:, e, kf, :], start=kf == 0, stop=False)
                            mm = nc.tensor.matmul(o, ones_row[:, :], b3_sb[:, e, :], start=False, stop=True)
                        mm.then_inc(outs_ready, 1)

                with pe.Fori(0, groups) as g:
                    pe.wait_ge(y_ready, g + 1)
                    for k in range(4):
                        item(g, k)
                    wait_all_emptied(pe, g, 3)
                    for k in range(4, 10):
                        item(g, k)
                    wait_all_emptied(pe, g, 5)
                    pe.wait_ge(logits_used, g + 1)
                    for t in range(GROUP):
                        o = logit_bank[:, t * experts:(t + 1) * experts]
                        nc.tensor.matmul(o, router_t[:, t * P:(t + 1) * P], router_w2_sb[:, :], start=True, stop=False)
                        mm = nc.tensor.matmul(o, ones_row[:, :], router_b2_sb[:, :], start=False, stop=True)
                    mm.then_inc(logits_ready, 1)
                    k = 10
                    for e in range(experts):
                        wait_all_emptied(pe, g, index_of("h1", e))
                        for _i in range(8 if e + 1 < experts else 4):
                            item(g, k)
                            k += 1
                        outs(g, e)

            def empty(eng, g, k):
                it = items[k]
                b = ring[k % RING]
                eng.wait_ge(item_ready, g * ITEMS + (k + 1))
                if it[0] == "turn":
                    n = 4 * P if it[2] == 0 else (GROUP - 4) * P
                    to, bias, frm = y_t[:, it[1], it[2] * 4 * P:it[2] * 4 * P + n], None, b[:, 0:n]
                elif it[0] == "route":
                    to, bias, frm = router_t[:, cols_of(it[2])], router_b1_sb[:, 0:1], b[:, 0:HALF]
                else:
                    kind, e, m, n = it
                    h, bb = (h1_t, b1_sb) if kind == "h1" else (h2_t, b2_sb)
                    to, bias, frm = h[:, e % 2, m, cols_of(n)], bb[:, e, m:m + 1], b[:, 0:HALF]
                if k % 2 == 0:
                    if bias is None:
                        ins = nc.scalar.activation(to, frm, ACT.Copy)
                    else:
                        ins = nc.scalar.activation(to, frm, ACT.Relu, bias=bias)
                    ins.then_inc(act_out, 1)
                else:
                    if bias is None:
                        ins = nc.vector.tensor_copy(to, frm)
                    else:
                        ins = nc.vector.tensor_scalar(to, frm, bias, 0.0, ALU.add, ALU.max)
                    ins.then_inc(dve_out, 1)

            @block.scalar
            def _(act):
                act.sem_inc(act_out, FREE)
                with act.Fori(0, groups) as g:
                    act.wait_ge(ffn_var, g + 1)
                    nc.scalar.activation(g_rstd[:, :], g_s[:, :], ACT.Sqrt, bias=eps_col[:, 0:1], scale=1.0 / dim).then_inc(ffn_std, 1)
                    for k in range(0, 10, 2):
                        empty(act, g, k)
                    act.wait_ge(shifted, g + 1)
                    nc.scalar.activation(prob[:, :, :], prob[:, :, :], ACT.Exp).then_inc(exped, 1)
                    act.wait_ge(gap_ready, g + 1)
                    nc.scalar.activation(top[:, 4, :], top[:, 4, :], ACT.Exp).then_inc(gap_exped, 1)
                    for k in range(10, ITEMS, 2):
                        empty(act, g, k)

            @block.vector
            def _(dve):
                link = Link(dve, ffn_link)
                for j in range(experts):
                    nc.vector.memset(rank[:, j:j + 1], float(experts - j)).then_inc(rank_made, 1)
                dve.wait_ge(rank_made, experts)
                dve.sem_inc(dve_out, FREE)
                dve.sem_inc(outs_used, 4)
                dve.sem_inc(acc_free, 1)
                dve.sem_inc(logits_used, 1)
                LINKS = GROUP + 6 + GROUP + 4 + 2 + 10 + 1 + 3 + experts * GROUP
                with dve.Fori(0, groups) as g:
                    link.loop(g, LINKS_PER_GROUP)
                    gf = feat[:, bass.ds(g * GROUP, GROUP), :]
                    for t in range(GROUP):
                        nc.vector.bn_stats(g_stats[:, t, :], gf[:, t, :]).then_inc(ffn_link, 1)
                    link.count += GROUP
                    dve.wait_ge(ffn_link, link.count + g * LINKS_PER_GROUP)
                    st = g_stats[:, :, :]
                    link(nc.vector.tensor_tensor(g_a[:, :], st[:, :, 1], st[:, :, 4], ALU.add))
                    link(nc.vector.tensor_tensor(g_d[:, :], st[:, :, 1], st[:, :, 4], ALU.subtract))
                    link(nc.vector.tensor_tensor(g_s[:, :], st[:, :, 2], st[:, :, 5], ALU.add))
                    link(nc.vector.tensor_tensor(g_d[:, :], g_d[:, :], g_d[:, :], ALU.mult))
                    link(nc.vector.tensor_scalar(g_mean[:, :], g_a[:, :], 0.5, None, ALU.mult))
                    nc.vector.scalar_tensor_tensor(g_s[:, :], g_d[:, :], dim / 4.0, g_s[:, :], ALU.mult, ALU.add).then_inc(ffn_var, 1)
                    dve.wait_ge(ffn_std, g + 1)
                    link(nc.vector.reciprocal(g_rstd[:, :], g_rstd[:, :]))
                    for t in range(GROUP):
                        ins = nc.vector.tensor_scalar(y[:, t, :], gf[:, t, :], g_mean[:, t:t + 1], g_rstd[:, t:t + 1], ALU.subtract, ALU.mult)
                    ins.then_inc(y_ready, 1)
                    for k in range(1, 10, 2):
                        empty(dve, g, k)

                    def wide(v):
                        return v.unsqueeze(2).to_broadcast([P, GROUP, experts])

                    logits = logit_bank[:, 0:GROUP * experts].rearrange("p (t e) -> p t e", e=experts)
                    ranks = rank[:, :].unsqueeze(1).to_broadcast([P, GROUP, experts])
                    dve.wait_ge(logits_ready, g + 1)
                    link(nc.vector.tensor_reduce(top[:, 0, :], logits, AX, ALU.max))
                    nc.vector.tensor_tensor(prob[:, :, :], logits, wide(top[:, 0, :]), ALU.subtract).then_inc(shifted, 1)
                    dve.wait_ge(shifted, g + 1)
                    dve.sem_inc(logits_used, 1)
                    dve.wait_ge(exped, g + 1)
                    link(nc.vector.tensor_reduce(top[:, 0, :], prob[:, :, :], AX, ALU.add))
                    link(nc.vector.reciprocal(top[:, 0, :], top[:, 0, :]))
                    link(nc.vector.tensor_tensor(prob[:, :, :], prob[:, :, :], wide(top[:, 0, :]), ALU.mult))
                    for i in range(2):
                        link(nc.vector.tensor_reduce(top[:, 1 + i, :], prob[:, :, :], AX, ALU.max))
                        link(nc.vector.tensor_tensor(pick[:, 2, :, :], prob[:, :, :], wide(top[:, 1 + i, :]), ALU.is_equal))
                        link(nc.vector.tensor_tensor(pick[:, 2, :, :], pick[:, 2, :, :], ranks, ALU.mult))
                        link(nc.vector.tensor_reduce(top[:, 3, :], pick[:, 2, :, :], AX, ALU.max))
                        link(nc.vector.tensor_tensor(pick[:, i, :, :], ranks, wide(top[:, 3, :]), ALU.is_equal))
                        if i == 0:
                            link(nc.vector.scalar_tensor_tensor(prob[:, :, :], pick[:, 0, :, :], -4.0, prob[:, :, :], ALU.mult, ALU.add))
                    nc.vector.tensor_tensor(top[:, 4, :], top[:, 2, :], top[:, 1, :], ALU.subtract).then_inc(gap_ready, 1)
                    dve.wait_ge(gap_exped, g + 1)
                    link(nc.vector.tensor_scalar(top[:, 0, :], top[:, 4, :], 1.0, None, ALU.add))
                    link(nc.vector.reciprocal(top[:, 0, :], top[:, 0, :]))
                    link(nc.vector.tensor_tensor(top[:, 5, :], top[:, 4, :], top[:, 0, :], ALU.mult))
                    link(nc.vector.tensor_tensor(pick[:, 0, :, :], pick[:, 0, :, :], wide(top[:, 0, :]), ALU.mult))
                    link(nc.vector.tensor_tensor(pick[:, 1, :, :], pick[:, 1, :, :], wide(top[:, 5, :]), ALU.mult))
                    link(nc.vector.tensor_tensor(gate[:, :, :], pick[:, 0, :, :], pick[:, 1, :, :], ALU.add))
                    dve.wait_ge(acc_free, g + 1)

                    k = 10
                    for e in range(experts):
                        for _i in range(8 if e + 1 < experts else 4):
                            if k % 2 == 1:
                                empty(dve, g, k)
                            k += 1
                        for q in range(4):
                            dve.wait_ge(outs_ready, g * OUTS + (e * 4 + q + 1))
                            if e:
                                dve.wait_ge(ffn_link, acc_base + (e - 1) * 4 + q + 1 + g * LINKS_PER_GROUP)
                            else:
                                acc_base = link.count if q == 0 else acc_base
                            for t in range(2 * q, min(2 * q + 2, GROUP)):
                                o = out_bank[q][:, (t % 2) * dim:(t % 2 + 1) * dim]
                                ins = nc.vector.scalar_tensor_tensor(acc[:, t, :], o, gate[:, t, e:e + 1], acc[:, t, :] if e else gf[:, t, :], ALU.mult, ALU.add)
                            ins.then_inc(ffn_link, 1)
                            dve.wait_ge(ffn_link, acc_base + e * 4 + q + 1 + g * LINKS_PER_GROUP)
                            dve.sem_inc(outs_used, 1)
                    link.count = acc_base + experts * 4
                    assert link.count - link.start == LINKS_PER_GROUP, link.count - link.start

            @block.sync
            def _(sp):
                done = ACC_BASE + experts * 4
                with sp.Fori(0, groups - 1) as g:
                    sp.wait_ge(ffn_link, g * LINKS_PER_GROUP + done)
                    sp.dma_start(out[bass.ds(g * (GROUP * P), GROUP * P), :].rearrange("(t p) d -> p t d", p=P), acc[:, :, :]).then_inc(acc_stored, 16)
                    sp.wait_ge(acc_stored, 16 * g + 16)
                    sp.sem_inc(acc_free, 1)
                g = groups - 1
                sp.wait_ge(ffn_link, g * LINKS_PER_GROUP + done)
                sp.dma_start(out[g * GROUP * P:full, :].rearrange("(t p) d -> p t d", p=P), acc[:, 0:GROUP - 1, :]).then_inc(acc_stored, 16)
                sp.dma_start(out[full:nodes, :], acc[0:last_rows, GROUP - 1, :]).then_inc(acc_stored, 16)
                sp.wait_ge(acc_stored, 16 * (groups + 1))


LINKS_PER_GROUP = 7 + 5 + 1 + 1 + 3 + 11 + 6 + 24
ACC_BASE = LINKS_PER_GROUP - 24

_INS = ['x', 'src', 'dst', 'L0_gnn_W', 'L0_gnn_b', 'L0_gnn_resW', 'L0_gnn_resb', 'L0_ffn_router_w1', 'L0_ffn_router_b1',
        'L0_ffn_router_w2', 'L0_ffn_router_b2', 'L0_ffn_expert_w1', 'L0_ffn_expert_b1', 'L0_ffn_expert_w2', 'L0_ffn_expert_b2',
        'L0_ffn_expert_w3', 'L0_ffn_expert_b3']


def kernel(**inputs):
    import numpy as _np
    import concourse.bacc as _bacc
    from concourse import mybir as _mybir
    from concourse.bass_utils import run_bass_kernel_spmd as _run

    nc = _bacc.Bacc("TRN2", target_bir_lowering=False, num_devices=1)
    arrays, args = {}, []
    for name in _INS:
        a = _np.ascontiguousarray(inputs[name])
        arrays[f"in_{name}_dram"] = a
        args.append(nc.dram_tensor(f"in_{name}_dram", a.shape, _mybir.dt.from_np(a.dtype), kind="ExternalInput").ap())
    shape = inputs['x'].shape
    args.append(nc.dram_tensor("out_dram", shape, _mybir.dt.float32, kind="ExternalOutput").ap())
    gnn_moe_kernel(nc, *args)
    r = _run(nc, [arrays], core_ids=[0])
    return r.results[0]["out_dram"]
```

```python
from contextlib import ExitStack

import concourse.bass as bass
from concourse import mybir

P = 128
F32 = mybir.dt.float32
BF16 = mybir.dt.bfloat16
I32 = mybir.dt.int32
U32 = mybir.dt.uint32
ALU = mybir.AluOpType
ACT = mybir.ActivationFunctionType
AX = mybir.AxisListType.X
EPS = 1e-5
FAR = 16384


class Link:

    def __init__(self, engine, sem):
        self.engine, self.sem, self.count, self.trip = engine, sem, 0, None

    def loop(self, i, per):
        self.trip, self.per, self.start = i, per, self.count

    def end(self, trips):
        assert self.count - self.start == self.per, (self.count - self.start)
        self.count = self.start + self.per * trips
        self.trip = None

    def __call__(self, ins):
        ins.then_inc(self.sem, 1)
        self.count += 1
        self.engine.wait_ge(self.sem, self.count + self.trip * self.per if self.trip is not None else self.count)


def gnn_moe_kernel(nc, x, src, dst, gnn_w, gnn_b, res_w, res_b, router_w1, router_b1, router_w2, router_b2,
                   expert_w1, expert_b1, expert_w2, expert_b2, expert_w3, expert_b3, out):
    nodes, dim = x.shape
    edges = src.shape[0]
    layers = gnn_w.shape[0]
    experts = expert_w1.shape[0]
    router_h = router_w1.shape[1]
    tiles = -(-nodes // P)
    padded = tiles * P
    last_rows = nodes - (tiles - 1) * P
    cols = -(-edges // P)
    last_cols = edges - (P - 1) * cols
    K2 = dim // P
    GROUP = 7
    groups = tiles // GROUP
    HALF = GROUP * P // 2
    pairs = -(-tiles // 2)
    slots = 64
    align = 4
    rows = edges // align + 1
    width = 2 * tiles
    HIST = 16
    hist_steps = -(-cols // HIST)
    assert tiles % GROUP == 0 and router_h == P and dim == 2 * P
    assert hist_steps % 2 == 0 and pairs % 2 == 1 and edges % align == 0 and edges % (16 * align) == 0

    ctx = ExitStack()
    with ctx:
        scopes = [ctx]

        def sb(name, shape, dt):
            return scopes[-1].enter_context(nc.sbuf_tensor(name, shape, dt))

        def open_scope():
            scopes.append(ExitStack())

        def close_scope():
            scopes.pop().close()

        def psum(name):
            return ctx.enter_context(nc.psum_tensor(name, [P, 512], F32))

        def sem(name):
            return ctx.enter_context(nc.semaphore(name))

        ident = sb("ident", [P, P], F32)
        ident_bf = sb("ident_bf", [P, P], BF16)
        ones_row = sb("ones_row", [1, P], F32)
        eps_col = sb("eps_col", [P, 1], F32)
        dis = sb("dis", [P, tiles], F32)
        flag = sb("flag", [P, 1], I32)
        gnn_w_sb = sb("gnn_w_sb", [P, layers, K2, dim], F32)
        res_w_sb = sb("res_w_sb", [P, K2, dim], F32)
        bias_rows = sb("bias_rows", [1, layers + 1, dim], F32)
        bias_sum = sb("bias_sum", [1, layers, dim], F32)

        hs_table = [nc.dram_tensor(f"hs_table{l}", (2 * pairs * P, dim), F32).ap() for l in range(layers)]
        feat_table = [nc.dram_tensor(f"feat_table{l}", (2 * pairs * P, dim), F32).ap() for l in range(layers)]
        agg_table = [nc.dram_tensor(f"agg_table{l}", (2 * pairs * P, dim), F32).ap() for l in range(layers)]

        src_pad = nc.dram_tensor("src_pad", (P * cols,), I32).ap()
        dst_pad = nc.dram_tensor("dst_pad", (P * cols,), I32).ap()
        src_rows = nc.dram_tensor("src_rows", (rows, slots), I32).ap()
        counts_table = nc.dram_tensor("counts_table", (pairs, P, tiles * 2 * P), BF16).ap()

        bank = [psum(f"bank{i}") for i in range(8)]

        def rows_of(table, n):
            return table.rearrange("(t p) d -> p t d", p=P)

        open_scope()
        parts = sb("parts", [P, 2 * pairs, 3 * dim], BF16)
        keys_t = sb("keys_t", [P, pairs, 2, P], F32)
        iota_lo = sb("iota_lo", [P, P], BF16)
        iota_hi = sb("iota_hi", [P, width], BF16)
        open_scope()
        feat = sb("feat", [P, tiles, dim], F32)
        iota_slot = sb("iota_slot", [P, slots], F32)
        deg = sb("deg", [P, 2 * pairs], F32)
        ones = sb("ones", [P, P], F32)
        upper = sb("upper", [P, P], F32)
        real = sb("real", [P, 1], F32)
        row_sum = sb("row_sum", [P, tiles], F32)
        row_mean = sb("row_mean", [P, tiles], F32)
        row_squares = sb("row_squares", [P, tiles], F32)
        rstd = sb("rstd", [P, tiles], F32)
        disorder = sb("disorder", [P, 3], F32)
        open_scope()
        src_sb = sb("src_sb", [P, cols], I32)
        dst_sb = sb("dst_sb", [P, cols + 1], I32)
        key_i = sb("key_i", [P, cols], I32)
        dst_lo = sb("dst_lo", [P, HIST * hist_steps], F32)
        dst_hi = sb("dst_hi", [P, HIST * hist_steps], BF16)
        hi_keys = sb("hi_keys", [P, 2, HIST], BF16)
        lo_keys = sb("lo_keys", [P, 2, HIST], F32)
        onehot_lo = sb("onehot_lo", [P, 2, HIST, P], BF16)
        onehot_hi = sb("onehot_hi", [P, 2, HIST, tiles], BF16)

        x_loaded = sem("x_loaded")
        dst_loaded = sem("dst_loaded")
        next_loaded = sem("next_loaded")
        src_loaded = sem("src_loaded")
        pad_stored = sem("pad_stored")
        dst_stored = sem("dst_stored")
        rows_stored = sem("rows_stored")
        gnn_w_loaded = sem("gnn_w_loaded")
        edges_cleared = sem("edges_cleared")
        feat_cleared = sem("feat_cleared")
        iotas_made = sem("iotas_made")
        pool_link = sem("pool_link")
        prep_link = sem("prep_link")
        pool_passed = sem("pool_passed")
        act_link = sem("act_link")
        hi_keys_ready = sem("hi_keys_ready")
        lo_ready = sem("lo_ready")
        hi_ready = sem("hi_ready")
        hist_used = sem("hist_used")
        full = (tiles - 1) * P

        with nc.Block() as block:
            @block.sync
            def _(sp):
                sp.wait_ge(edges_cleared, 3)
                for table, tile, s in ((dst, dst_sb, dst_loaded), (src, src_sb, src_loaded)):
                    for a, b in ((0, 112), (112, P - 1)):
                        sp.dma_start(tile[a:b, 0:cols], table[a * cols:b * cols].rearrange("(p c) -> p c", c=cols)).then_inc(s, 16)
                    sp.dma_start(tile[P - 1:P, 0:last_cols], table[(P - 1) * cols:edges].rearrange("(p c) -> p c", p=1)).then_inc(s, 16)
                sp.dma_start(dst_sb[0:P - 1, cols:cols + 1], bass.AP(tensor=dst.tensor, offset=dst.offset + cols, ap=[[cols, P - 1], [1, 1]]), allow_slow_non_contiguous=True).then_inc(next_loaded, 16)
                sp.wait_ge(src_loaded, 16 * 3)
                sp.dma_start(src_pad.rearrange("(p c) -> p c", c=cols), src_sb[:, :]).then_inc(pad_stored, 16)
                sp.wait_ge(dst_loaded, 16 * 3)
                sp.dma_start(dst_pad.rearrange("(p c) -> p c", c=cols), dst_sb[:, 0:cols]).then_inc(dst_stored, 16)
                sp.wait_ge(pad_stored, 16)
                share = (rows - 1) // 16
                sp.dma_start(src_rows[0:rows - 1, :].rearrange("(q r) s -> q r s", q=16),
                             bass.AP(tensor=src_pad.tensor, offset=src_pad.offset, ap=[[share * align, 16], [align, share], [1, slots]])).then_inc(rows_stored, 16)
                sp.dma_start(src_rows[rows - 1:rows, :], src_pad[(rows - 1) * align:(rows - 1) * align + slots].rearrange("(a s) -> a s", a=1)).then_inc(rows_stored, 16)
                sp.wait_ge(dst_stored, 16)
                sp.wait_ge(rows_stored, 32)

            @block.gpsimd
            def _(pool):
                link = Link(pool, pool_link)
                nc.gpsimd.iota(iota_lo[:, :], [[1, P]], 0, 0, allow_small_or_imprecise_dtypes=True).then_inc(iotas_made, 1)
                nc.gpsimd.iota(iota_hi[:, :], [[1, width]], -P, 0, allow_small_or_imprecise_dtypes=True).then_inc(iotas_made, 1)
                nc.gpsimd.iota(iota_slot[:, :], [[1, slots]], 0, 0, allow_small_or_imprecise_dtypes=True).then_inc(iotas_made, 1)
                link(nc.gpsimd.memset(ident[:, :], 0.0))
                link(nc.gpsimd.affine_select(out=ident[:, :], in_=ident[:, :], compare_op=ALU.not_equal, fill=1.0,
                                             base=0, pattern=[[-1, P]], channel_multiplier=1))
                link(nc.gpsimd.tensor_copy(ident_bf[:, :], ident[:, :]))
                link(nc.gpsimd.memset(upper[:, :], 1.0))
                link(nc.gpsimd.affine_select(out=upper[:, :], in_=upper[:, :], compare_op=ALU.is_gt, fill=0.0,
                                             base=0, pattern=[[1, P]], channel_multiplier=-1))
                link(nc.gpsimd.memset(real[:, :], 1.0))
                link(nc.gpsimd.affine_select(out=real[:, :], in_=real[:, :], compare_op=ALU.is_gt, fill=0.0,
                                             base=last_rows, pattern=[[0, 1]], channel_multiplier=-1))
                link(nc.gpsimd.memset(ones[:, :], 1.0))
                pool.wait_ge(hi_keys_ready, 2)

                def hi_onehots(b):
                    for u in range(HIST):
                        last = nc.gpsimd.tensor_scalar(onehot_hi[:, b, u, :], iota_lo[:, 0:tiles], hi_keys[:, b, u:u + 1], None, ALU.is_equal)
                    last.then_inc(hi_ready, 1)

                for b in range(2):
                    link(nc.gpsimd.tensor_copy(hi_keys[:, b, :], dst_hi[:, b * HIST:(b + 1) * HIST]))
                    hi_onehots(b)
                with pool.Fori(1, hist_steps // 2) as i:
                    for b in range(2):
                        pool.wait_ge(hi_ready, 2 * i - 1 + b)
                        pool.wait_ge(hist_used, 2 * i - 1 + b)
                        pool.sem_inc(pool_passed, 1)
                        nc.gpsimd.tensor_copy(hi_keys[:, b, :], dst_hi[:, bass.ds(i * (2 * HIST) + b * HIST, HIST)]).then_inc(pool_link, 1)
                        pool.wait_ge(pool_link, link.count - 2 + 2 * i + b + 1)
                        pool.sem_inc(pool_passed, 1)
                        hi_onehots(b)

            @block.scalar
            def _(act):
                act.wait_ge(feat_cleared, 1)
                for t0 in range(0, tiles - 1, 8):
                    act.dma_start(feat[:, t0:t0 + 8, :], x[t0 * P:(t0 + 8) * P, :].rearrange("(t p) d -> p t d", p=P)).then_inc(x_loaded, 16)
                act.dma_start(feat[0:last_rows, tiles - 1, :], x[full:nodes, :]).then_inc(x_loaded, 16)
                act.dma_start(gnn_w_sb[:, :, :, :].rearrange("p l k d -> p (l k) d"), gnn_w.rearrange("l (k p) d -> p (l k) d", p=P)).then_inc(gnn_w_loaded, 16)
                act.dma_start(res_w_sb[:, :, :], res_w.rearrange("(k p) d -> p k d", p=P)).then_inc(gnn_w_loaded, 16)
                act.dma_start(bias_rows[:, 0:layers, :], gnn_b.rearrange("(a l) d -> a l d", a=1)).then_inc(gnn_w_loaded, 16)
                act.dma_start(bias_rows[:, layers, :], res_b.rearrange("(a d) -> a d", a=1)).then_inc(gnn_w_loaded, 16)
                link = Link(act, act_link)

                def row(t):
                    return feat[:, bass.ds(t, 1), :].rearrange("p a d -> p (a d)")

                def unused(t, i):
                    return parts[:, bass.ds(t, 1), i * dim:(i + 1) * dim].rearrange("p a d -> p (a d)")

                act.wait_ge(x_loaded, 16 * ((tiles - 1) // 8 + 1))
                with act.Fori(0, tiles) as t:
                    nc.scalar.activation(unused(t, 0), row(t), ACT.Copy, accum_out=row_sum[:, bass.ds(t, 1)]).then_inc(act_link, 1)
                link.count += tiles
                act.wait_ge(act_link, link.count)
                link(nc.scalar.activation(row_mean[:, :], row_sum[:, :], ACT.Copy, scale=-1.0 / dim))
                with act.Fori(0, tiles) as t:
                    nc.scalar.activation(row(t), row(t), ACT.Identity, bias=row_mean[:, bass.ds(t, 1)]).then_inc(act_link, 1)
                link.count += tiles
                act.wait_ge(act_link, link.count)
                with act.Fori(0, tiles) as t:
                    nc.scalar.activation(unused(t, 1), row(t), ACT.Square, accum_out=row_squares[:, bass.ds(t, 1)]).then_inc(act_link, 1)
                link.count += tiles
                act.wait_ge(act_link, link.count)

            @block.tensor
            def _(pe):
                def count(b, first, last):
                    for u in range(HIST):
                        mm = nc.tensor.matmul(bank[0][:, 0:tiles], onehot_lo[:, b, u, :], onehot_hi[:, b, u, :],
                                              start=first and u == 0, stop=last and u == HIST - 1)
                    mm.then_inc(hist_used, 1)

                for i in range(2):
                    pe.wait_ge(lo_ready, i + 1)
                    pe.wait_ge(hi_ready, i + 1)
                    count(i, i == 0, False)
                with pe.Fori(1, hist_steps // 2 - 1) as i:
                    for b in range(2):
                        pe.wait_ge(lo_ready, 2 * i + b + 1)
                        pe.wait_ge(hi_ready, 2 * i + b + 1)
                        count(b, False, False)
                for b in range(2):
                    pe.wait_ge(lo_ready, hist_steps - 1 + b)
                    pe.wait_ge(hi_ready, hist_steps - 1 + b)
                    count(b, False, b == 1)

            @block.vector
            def _(dve):
                link = Link(dve, prep_link)
                pad = padded - 1
                last_quarter = slice(P - 32, P)
                nc.vector.memset(src_sb[last_quarter, :], pad).then_inc(edges_cleared, 1)
                nc.vector.memset(dst_sb[last_quarter, :], pad).then_inc(edges_cleared, 2)
                nc.vector.memset(feat[:, tiles - 1, :], 0.0).then_inc(feat_cleared, 1)
                nc.vector.memset(ones_row[:, :], 1.0)
                link(nc.vector.memset(eps_col[:, :], EPS))
                nc.vector.memset(dst_hi[:, cols:], -1.0).then_inc(hi_keys_ready, 1)
                link(nc.vector.memset(dst_lo[:, cols:], -1.0))
                dve.wait_ge(dst_loaded, 16 * 3)
                link(nc.vector.tensor_scalar(key_i[:, :], dst_sb[:, 0:cols], 7, None, ALU.logical_shift_right))
                nc.vector.tensor_copy(dst_hi[:, 0:cols], key_i[:, :]).then_inc(hi_keys_ready, 1)
                dve.wait_ge(hi_keys_ready, 2)
                link(nc.vector.tensor_scalar(key_i[:, :], dst_sb[:, 0:cols], P - 1, None, ALU.bitwise_and))
                link(nc.vector.tensor_copy(dst_lo[:, 0:cols], key_i[:, :]))
                dve.wait_ge(iotas_made, 3)
                base = link.count

                def lo_onehots(b):
                    for u in range(HIST):
                        last = nc.vector.tensor_scalar(onehot_lo[:, b, u, :], iota_lo[:, :], lo_keys[:, b, u:u + 1], None, ALU.is_equal)
                    last.then_inc(lo_ready, 1)

                for b in range(2):
                    link(nc.vector.tensor_copy(lo_keys[:, b, :], dst_lo[:, b * HIST:(b + 1) * HIST]))
                    lo_onehots(b)
                with dve.Fori(1, hist_steps // 2) as i:
                    for b in range(2):
                        dve.wait_ge(hist_used, 2 * i - 1 + b)
                        dve.wait_ge(lo_ready, 2 * i - 1 + b)
                        nc.vector.tensor_copy(lo_keys[:, b, :], dst_lo[:, bass.ds(i * (2 * HIST) + b * HIST, HIST)]).then_inc(prep_link, 1)
                        dve.wait_ge(prep_link, link.count - 2 + 2 * i + b + 1)
                        lo_onehots(b)
                link.count += hist_steps - 2

                link(nc.vector.memset(disorder[:, :], 0.0))
                dve.wait_ge(next_loaded, 16)
                link(nc.vector.tensor_tensor(dst_lo[:, 0:cols - 1], dst_sb[:, 1:cols], dst_sb[:, 0:cols - 1], ALU.is_lt))
                link(nc.vector.tensor_reduce(disorder[:, 0:1], dst_lo[:, 0:cols - 1], AX, ALU.add))
                link(nc.vector.tensor_tensor(disorder[0:P - 1, 1:2], dst_sb[0:P - 1, cols:cols + 1], dst_sb[0:P - 1, cols - 1:cols], ALU.is_lt))
                dve.wait_ge(gnn_w_loaded, 16 * 4)
                for l in range(layers):
                    link(nc.vector.tensor_tensor(bias_sum[:, l, :], bias_rows[:, l, :], bias_rows[:, layers, :], ALU.add))
        close_scope()

        total = sb("total", [P, 2 * pairs], F32)
        zeros = sb("zeros", [P, 2 * pairs], F32)
        start = sb("start", [P, 2 * pairs], F32)
        start_i = sb("start_i", [P, 2 * pairs], I32)
        row_i = sb("row_i", [P, 2 * pairs], I32)
        skip_i = sb("skip_i", [P, 2 * pairs], I32)
        skip = sb("skip", [P, 2 * pairs], F32)
        over = sb("over", [P, 2 * pairs], F32)
        sources = sb("sources", [P, 2 * pairs, slots], I32)
        BATCH = 10
        batches = 2 * pairs // BATCH
        src_hi = sb("src_hi", [P, BATCH, slots], I32)
        src_lo = sb("src_lo", [P, BATCH, slots], I32)
        place = sb("place", [P, BATCH, slots], F32)
        inside = sb("inside", [P, BATCH, slots], F32)
        node_keys = sb("node_keys", [P, 2, 2, BATCH, slots], F32)
        scaled = sb("scaled", [P, 4, dim], F32)
        rest = sb("rest", [P, 4, dim], F32)
        deg_ready = sem("deg_ready")
        offsets_ready = sem("offsets_ready")
        csr_link = sem("csr_link")
        roots_ready = sem("roots_ready")
        inverses_ready = sem("inverses_ready")
        rows_ready = sem("rows_ready")
        fetched = [sem(f"fetched{n}") for n in range(batches)]
        keys_ready = sem("keys_ready")
        keys_turned = sem("keys_turned")
        keys_out = sem("keys_out")
        flag_summed = sem("flag_summed")
        normal_ready = sem("normal_ready")
        messages_ready = sem("messages_ready")
        high_ready = sem("high_ready")
        rest_ready = sem("rest_ready")
        middle_ready = sem("middle_ready")
        low_ready = sem("low_ready")
        feat_stored = sem("feat_stored")
        hs_stored = [sem(f"first_hs_stored{b}") for b in range(4)]
        assert 2 * pairs % BATCH == 0 and BATCH % 2 == 0

        def feat_row(t):
            return feat[:, bass.ds(t, 1), :].rearrange("p a d -> p (a d)")

        with nc.Block() as block:
            @block.tensor
            def _(pe):
                pe.wait_ge(deg_ready, 1)
                nc.tensor.matmul(bank[0][:, 0:2 * pairs], upper[:, :], deg[:, :], start=True, stop=True).then_inc(offsets_ready, 1)
                nc.tensor.matmul(bank[1][:, 0:2 * pairs], ones[:, :], deg[:, :], start=True, stop=True).then_inc(offsets_ready, 1)
                pe.wait_ge(rows_ready, 2)
                nc.tensor.matmul(bank[2][:, 0:3], ones[:, :], disorder[:, :], start=True, stop=True).then_inc(flag_summed, 1)
                for i in range(pairs):
                    n, j = divmod(2 * i, BATCH)
                    b = bank[4 + i % 4]
                    pe.wait_ge(keys_ready, n + 1)
                    if i >= 4:
                        pe.wait_ge(keys_out, i - 3)
                    for k in range(2):
                        tr = nc.tensor.transpose(b[:, k * P:(k + 1) * P], node_keys[:, n % 2, k, j:j + 2, :].rearrange("p t s -> p (t s)"), ident[:, :])
                    tr.then_inc(keys_turned, 1)

            @block.gpsimd
            def _(pool):
                pool.wait_ge(rows_ready, 1)
                for t in range(tiles):
                    pool.indirect_dma_start(sources[:, t, :], None, src_rows, bass.IndirectOffsetOnAxis(ap=row_i[:, t:t + 1], axis=0)).then_inc(fetched[t // BATCH], 16)

            @block.scalar
            def _(act):
                act.wait_ge(inverses_ready, 1)
                nc.scalar.activation(dis[:, :], deg[:, 0:tiles], ACT.Sqrt, bias=1.0).then_inc(roots_ready, 1)
                nc.scalar.activation(rstd[:, :], row_squares[:, :], ACT.Sqrt, bias=eps_col[:, 0:1], scale=1.0 / dim).then_inc(roots_ready, 1)
                act.wait_ge(inverses_ready, 3)

                def turn_out(i):
                    act.wait_ge(keys_turned, i + 1)
                    nc.scalar.activation(keys_t[:, i, :, :].rearrange("p k n -> p (k n)"), bank[4 + i % 4][:, 0:2 * P], ACT.Copy).then_inc(keys_out, 1)

                for t in range(tiles):
                    b = t % 4
                    nc.scalar.activation(feat[:, t, :], feat[:, t, :], ACT.Copy, scale=rstd[:, t:t + 1]).then_inc(normal_ready, 1)
                    if t >= 4:
                        act.wait_ge(low_ready, t - 3)
                        act.wait_ge(hs_stored[b], 16 * (t // 4))
                    act.wait_ge(normal_ready, t + 1)
                    nc.scalar.activation(scaled[:, b, :], feat[:, t, :], ACT.Copy, scale=dis[:, t:t + 1]).then_inc(messages_ready, 1)
                    act.wait_ge(messages_ready, t + 1)
                    nc.scalar.activation(parts[:, t, 0:dim], scaled[:, b, :], ACT.Copy).then_inc(high_ready, 1)
                    if t >= 1:
                        act.wait_ge(rest_ready, t)
                        nc.scalar.activation(parts[:, t - 1, dim:2 * dim], rest[:, (t - 1) % 4, :], ACT.Copy).then_inc(middle_ready, 1)
                t = tiles
                act.wait_ge(rest_ready, t)
                nc.scalar.activation(parts[:, t - 1, dim:2 * dim], rest[:, (t - 1) % 4, :], ACT.Copy).then_inc(middle_ready, 1)
                for i in range(pairs):
                    turn_out(i)

            @block.sync
            def _(sp):
                for t in range(tiles):
                    sp.wait_ge(messages_ready, t + 1)
                    sp.dma_start(hs_table[0][t * P:(t + 1) * P, :], scaled[:, t % 4, :]).then_inc(hs_stored[t % 4], 16)
                sp.wait_ge(normal_ready, tiles)
                sp.dma_start(feat_table[0][0:padded, :].rearrange("(t p) d -> p t d", p=P), feat[:, :, :]).then_inc(feat_stored, 16)
                for b in range(4):
                    sp.wait_ge(hs_stored[b], 16 * len(range(b, tiles, 4)))
                sp.wait_ge(feat_stored, 16)

            @block.vector
            def _(dve):
                link = Link(dve, csr_link)
                nc.vector.memset(parts[:, tiles, :], 0.0)
                nc.vector.memset(sources[:, tiles, :], 0)
                nc.vector.memset(zeros[:, :], 0.0)
                link(nc.vector.memset(deg[:, tiles:], 0.0))
                link(nc.vector.tensor_copy(deg[:, 0:tiles], bank[0][:, 0:tiles]))
                nc.vector.tensor_tensor(deg[:, tiles - 1:tiles], deg[:, tiles - 1:tiles], real[:, :], ALU.mult).then_inc(deg_ready, 1)
                dve.wait_ge(deg_ready, 1)
                dve.sem_inc(inverses_ready, 1)
                dve.wait_ge(offsets_ready, 2)
                link(nc.vector.tensor_copy(total[:, :], bank[1][:, 0:2 * pairs]))
                link(nc.vector.tensor_tensor_scan(start[:, :], total[:, :], zeros[:, :], 0.0, ALU.add, ALU.add))
                link(nc.vector.tensor_tensor(start[:, :], start[:, :], total[:, :], ALU.subtract))
                link(nc.vector.tensor_tensor(start[:, :], start[:, :], bank[0][:, 0:2 * pairs], ALU.add))
                link(nc.vector.tensor_copy(start_i[:, :], start[:, :]))
                nc.vector.tensor_scalar(row_i[:, :], start_i[:, :], align.bit_length() - 1, None, ALU.logical_shift_right).then_inc(rows_ready, 1)
                link(nc.vector.tensor_scalar(skip_i[:, :], start_i[:, :], align - 1, None, ALU.bitwise_and))
                link(nc.vector.tensor_copy(skip[:, :], skip_i[:, :]))
                link(nc.vector.tensor_tensor(over[:, :], skip[:, :], deg[:, :], ALU.add))
                link(nc.vector.tensor_scalar(over[:, :], over[:, :], float(slots), None, ALU.is_gt))
                nc.vector.tensor_reduce(disorder[:, 2:3], over[:, :], AX, ALU.add).then_inc(rows_ready, 1)
                dve.wait_ge(roots_ready, 2)
                nc.vector.reciprocal(dis[:, :], dis[:, :]).then_inc(inverses_ready, 1)
                nc.vector.reciprocal(rstd[:, :], rstd[:, :]).then_inc(inverses_ready, 1)
                dve.wait_ge(flag_summed, 1)
                link(nc.vector.tensor_reduce(over[:, 0:1], bank[2][:, 0:3], AX, ALU.add))
                link(nc.vector.tensor_scalar(over[:, 0:1], over[:, 0:1], 1.0, None, ALU.min))
                link(nc.vector.tensor_copy(flag[:, :], over[:, 0:1]))
                dve.wait_ge(iotas_made, 3)

                def split(t):
                    b = t % 4
                    dve.wait_ge(high_ready, t + 1)
                    nc.vector.tensor_tensor(rest[:, b, :], scaled[:, b, :], parts[:, t, 0:dim], ALU.subtract).then_inc(rest_ready, 1)
                    dve.wait_ge(middle_ready, t + 1)
                    nc.vector.tensor_tensor(parts[:, t, 2 * dim:3 * dim], rest[:, b, :], parts[:, t, dim:2 * dim], ALU.subtract).then_inc(low_ready, 1)

                def batch_keys(n):
                    ts = slice(n * BATCH, (n + 1) * BATCH)

                    def each_slot(v):
                        return v[:, ts].unsqueeze(2).to_broadcast([P, BATCH, slots])

                    dve.wait_ge(fetched[n], 16 * (min((n + 1) * BATCH, tiles) - n * BATCH))
                    if n >= 1:
                        dve.wait_ge(keys_ready, n)
                    if n >= 2:
                        dve.wait_ge(keys_turned, (n - 1) * BATCH // 2)
                    nc.vector.tensor_scalar(src_hi[:, :, :], sources[:, ts, :], 7, None, ALU.logical_shift_right)
                    nc.vector.tensor_scalar(src_lo[:, :, :], sources[:, ts, :], P - 1, None, ALU.bitwise_and)
                    link(nc.vector.tensor_tensor(place[:, :, :], iota_slot[:, :].unsqueeze(1).to_broadcast([P, BATCH, slots]), each_slot(skip), ALU.subtract))
                    link(nc.vector.tensor_tensor(inside[:, :, :], place[:, :, :], each_slot(deg), ALU.is_lt))
                    link(nc.vector.scalar_tensor_tensor(inside[:, :, :], place[:, :, :], 0.0, inside[:, :, :], ALU.is_ge, ALU.mult))
                    link(nc.vector.scalar_tensor_tensor(node_keys[:, n % 2, 0, :, :], inside[:, :, :], -float(P), src_hi[:, :, :], ALU.mult, ALU.add))
                    odd = node_keys[:, n % 2, 0, :, :].rearrange("p (t o) s -> p t o s", o=2)[:, :, 1, :]
                    link(nc.vector.tensor_scalar(odd, odd, float(tiles), None, ALU.add))
                    nc.vector.tensor_copy(node_keys[:, n % 2, 1, :, :], src_lo[:, :, :]).then_inc(keys_ready, 1)

                for t in range(tiles):
                    split(t)
                for n in range(batches):
                    batch_keys(n)
        close_scope()

        def gather_sum(l):
            index_ready = sem(f"index_ready{l}")
            rows_t_ready = sem(f"rows_t_ready{l}")
            same_ready = sem(f"same_ready{l}")
            count_ready = sem(f"count_ready{l}")
            target_ready = sem(f"target_ready{l}")
            hs_gathered = sem(f"hs_gathered{l}")
            agg_gathered = sem(f"agg_gathered{l}")
            summed = sem(f"summed{l}")
            added = sem(f"added{l}")
            scattered = sem(f"scattered{l}")
            passed = sem(f"passed{l}")
            edges_back = sem(f"edges_back{l}")
            open_scope()
            src_sb = sb(f"gs_src{l}", [P, cols], I32)
            dst_sb = sb(f"gs_dst_all{l}", [P, cols], I32)
            lower = sb(f"gs_lower{l}", [P, P], F32)
            index = sb(f"gs_index{l}", [P, 3], I32)
            gs_dst = sb(f"gs_dst{l}", [P, 1], F32)
            gs_count = sb(f"gs_count{l}", [P, 1], F32)
            gs_same = sb(f"gs_same{l}", [P, P], F32)
            gs_before = sb(f"gs_before{l}", [P, P], F32)
            gs_hs = sb(f"gs_hs{l}", [P, dim], F32)
            gs_agg = sb(f"gs_agg{l}", [P, dim], F32)
            lower_set = sem(f"lower_set{l}")
            with nc.Block() as block:
                @block.gpsimd
                def _(pool):
                    pool.dma_start(agg_table[l][0:padded, :], hs_table[l][0:padded, :]).then_inc(scattered, 16)
                    nc.gpsimd.memset(lower[:, :], 1.0).then_inc(lower_set, 1)
                    pool.wait_ge(lower_set, 1)
                    nc.gpsimd.affine_select(out=lower[:, :], in_=lower[:, :], compare_op=ALU.is_gt, fill=0.0,
                                            base=0, pattern=[[-1, P]], channel_multiplier=1).then_inc(lower_set, 1)
                    with pool.Fori(0, cols) as c:
                        pool.wait_ge(index_ready, 3 * c + 3)
                        pool.wait_ge(scattered, 16 * c + 16)
                        pool.sem_inc(passed, 1)
                        pool.indirect_dma_start(gs_hs[:, :], None, hs_table[l], bass.IndirectOffsetOnAxis(ap=index[:, 0:1], axis=0)).then_inc(hs_gathered, 16)
                        pool.indirect_dma_start(gs_agg[:, :], None, agg_table[l], bass.IndirectOffsetOnAxis(ap=index[:, 1:2], axis=0)).then_inc(agg_gathered, 16)
                        pool.wait_ge(target_ready, c + 1)
                        pool.wait_ge(added, c + 1)
                        pool.sem_inc(passed, 1)
                        pool.indirect_dma_start(agg_table[l], bass.IndirectOffsetOnAxis(ap=index[:, 2:3], axis=0), gs_agg[:, :], None,
                                                bounds_check=padded - 1, oob_is_err=False).then_inc(scattered, 16)
                    pool.wait_ge(scattered, 16 * (cols + 1))

                @block.tensor
                def _(pe):
                    with pe.Fori(0, cols) as c:
                        pe.wait_ge(index_ready, 3 * c + 3)
                        nc.tensor.transpose(bank[0][:, 0:P], gs_dst[:, 0:1].to_broadcast([P, P]), ident[:, :]).then_inc(rows_t_ready, 1)
                        pe.wait_ge(same_ready, c + 1)
                        pe.wait_ge(hs_gathered, 16 * c + 16)
                        nc.tensor.matmul(bank[1][:, 0:dim], gs_same[:, :], gs_hs[:, :], start=True, stop=True).then_inc(summed, 1)

                @block.sync
                def _(sp):
                    sp.dma_start(src_sb[:, :], src_pad.rearrange("(p c) -> p c", c=cols)).then_inc(edges_back, 16)
                    sp.dma_start(dst_sb[:, :], dst_pad.rearrange("(p c) -> p c", c=cols)).then_inc(edges_back, 16)

                @block.vector
                def _(dve):
                    dve.wait_ge(edges_back, 32)
                    dve.wait_ge(lower_set, 2)
                    with dve.Fori(0, cols) as c:
                        dve.wait_ge(scattered, 16 * c + 16)
                        nc.vector.tensor_copy(index[:, 0:1], src_sb[:, bass.ds(c, 1)]).then_inc(index_ready, 1)
                        nc.vector.tensor_copy(index[:, 1:2], dst_sb[:, bass.ds(c, 1)]).then_inc(index_ready, 1)
                        nc.vector.tensor_copy(gs_dst[:, :], dst_sb[:, bass.ds(c, 1)]).then_inc(index_ready, 1)
                        dve.wait_ge(rows_t_ready, c + 1)
                        nc.vector.tensor_scalar(gs_same[:, :], bank[0][:, 0:P], gs_dst[:, 0:1], None, ALU.is_equal).then_inc(same_ready, 1)
                        dve.wait_ge(same_ready, c + 1)
                        nc.vector.tensor_tensor(gs_before[:, :], gs_same[:, :], lower[:, :], ALU.mult).then_inc(count_ready, 1)
                        dve.wait_ge(count_ready, 3 * c + 1)
                        nc.vector.tensor_reduce(gs_count[:, :], gs_before[:, :], AX, ALU.add).then_inc(count_ready, 1)
                        dve.wait_ge(count_ready, 3 * c + 2)
                        nc.vector.scalar_tensor_tensor(gs_count[:, :], gs_count[:, :], float(FAR), gs_dst[:, :], ALU.mult, ALU.add).then_inc(count_ready, 1)
                        dve.wait_ge(count_ready, 3 * c + 3)
                        nc.vector.tensor_copy(index[:, 2:3], gs_count[:, :]).then_inc(target_ready, 1)
                        dve.wait_ge(summed, c + 1)
                        dve.wait_ge(agg_gathered, 16 * c + 16)
                        nc.vector.tensor_tensor(gs_agg[:, :], gs_agg[:, :], bank[1][:, 0:dim], ALU.add).then_inc(added, 1)

            close_scope()

        QUAD = 4
        quads = P // QUAD
        UNITS = 2 * (tiles + 1)
        half_bank = 2

        def sum_units(pe, counts, b, i, lo, hi, sums_out, sums_ready, first):
            for n in range(lo, hi):
                o, s = divmod(n, tiles + 1)
                acc = bank[half_bank + o]
                if s == 0 and not first:
                    pe.wait_ge(sums_out, 2 * i + o - 1)
                if s < tiles:
                    lhs, rhs = counts[:, b, s, o * P:(o + 1) * P], parts[:, s, :]
                else:
                    lhs, rhs = ident_bf[:, :], parts[:, bass.ds(i * 2 + o, 1), :].rearrange("p a d -> p (a d)")
                nc.tensor.matmul(acc[:, 0:2 * dim], lhs, rhs[:, 0:2 * dim], start=s == 0, stop=False)
                mm = nc.tensor.matmul(acc[:, 0:dim], lhs, rhs[:, 2 * dim:3 * dim], start=False, stop=s == tiles)
                if s == tiles:
                    mm.then_inc(sums_ready, 1)

        def sums_middle(act, i, o, sums_ready, middle_out, middle, sums_out, first):
            act.wait_ge(sums_ready, 2 * i + o + 1)
            if not first:
                act.wait_ge(sums_out, 2 * i + o - 1)
            nc.scalar.activation(middle[:, o, :], bank[half_bank + o][:, dim:2 * dim], ACT.Copy).then_inc(middle_out, 1)

        def sums_high(dve, i, o, middle_out, middle, sums, sums_out, sums_stored, first):
            dve.wait_ge(middle_out, 2 * i + o + 1)
            if not first:
                dve.wait_ge(sums_stored[o], 16 * i)
            nc.vector.tensor_tensor(sums[:, o, :], middle[:, o, :], bank[half_bank + o][:, 0:dim], ALU.add).then_inc(sums_out, 1)

        def count_and_sum():
            layer = 0
            keys_copied = sem("keys_copied")
            rows_ready = sem("onehot_rows_ready")
            quad_ready = sem("quad_ready")
            quad_out = sem("quad_out")
            sums_ready = sem("sums_ready0")
            sums_out = sem("sums_out0")
            middle_out = sem("middle_out0")
            counts_stored = [sem(f"counts_stored{b}") for b in range(2)]
            sums_stored = [sem(f"sums_stored0_{b}") for b in range(2)]
            RING = 4
            open_scope()
            counts = sb("counts", [P, 2, tiles, 2 * P], BF16)
            keys = sb("pair_keys", [P, 2, 2, P], F32)
            rows_lo = sb("rows_lo", [P, RING, QUAD, P], BF16)
            rows_hi = sb("rows_hi", [P, RING, QUAD, width], BF16)
            middle = sb("middle", [P, 2, dim], F32)
            sums = sb("sums", [P, 2, dim], F32)

            with nc.Block() as block:
                @block.tensor
                def _(pe):
                    def build(q, i, first):
                        pe.wait_ge(rows_ready, i * quads + (q + 1))
                        if not (first and q < RING):
                            pe.wait_ge(quad_out, i * quads + (q + 1 - RING))
                        for u in range(QUAD):
                            mm = nc.tensor.matmul(bank[4 + q % 4][:, u * width:(u + 1) * width], rows_lo[:, q % RING, u, :],
                                                  rows_hi[:, q % RING, u, :], start=True, stop=True)
                        mm.then_inc(quad_ready, 1)

                    def sum_pair(i, b, first, more):
                        pe.wait_ge(quad_out, i * quads + quads)
                        for q in range(quads):
                            if more:
                                build(q, i + 1, False)
                            sum_units(pe, counts, b, i, q * UNITS // quads, (q + 1) * UNITS // quads, sums_out, sums_ready, first)

                    for q in range(quads):
                        build(q, 0, True)
                    sum_pair(0, 0, True, True)
                    sum_pair(1, 1, False, True)
                    with pe.Fori(1, pairs // 2) as j:
                        sum_pair(j * 2, 0, False, True)
                        sum_pair(j * 2 + 1, 1, False, True)
                    sum_pair(pairs - 1, 0, False, False)

                @block.vector
                def _(dve):
                    def rows_of_quad(q, i, b, first):
                        if not (first and q < RING):
                            dve.wait_ge(quad_ready, i * quads + (q + 1 - RING))
                        for u in range(QUAD):
                            n = q * QUAD + u
                            nc.vector.tensor_scalar(rows_lo[:, q % RING, u, :], iota_lo[:, :], keys[:, b, 1, n:n + 1], None, ALU.is_equal)
                            last = nc.vector.tensor_scalar(rows_hi[:, q % RING, u, :], iota_hi[:, :], keys[:, b, 0, n:n + 1], None, ALU.is_equal)
                        last.then_inc(rows_ready, 1)

                    def pair(i, b, first, second=False):
                        nc.vector.tensor_copy(keys[:, b, :, :].rearrange("p k n -> p (k n)"),
                                              keys_t[:, bass.ds(i, 1), :, :].rearrange("p a k n -> p (a k n)")).then_inc(keys_copied, 1)
                        dve.wait_ge(keys_copied, i + 1)
                        for q in range(quads):
                            rows_of_quad(q, i, b, first)
                            if q == 3 and not first and not second:
                                sums_high(dve, i - 2, 1, middle_out, middle, sums, sums_out, sums_stored, third)
                            if q == quads // 2 + 5 and not first:
                                sums_high(dve, i - 1, 0, middle_out, middle, sums, sums_out, sums_stored, second)

                    third = True
                    pair(0, 0, True)
                    pair(1, 1, False, True)
                    pair(2, 0, False)
                    third = False
                    pair(3, 1, False)
                    with dve.Fori(2, pairs // 2) as j:
                        pair(j * 2, 0, False)
                        pair(j * 2 + 1, 1, False)
                    pair(pairs - 1, 0, False)
                    sums_high(dve, pairs - 2, 1, middle_out, middle, sums, sums_out, sums_stored, False)
                    sums_high(dve, pairs - 1, 0, middle_out, middle, sums, sums_out, sums_stored, False)
                    sums_high(dve, pairs - 1, 1, middle_out, middle, sums, sums_out, sums_stored, False)

                @block.scalar
                def _(act):
                    def quad(q, i, b):
                        act.wait_ge(quad_ready, i * quads + (q + 1))
                        nc.scalar.activation(
                            counts[:, b, :, :].rearrange("p s (o n) -> p n o s", o=2)[:, q * QUAD:(q + 1) * QUAD, :, :],
                            bank[4 + q % 4][:, 0:QUAD * width].rearrange("p (n o s) -> p n o s", o=2, s=tiles), ACT.Copy).then_inc(quad_out, 1)

                    def pair(i, b, first, second=False):
                        if not first and not second:
                            act.wait_ge(counts_stored[b], stored_before(i))
                        for q in range(quads):
                            if q == 0 and not first and not second:
                                act.wait_ge(sums_ready, 2 * i - 2)
                                sums_middle(act, i - 2, 1, sums_ready, middle_out, middle, sums_out, third)
                            quad(q, i, b)
                            if q == quads // 2 + 2 and not first:
                                sums_middle(act, i - 1, 0, sums_ready, middle_out, middle, sums_out, second)

                    def stored_before(i):
                        return i // 2 * 16 if isinstance(i, int) else halves * 16

                    third = True
                    pair(0, 0, True)
                    pair(1, 1, False, True)
                    pair(2, 0, False)
                    third = False
                    pair(3, 1, False)
                    with act.Fori(2, pairs // 2) as j:
                        halves = j
                        pair(j * 2, 0, False)
                        pair(j * 2 + 1, 1, False)
                    pair(pairs - 1, 0, False)
                    sums_middle(act, pairs - 2, 1, sums_ready, middle_out, middle, sums_out, False)
                    sums_middle(act, pairs - 1, 0, sums_ready, middle_out, middle, sums_out, False)
                    sums_middle(act, pairs - 1, 1, sums_ready, middle_out, middle, sums_out, False)

                @block.sync
                def _(sp):
                    def store_counts(i, b):
                        sp.wait_ge(quad_out, i * quads + quads)
                        sp.dma_start(counts_table[bass.ds(i, 1), :, :].rearrange("a p n -> p (a n)"),
                                     counts[:, b, :, :].rearrange("p s n -> p (s n)")).then_inc(counts_stored[b], 16)

                    def store_sums(i):
                        for o in range(2):
                            sp.wait_ge(sums_out, 2 * i + o + 1)
                            sp.dma_start(agg_table[layer][bass.ds(i * (2 * P) + o * P, P), :], sums[:, o, :]).then_inc(sums_stored[o], 16)

                    store_counts(0, 0)
                    with sp.Fori(0, pairs // 2) as j:
                        store_counts(j * 2 + 1, 1)
                        store_sums(j * 2)
                        store_counts(j * 2 + 2, 0)
                        store_sums(j * 2 + 1)
                    store_sums(pairs - 1)
                    for s, n in ((counts_stored[0], pairs - pairs // 2), (counts_stored[1], pairs // 2), (sums_stored[0], pairs), (sums_stored[1], pairs)):
                        sp.wait_ge(s, 16 * n)
            close_scope()

        def sum_by_counts(l):
            counts_back = [sem(f"counts_back{l}_{b}") for b in range(2)]
            sums_ready = sem(f"sums_ready{l}")
            sums_out = sem(f"sums_out{l}")
            middle_out = sem(f"middle_out{l}")
            sums_stored = [sem(f"sums_stored{l}_{b}") for b in range(2)]
            open_scope()
            counts = sb(f"counts{l}", [P, 2, tiles, 2 * P], BF16)
            middle = sb(f"middle{l}", [P, 2, dim], F32)
            sums = sb(f"sums{l}", [P, 2, dim], F32)

            def by_pairs(eng, body):
                body(0, 0, 0, True)
                body(1, 0, 1, False)
                with eng.Fori(1, pairs // 2) as j:
                    body(j * 2, j, 0, False)
                    body(j * 2 + 1, j, 1, False)
                body(pairs - 1, pairs // 2, 0, False)

            with nc.Block() as block:
                @block.sync
                def _(sp):
                    def load(i, j, b, first):
                        if not (isinstance(i, int) and i < 2):
                            sp.wait_ge(sums_ready, 2 * i - 2)
                        sp.dma_start(counts[:, b, :, :].rearrange("p s n -> p (s n)"),
                                     counts_table[bass.ds(i, 1), :, :].rearrange("a p n -> p (a n)")).then_inc(counts_back[b], 16)
                    by_pairs(sp, load)

                @block.tensor
                def _(pe):
                    def pair(i, j, b, first):
                        pe.wait_ge(counts_back[b], j * 16 + 16)
                        sum_units(pe, counts, b, i, 0, UNITS, sums_out, sums_ready, first)
                    by_pairs(pe, pair)

                @block.scalar
                def _(act):
                    def pair(i, j, b, first):
                        for o in range(2):
                            sums_middle(act, i, o, sums_ready, middle_out, middle, sums_out, first)
                    by_pairs(act, pair)

                @block.vector
                def _(dve):
                    def pair(i, j, b, first):
                        for o in range(2):
                            sums_high(dve, i, o, middle_out, middle, sums, sums_out, sums_stored, first)
                    by_pairs(dve, pair)

                @block.gpsimd
                def _(pool):
                    with pool.Fori(0, pairs) as i:
                        for o in range(2):
                            pool.wait_ge(sums_out, 2 * i + o + 1)
                            pool.dma_start(agg_table[l][bass.ds(i * (2 * P) + o * P, P), :], sums[:, o, :]).then_inc(sums_stored[o], 16)
                    for o in range(2):
                        pool.wait_ge(sums_stored[o], 16 * pairs)
            close_scope()

        def update_nodes(l):
            last = l == layers - 1
            agg_loaded = [sem(f"agg_loaded{l}_{b}") for b in range(2)]
            x_back = [sem(f"x_back{l}_{b}") for b in range(2)]
            turned_ready = sem(f"turned_ready{l}")
            turned_out = sem(f"turned_out{l}")
            products_ready = sem(f"products_ready{l}")
            res_out = sem(f"res_out{l}")
            sum_ready = sem(f"sum_ready{l}")
            feat_ready = sem(f"feat_ready{l}")
            hs_ready = sem(f"hs_ready{l}")
            hs_stored = [sem(f"hs_stored{l}_{b}") for b in range(2)]
            x_cleared = sem(f"x_cleared{l}")
            split_hi = sem(f"split_hi{l}")
            split_mid = sem(f"split_mid{l}")
            rest_ready = sem(f"rest_ready{l}")
            split_lo = sem(f"split_lo{l}")
            open_scope()
            agg_tile = sb(f"agg_tile{l}", [P, 2, dim], F32)
            feat_tile = sb(f"feat_tile{l}", [P, 2, dim], F32)
            feat_out = sb(f"feat_out{l}", [P, 2, dim], F32)
            turned = sb(f"turned{l}", [P, 2, 4, P], F32)
            res_part = sb(f"res_part{l}", [P, 2, dim], F32)
            layer_sum = sb(f"layer_sum{l}", [P, 2, dim], F32)
            x_tile = sb(f"x_tile{l}", [P, 2, dim], F32)
            scaled = sb(f"scaled{l}", [P, 2, dim], F32)
            rest = sb(f"rest{l}", [P, 2, dim], F32)

            def each(eng, body):
                with eng.Fori(0, tiles // 2) as u:
                    body(u * 2, u, 0)
                    body(u * 2 + 1, u, 1)
                body(tiles - 1, tiles // 2, 0)

            def featc(t):
                return feat[:, bass.ds(t, 1), :].rearrange("p a d -> p (a d)")

            def part(t, i):
                return parts[:, bass.ds(t, 1), i * dim:(i + 1) * dim].rearrange("p a d -> p (a d)")

            with nc.Block() as block:
                @block.sync
                def _(sp):
                    def first(t):
                        sp.dma_start(agg_tile[:, t, :], agg_table[l][t * P:(t + 1) * P, :]).then_inc(agg_loaded[t], 16)
                        sp.dma_start(feat_tile[:, t, :], feat_table[l][t * P:(t + 1) * P, :]).then_inc(agg_loaded[t], 16)
                        if last:
                            sp.dma_start(x_tile[:, t, :], x[t * P:(t + 1) * P, :]).then_inc(x_back[t], 16)

                    def later(t, b):
                        sp.wait_ge(turned_ready, t - 1)
                        sp.dma_start(agg_tile[:, b, :], agg_table[l][bass.ds(t * P, P), :]).then_inc(agg_loaded[b], 16)
                        sp.dma_start(feat_tile[:, b, :], feat_table[l][bass.ds(t * P, P), :]).then_inc(agg_loaded[b], 16)
                        if last:
                            sp.wait_ge(feat_ready, t - 1)
                            sp.dma_start(x_tile[:, b, :], x[bass.ds(t * P, P), :]).then_inc(x_back[b], 16)

                    first(0)
                    first(1)
                    with sp.Fori(1, tiles // 2) as u:
                        later(u * 2, 0)
                        later(u * 2 + 1, 1)
                    t = tiles - 1
                    sp.wait_ge(turned_ready, t - 1)
                    sp.dma_start(agg_tile[:, 0, :], agg_table[l][t * P:padded, :]).then_inc(agg_loaded[0], 16)
                    sp.dma_start(feat_tile[:, 0, :], feat_table[l][t * P:padded, :]).then_inc(agg_loaded[0], 16)
                    if last:
                        sp.wait_ge(feat_ready, t - 1)
                        sp.wait_ge(x_cleared, 1)
                        sp.dma_start(x_tile[0:last_rows, 0, :], x[full:nodes, :]).then_inc(x_back[0], 16)

                @block.tensor
                def _(pe):
                    def body(t, u, b):
                        turn, prod = bank[b], (bank[2 + b], bank[4 + b])
                        pe.wait_ge(agg_loaded[b], u * 32 + 32)
                        pe.wait_ge(turned_out, t + 1)
                        for k in range(K2):
                            nc.tensor.transpose(turn[:, k * P:(k + 1) * P], agg_tile[:, b, k * P:(k + 1) * P], ident[:, :])
                            mm = nc.tensor.transpose(turn[:, (2 + k) * P:(3 + k) * P], feat_tile[:, b, k * P:(k + 1) * P], ident[:, :])
                        mm.then_inc(turned_ready, 1)
                        pe.wait_ge(turned_out, t + 2)
                        pe.wait_ge(sum_ready, t + 1)
                        for k in range(K2):
                            nc.tensor.matmul(prod[0][:, 0:dim], turned[:, b, k, :], gnn_w_sb[:, l, k, :], start=k == 0, stop=k == K2 - 1)
                        for k in range(K2):
                            nc.tensor.matmul(prod[1][:, 0:dim], turned[:, b, 2 + k, :], res_w_sb[:, k, :], start=k == 0, stop=False)
                        nc.tensor.matmul(prod[1][:, 0:dim], ones_row[:, :], bias_sum[:, l, :], start=False, stop=True).then_inc(products_ready, 1)
                    each(pe, body)

                @block.scalar
                def _(act):
                    act.sem_inc(turned_out, 1)

                    def body(t, u, b):
                        act.wait_ge(turned_ready, t + 1)
                        nc.scalar.activation(turned[:, b, :, :].rearrange("p k d -> p (k d)"), bank[b][:, :], ACT.Copy).then_inc(turned_out, 1)
                        act.wait_ge(products_ready, t + 1)
                        act.wait_ge(sum_ready, t + 1)
                        nc.scalar.activation(res_part[:, b, :], bank[4 + b][:, 0:dim], ACT.Copy).then_inc(res_out, 1)
                        if not last:
                            act.wait_ge(hs_ready, t + 1)
                            nc.scalar.activation(part(t, 0), scaled[:, b, :], ACT.Copy).then_inc(split_hi, 1)
                            act.wait_ge(rest_ready, t + 1)
                            nc.scalar.activation(part(t, 1), rest[:, b, :], ACT.Copy).then_inc(split_mid, 1)
                    each(act, body)

                @block.vector
                def _(dve):
                    dve.sem_inc(sum_ready, 1)

                    def body(t, u, b):
                        dve.wait_ge(res_out, t + 1)
                        nc.vector.scalar_tensor_tensor(layer_sum[:, b, :], bank[2 + b][:, 0:dim], dis[:, bass.ds(t, 1)], res_part[:, b, :],
                                                       ALU.mult, ALU.add).then_inc(sum_ready, 1)
                        dve.wait_ge(sum_ready, t + 2)
                        if last:
                            dve.wait_ge(x_back[b], 16 if u is None else u * 16 + 16)
                            nc.vector.scalar_tensor_tensor(featc(t), layer_sum[:, b, :], 0.0, x_tile[:, b, :], ALU.max, ALU.add).then_inc(feat_ready, 1)
                        else:
                            if u is not None:
                                dve.wait_ge(hs_stored[b], u * 32)
                            nc.vector.tensor_scalar(feat_out[:, b, :], layer_sum[:, b, :], 0.0, None, ALU.max).then_inc(feat_ready, 1)
                            dve.wait_ge(feat_ready, t + 1)
                            nc.vector.tensor_scalar(scaled[:, b, :], feat_out[:, b, :], dis[:, bass.ds(t, 1)], None, ALU.mult).then_inc(hs_ready, 1)
                            dve.wait_ge(split_hi, t + 1)
                            nc.vector.tensor_tensor(rest[:, b, :], scaled[:, b, :], part(t, 0), ALU.subtract).then_inc(rest_ready, 1)
                            dve.wait_ge(split_mid, t + 1)
                            nc.vector.tensor_tensor(part(t, 2), rest[:, b, :], part(t, 1), ALU.subtract).then_inc(split_lo, 1)
                    body(0, None, 0)
                    body(1, None, 1)
                    with dve.Fori(1, tiles // 2) as u:
                        body(u * 2, u, 0)
                        body(u * 2 + 1, u, 1)
                    if last:
                        dve.wait_ge(feat_ready, tiles - 1)
                        nc.vector.memset(x_tile[:, 0, :], 0.0).then_inc(x_cleared, 1)
                    body(tiles - 1, tiles // 2, 0)

                @block.gpsimd
                def _(pool):
                    if not last:
                        def body(t, u, b):
                            pool.wait_ge(hs_ready, t + 1)
                            pool.dma_start(hs_table[l + 1][bass.ds(t * P, P), :], scaled[:, b, :]).then_inc(hs_stored[b], 16)
                            pool.dma_start(feat_table[l + 1][bass.ds(t * P, P), :], feat_out[:, b, :]).then_inc(hs_stored[b], 16)
                        each(pool, body)
                        pool.wait_ge(hs_stored[0], 32 * (tiles - tiles // 2))
                        pool.wait_ge(hs_stored[1], 32 * (tiles // 2))
            close_scope()

        many = nc.values_load(flag[0:1, 0:1], min_val=0, max_val=1)
        for l in range(layers):
            with nc.If(many == 0):
                if l == 0:
                    count_and_sum()
                else:
                    sum_by_counts(l)
            with nc.Else():
                gather_sum(l)
            if l == layers - 1:
                close_scope()
                feat = sb("features", [P, tiles, dim], F32)
            update_nodes(l)

        router_w1_sb = sb("router_w1_sb", [P, K2, router_h], F32)
        router_b1_sb = sb("router_b1_sb", [P, 1], F32)
        router_w2_sb = sb("router_w2_sb", [P, experts], F32)
        router_b2_sb = sb("router_b2_sb", [1, experts], F32)
        w1_sb = sb("w1_sb", [P, experts, K2, dim], F32)
        w2_sb = sb("w2_sb", [P, experts, K2, dim], F32)
        w3_sb = sb("w3_sb", [P, experts, K2, dim], F32)
        b1_sb = sb("b1_sb", [P, experts, K2], F32)
        b2_sb = sb("b2_sb", [P, experts, K2], F32)
        b3_sb = sb("b3_sb", [1, experts, dim], F32)
        y = sb("y", [P, GROUP, dim], F32)
        y_t = sb("y_t", [P, K2, GROUP * P], F32)
        router_t = sb("router_t", [P, GROUP * P], F32)
        h1_t = sb("h1_t", [P, 2, K2, GROUP * P], F32)
        h2_t = sb("h2_t", [P, 2, K2, GROUP * P], F32)
        acc = sb("acc", [P, GROUP, dim], F32)
        g_stats = sb("g_stats", [P, GROUP, 6], F32)
        g_a = sb("g_a", [P, GROUP], F32)
        g_d = sb("g_d", [P, GROUP], F32)
        g_s = sb("g_s", [P, GROUP], F32)
        g_mean = sb("g_mean", [P, GROUP], F32)
        g_rstd = sb("g_rstd", [P, GROUP], F32)
        rank = sb("rank", [P, experts], F32)
        top = sb("top", [P, 6, GROUP], F32)
        prob = sb("prob", [P, GROUP, experts], F32)
        pick = sb("pick", [P, 3, GROUP, experts], F32)
        gate = sb("gate", [P, GROUP, experts], F32)

        ffn_w_loaded = sem("ffn_w_loaded")
        ffn_link = sem("ffn_link")
        ffn_var = sem("ffn_var")
        ffn_std = sem("ffn_std")
        y_ready = sem("y_ready")
        item_ready = sem("item_ready")
        act_out = sem("act_out")
        dve_out = sem("dve_out")
        logits_ready = sem("logits_ready")
        logits_used = sem("logits_used")
        shifted = sem("shifted")
        exped = sem("exped")
        gap_ready = sem("gap_ready")
        gap_exped = sem("gap_exped")
        outs_ready = sem("outs_ready")
        outs_used = sem("outs_used")
        acc_stored = sem("acc_stored")
        acc_free = sem("acc_free")
        rank_made = sem("rank_made")

        RING = 3
        ring, out_bank, logit_bank = bank[0:3], bank[3:7], bank[7]
        items = [("turn", k, n) for k in range(K2) for n in range(2)]
        items += [("route", 0, n) for n in range(2)]
        items += [("h1", 0, m, n) for m in range(K2) for n in range(2)]
        for e in range(experts):
            items += [("h2", e, m, n) for m in range(K2) for n in range(2)]
            if e + 1 < experts:
                items += [("h1", e + 1, m, n) for m in range(K2) for n in range(2)]
        ITEMS = len(items)
        EACH = ITEMS // 2
        FREE = 2
        assert ITEMS % RING == 0 and ITEMS % 2 == 0
        OUTS = experts * 4

        def wait_emptied(eng, g, k):
            s = (act_out, dve_out)[k % 2]
            eng.wait_ge(s, g * EACH + (FREE + k // 2 + 1))

        def wait_all_emptied(eng, g, k):
            wait_emptied(eng, g, k)
            wait_emptied(eng, g, k - 1)

        def index_of(kind, e):
            return max(k for k, it in enumerate(items) if it[0] == kind and it[1] == e)

        def cols_of(n):
            return slice(n * HALF, (n + 1) * HALF)

        with nc.Block() as block:
            @block.tensor
            def _(pe):
                def item(g, k):
                    it = items[k]
                    dstb = ring[k % RING]
                    wait_emptied(pe, g, k - RING)
                    if it[0] == "turn":
                        _, kf, n = it
                        ts = range(4) if n == 0 else range(4, GROUP)
                        for j, t in enumerate(ts):
                            mm = nc.tensor.transpose(dstb[:, j * P:(j + 1) * P], y[:, t, kf * P:(kf + 1) * P], ident[:, :])
                    elif it[0] == "route":
                        for kf in range(K2):
                            mm = nc.tensor.matmul(dstb[:, 0:HALF], router_w1_sb[:, kf, :], y_t[:, kf, cols_of(it[2])], start=kf == 0, stop=kf == K2 - 1)
                    else:
                        kind, e, m, n = it
                        w, source = (w1_sb, y_t[:, :, :]) if kind == "h1" else (w2_sb, h1_t[:, e % 2, :, :])
                        for kf in range(K2):
                            mm = nc.tensor.matmul(dstb[:, 0:HALF], w[:, e, kf, m * P:(m + 1) * P], source[:, kf, cols_of(n)], start=kf == 0, stop=kf == K2 - 1)
                    mm.then_inc(item_ready, 1)

                def outs(g, e):
                    wait_all_emptied(pe, g, index_of("h2", e))
                    for q in range(4):
                        pe.wait_ge(outs_used, g * OUTS + (e * 4 + q + 1))
                        for t in range(2 * q, min(2 * q + 2, GROUP)):
                            o = out_bank[q][:, (t % 2) * dim:(t % 2 + 1) * dim]
                            for kf in range(K2):
                                nc.tensor.matmul(o, h2_t[:, e % 2, kf, t * P:(t + 1) * P], w3_sb[:, e, kf, :], start=kf == 0, stop=False)
                            mm = nc.tensor.matmul(o, ones_row[:, :], b3_sb[:, e, :], start=False, stop=True)
                        mm.then_inc(outs_ready, 1)

                pe.wait_ge(ffn_w_loaded, 16 * (8 + 2 * experts * K2))
                with pe.Fori(0, groups) as g:
                    pe.wait_ge(y_ready, g + 1)
                    for k in range(4):
                        item(g, k)
                    wait_all_emptied(pe, g, 3)
                    for k in range(4, 10):
                        item(g, k)
                    wait_all_emptied(pe, g, 5)
                    pe.wait_ge(logits_used, g + 1)
                    for t in range(GROUP):
                        o = logit_bank[:, t * experts:(t + 1) * experts]
                        nc.tensor.matmul(o, router_t[:, t * P:(t + 1) * P], router_w2_sb[:, :], start=True, stop=False)
                        mm = nc.tensor.matmul(o, ones_row[:, :], router_b2_sb[:, :], start=False, stop=True)
                    mm.then_inc(logits_ready, 1)
                    k = 10
                    for e in range(experts):
                        wait_all_emptied(pe, g, index_of("h1", e))
                        for _i in range(8 if e + 1 < experts else 4):
                            item(g, k)
                            k += 1
                        outs(g, e)

            def empty(eng, g, k):
                it = items[k]
                b = ring[k % RING]
                eng.wait_ge(item_ready, g * ITEMS + (k + 1))
                if it[0] == "turn":
                    n = 4 * P if it[2] == 0 else (GROUP - 4) * P
                    to, bias, frm = y_t[:, it[1], it[2] * 4 * P:it[2] * 4 * P + n], None, b[:, 0:n]
                elif it[0] == "route":
                    to, bias, frm = router_t[:, cols_of(it[2])], router_b1_sb[:, 0:1], b[:, 0:HALF]
                else:
                    kind, e, m, n = it
                    h, bb = (h1_t, b1_sb) if kind == "h1" else (h2_t, b2_sb)
                    to, bias, frm = h[:, e % 2, m, cols_of(n)], bb[:, e, m:m + 1], b[:, 0:HALF]
                if k % 2 == 0:
                    if bias is None:
                        ins = nc.scalar.activation(to, frm, ACT.Copy)
                    else:
                        ins = nc.scalar.activation(to, frm, ACT.Relu, bias=bias)
                    ins.then_inc(act_out, 1)
                else:
                    if bias is None:
                        ins = nc.vector.tensor_copy(to, frm)
                    else:
                        ins = nc.vector.tensor_scalar(to, frm, bias, 0.0, ALU.add, ALU.max)
                    ins.then_inc(dve_out, 1)

            @block.scalar
            def _(act):
                act.sem_inc(act_out, FREE)
                act.wait_ge(ffn_w_loaded, 16 * (8 + 2 * experts * K2))
                with act.Fori(0, groups) as g:
                    act.wait_ge(ffn_var, g + 1)
                    nc.scalar.activation(g_rstd[:, :], g_s[:, :], ACT.Sqrt, bias=eps_col[:, 0:1], scale=1.0 / dim).then_inc(ffn_std, 1)
                    for k in range(0, 10, 2):
                        empty(act, g, k)
                    act.wait_ge(shifted, g + 1)
                    nc.scalar.activation(prob[:, :, :], prob[:, :, :], ACT.Exp).then_inc(exped, 1)
                    act.wait_ge(gap_ready, g + 1)
                    nc.scalar.activation(top[:, 4, :], top[:, 4, :], ACT.Exp).then_inc(gap_exped, 1)
                    for k in range(10, ITEMS, 2):
                        empty(act, g, k)

            @block.vector
            def _(dve):
                link = Link(dve, ffn_link)
                for j in range(experts):
                    nc.vector.memset(rank[:, j:j + 1], float(experts - j)).then_inc(rank_made, 1)
                dve.wait_ge(rank_made, experts)
                dve.wait_ge(ffn_w_loaded, 16 * (8 + 2 * experts * K2))
                dve.sem_inc(dve_out, FREE)
                dve.sem_inc(outs_used, 4)
                dve.sem_inc(acc_free, 1)
                dve.sem_inc(logits_used, 1)
                LINKS = GROUP + 6 + GROUP + 4 + 2 + 10 + 1 + 3 + experts * GROUP
                with dve.Fori(0, groups) as g:
                    link.loop(g, LINKS_PER_GROUP)
                    gf = feat[:, bass.ds(g * GROUP, GROUP), :]
                    for t in range(GROUP):
                        nc.vector.bn_stats(g_stats[:, t, :], gf[:, t, :]).then_inc(ffn_link, 1)
                    link.count += GROUP
                    dve.wait_ge(ffn_link, link.count + g * LINKS_PER_GROUP)
                    st = g_stats[:, :, :]
                    link(nc.vector.tensor_tensor(g_a[:, :], st[:, :, 1], st[:, :, 4], ALU.add))
                    link(nc.vector.tensor_tensor(g_d[:, :], st[:, :, 1], st[:, :, 4], ALU.subtract))
                    link(nc.vector.tensor_tensor(g_s[:, :], st[:, :, 2], st[:, :, 5], ALU.add))
                    link(nc.vector.tensor_tensor(g_d[:, :], g_d[:, :], g_d[:, :], ALU.mult))
                    link(nc.vector.tensor_scalar(g_mean[:, :], g_a[:, :], 0.5, None, ALU.mult))
                    nc.vector.scalar_tensor_tensor(g_s[:, :], g_d[:, :], dim / 4.0, g_s[:, :], ALU.mult, ALU.add).then_inc(ffn_var, 1)
                    dve.wait_ge(ffn_std, g + 1)
                    link(nc.vector.reciprocal(g_rstd[:, :], g_rstd[:, :]))
                    for t in range(GROUP):
                        ins = nc.vector.tensor_scalar(y[:, t, :], gf[:, t, :], g_mean[:, t:t + 1], g_rstd[:, t:t + 1], ALU.subtract, ALU.mult)
                    ins.then_inc(y_ready, 1)
                    for k in range(1, 10, 2):
                        empty(dve, g, k)

                    def wide(v):
                        return v.unsqueeze(2).to_broadcast([P, GROUP, experts])

                    logits = logit_bank[:, 0:GROUP * experts].rearrange("p (t e) -> p t e", e=experts)
                    ranks = rank[:, :].unsqueeze(1).to_broadcast([P, GROUP, experts])
                    dve.wait_ge(logits_ready, g + 1)
                    link(nc.vector.tensor_reduce(top[:, 0, :], logits, AX, ALU.max))
                    nc.vector.tensor_tensor(prob[:, :, :], logits, wide(top[:, 0, :]), ALU.subtract).then_inc(shifted, 1)
                    dve.wait_ge(shifted, g + 1)
                    dve.sem_inc(logits_used, 1)
                    dve.wait_ge(exped, g + 1)
                    link(nc.vector.tensor_reduce(top[:, 0, :], prob[:, :, :], AX, ALU.add))
                    link(nc.vector.reciprocal(top[:, 0, :], top[:, 0, :]))
                    link(nc.vector.tensor_tensor(prob[:, :, :], prob[:, :, :], wide(top[:, 0, :]), ALU.mult))
                    for i in range(2):
                        link(nc.vector.tensor_reduce(top[:, 1 + i, :], prob[:, :, :], AX, ALU.max))
                        link(nc.vector.tensor_tensor(pick[:, 2, :, :], prob[:, :, :], wide(top[:, 1 + i, :]), ALU.is_equal))
                        link(nc.vector.tensor_tensor(pick[:, 2, :, :], pick[:, 2, :, :], ranks, ALU.mult))
                        link(nc.vector.tensor_reduce(top[:, 3, :], pick[:, 2, :, :], AX, ALU.max))
                        link(nc.vector.tensor_tensor(pick[:, i, :, :], ranks, wide(top[:, 3, :]), ALU.is_equal))
                        if i == 0:
                            link(nc.vector.scalar_tensor_tensor(prob[:, :, :], pick[:, 0, :, :], -4.0, prob[:, :, :], ALU.mult, ALU.add))
                    nc.vector.tensor_tensor(top[:, 4, :], top[:, 2, :], top[:, 1, :], ALU.subtract).then_inc(gap_ready, 1)
                    dve.wait_ge(gap_exped, g + 1)
                    link(nc.vector.tensor_scalar(top[:, 0, :], top[:, 4, :], 1.0, None, ALU.add))
                    link(nc.vector.reciprocal(top[:, 0, :], top[:, 0, :]))
                    link(nc.vector.tensor_tensor(top[:, 5, :], top[:, 4, :], top[:, 0, :], ALU.mult))
                    link(nc.vector.tensor_tensor(pick[:, 0, :, :], pick[:, 0, :, :], wide(top[:, 0, :]), ALU.mult))
                    link(nc.vector.tensor_tensor(pick[:, 1, :, :], pick[:, 1, :, :], wide(top[:, 5, :]), ALU.mult))
                    link(nc.vector.tensor_tensor(gate[:, :, :], pick[:, 0, :, :], pick[:, 1, :, :], ALU.add))
                    dve.wait_ge(acc_free, g + 1)

                    k = 10
                    for e in range(experts):
                        for _i in range(8 if e + 1 < experts else 4):
                            if k % 2 == 1:
                                empty(dve, g, k)
                            k += 1
                        for q in range(4):
                            dve.wait_ge(outs_ready, g * OUTS + (e * 4 + q + 1))
                            if e:
                                dve.wait_ge(ffn_link, acc_base + (e - 1) * 4 + q + 1 + g * LINKS_PER_GROUP)
                            else:
                                acc_base = link.count if q == 0 else acc_base
                            for t in range(2 * q, min(2 * q + 2, GROUP)):
                                o = out_bank[q][:, (t % 2) * dim:(t % 2 + 1) * dim]
                                ins = nc.vector.scalar_tensor_tensor(acc[:, t, :], o, gate[:, t, e:e + 1], acc[:, t, :] if e else gf[:, t, :], ALU.mult, ALU.add)
                            ins.then_inc(ffn_link, 1)
                            dve.wait_ge(ffn_link, acc_base + e * 4 + q + 1 + g * LINKS_PER_GROUP)
                            dve.sem_inc(outs_used, 1)
                    link.count = acc_base + experts * 4
                    assert link.count - link.start == LINKS_PER_GROUP, link.count - link.start

            @block.gpsimd
            def _(pool):
                for tile, w in ((w1_sb, expert_w1), (w2_sb, expert_w2), (w3_sb, expert_w3)):
                    pool.dma_start(tile[:, :, :, :].rearrange("p e k d -> p (e k) d"), w.rearrange("e (k p) d -> p (e k) d", p=P)).then_inc(ffn_w_loaded, 16)
                pool.dma_start(router_w1_sb[:, :, :], router_w1.rearrange("(k p) d -> p k d", p=P)).then_inc(ffn_w_loaded, 16)
                pool.dma_start(router_w2_sb[:, :], router_w2).then_inc(ffn_w_loaded, 16)
                pool.dma_start(router_b1_sb[:, :], router_b1.rearrange("(p a) -> p a", a=1)).then_inc(ffn_w_loaded, 16)
                pool.dma_start(router_b2_sb[:, :], router_b2.rearrange("(a d) -> a d", a=1)).then_inc(ffn_w_loaded, 16)
                pool.dma_start(b3_sb[:, :, :], expert_b3.rearrange("(a e) d -> a e d", a=1)).then_inc(ffn_w_loaded, 16)
                for e in range(experts):
                    for k in range(K2):
                        pool.dma_start(b1_sb[:, e, k:k + 1], expert_b1[e, k * P:(k + 1) * P].rearrange("(p a) -> p a", a=1)).then_inc(ffn_w_loaded, 16)
                        pool.dma_start(b2_sb[:, e, k:k + 1], expert_b2[e, k * P:(k + 1) * P].rearrange("(p a) -> p a", a=1)).then_inc(ffn_w_loaded, 16)

            @block.sync
            def _(sp):
                done = ACC_BASE + experts * 4
                with sp.Fori(0, groups - 1) as g:
                    sp.wait_ge(ffn_link, g * LINKS_PER_GROUP + done)
                    sp.dma_start(out[bass.ds(g * (GROUP * P), GROUP * P), :].rearrange("(t p) d -> p t d", p=P), acc[:, :, :]).then_inc(acc_stored, 16)
                    sp.wait_ge(acc_stored, 16 * g + 16)
                    sp.sem_inc(acc_free, 1)
                g = groups - 1
                sp.wait_ge(ffn_link, g * LINKS_PER_GROUP + done)
                sp.dma_start(out[g * GROUP * P:full, :].rearrange("(t p) d -> p t d", p=P), acc[:, 0:GROUP - 1, :]).then_inc(acc_stored, 16)
                sp.dma_start(out[full:nodes, :], acc[0:last_rows, GROUP - 1, :]).then_inc(acc_stored, 16)
                sp.wait_ge(acc_stored, 16 * (groups + 1))


LINKS_PER_GROUP = 7 + 5 + 1 + 1 + 3 + 11 + 6 + 24
ACC_BASE = LINKS_PER_GROUP - 24

_INS = ['x', 'src', 'dst', 'L0_gnn_W', 'L0_gnn_b', 'L0_gnn_resW', 'L0_gnn_resb', 'L0_ffn_router_w1', 'L0_ffn_router_b1',
        'L0_ffn_router_w2', 'L0_ffn_router_b2', 'L0_ffn_expert_w1', 'L0_ffn_expert_b1', 'L0_ffn_expert_w2', 'L0_ffn_expert_b2',
        'L0_ffn_expert_w3', 'L0_ffn_expert_b3']


def kernel(**inputs):
    import numpy as _np
    import concourse.bacc as _bacc
    from concourse import mybir as _mybir
    from concourse.bass_utils import run_bass_kernel_spmd as _run

    nc = _bacc.Bacc("TRN2", target_bir_lowering=False, num_devices=1)
    arrays, args = {}, []
    for name in _INS:
        a = _np.ascontiguousarray(inputs[name])
        arrays[f"in_{name}_dram"] = a
        args.append(nc.dram_tensor(f"in_{name}_dram", a.shape, _mybir.dt.from_np(a.dtype), kind="ExternalInput").ap())
    shape = inputs['x'].shape
    args.append(nc.dram_tensor("out_dram", shape, _mybir.dt.float32, kind="ExternalOutput").ap())
    gnn_moe_kernel(nc, *args)
    r = _run(nc, [arrays], core_ids=[0])
    return r.results[0]["out_dram"]
```

```python
from contextlib import ExitStack

import concourse.bass as bass
from concourse import mybir

P = 128
F32 = mybir.dt.float32
BF16 = mybir.dt.bfloat16
I32 = mybir.dt.int32
ALU = mybir.AluOpType
ACT = mybir.ActivationFunctionType
AX = mybir.AxisListType.X
EPS = 1e-5
FAR = 16384


class Link:

    def __init__(self, engine, sem):
        self.engine, self.sem, self.count, self.trip = engine, sem, 0, None

    def loop(self, i, per):
        self.trip, self.per, self.start = i, per, self.count

    def end(self, trips):
        assert self.count - self.start == self.per, (self.count - self.start)
        self.count = self.start + self.per * trips
        self.trip = None

    def __call__(self, ins):
        ins.then_inc(self.sem, 1)
        self.count += 1
        self.wait()

    def wait(self):
        self.engine.wait_ge(self.sem, self.trip * self.per + self.count if self.trip is not None else self.count)


class NodeUpdate:

    def __init__(self, nc, l, last, sb, sem, shapes, tables, dis, both_w, bias_sum, ident, turn_bank, product_bank):
        self.nc, self.l, self.last = nc, l, last
        self.nodes, self.tiles, self.dim = shapes
        self.res_table, self.parts_table, self.x, self.x2_table = tables
        self.dis, self.both_w, self.bias_sum, self.ident = dis, both_w, bias_sum, ident
        self.turn_bank, self.product_bank = turn_bank, product_bank
        dim = self.dim
        self.middle = sb(f"middle{l}", [P, 2, dim], F32)
        self.sums = sb(f"sums{l}", [P, 2, dim], F32)
        self.res_tile = sb(f"res_tile{l}", [P, 2, dim], F32)
        self.layer_sum = sb(f"layer_sum{l}", [P, 2, dim], F32)
        self.sums_ready = sem(f"sums_ready{l}")
        self.middle_out = sem(f"middle_out{l}")
        self.sums_out = sem(f"sums_out{l}")
        self.res_back = [sem(f"res_back{l}_{o}") for o in range(2)]
        self.sum_ready = sem(f"sum_ready{l}")
        if last:
            self.x_tile = sb(f"x_tile{l}", [P, 2, dim], F32)
            self.x2 = sb(f"x2_{l}", [P, 2, dim], F32)
            self.x_back = [sem(f"x_back{l}_{o}") for o in range(2)]
            self.x_cleared = sem(f"x_cleared{l}")
            self.x2_ready = sem(f"x2_ready{l}")
            self.x2_stored = [sem(f"x2_stored{l}_{o}") for o in range(2)]
        else:
            self.x1 = sb(f"x1_{l}", [P, 2, dim], F32)
            self.x1_t = sb(f"x1_t{l}", [P, 2, dim], F32)
            self.res_next = sb(f"res_next{l}", [P, 2, dim], F32)
            self.scaled = sb(f"scaled{l}", [P, 2, dim], F32)
            self.rest = sb(f"rest{l}", [P, 2, dim], F32)
            self.parts_out = sb(f"parts_out{l}", [P, 2, 3 * dim], BF16)
            self.x1_ready = sem(f"x1_ready{l}")
            self.turned_ready = sem(f"turned_ready{l}")
            self.turned_out = sem(f"turned_out{l}")
            self.products_ready = sem(f"products_ready{l}")
            self.res_out = sem(f"res_out{l}")
            self.messages_ready = sem(f"messages_ready{l}")
            self.high_ready = sem(f"high_ready{l}")
            self.rest_ready = sem(f"rest_ready{l}")
            self.middle_ready = sem(f"middle_ready{l}")
            self.low_ready = sem(f"low_ready{l}")
            self.res_stored = [sem(f"res_stored{l}_{o}") for o in range(2)]
            self.parts_stored = [sem(f"parts_stored{l}_{o}") for o in range(2)]

    def load(self, eng, T, o, u, last_tile=False):
        nc, later = self.nc, not (isinstance(T, int) and T < 2)
        if later:
            eng.wait_ge(self.sum_ready, T - 1)
        eng.dma_start(self.res_tile[:, o, :], self.res_table[self.l][bass.ds(T * P, P), :]).then_inc(self.res_back[o], 16)
        if self.last:
            if later:
                eng.wait_ge(self.x2_ready, T - 1)
            if last_tile:
                eng.wait_ge(self.x_cleared, 1)
                eng.dma_start(self.x_tile[0:self.nodes - T * P, o, :], self.x[T * P:self.nodes, :]).then_inc(self.x_back[o], 16)
            else:
                eng.dma_start(self.x_tile[:, o, :], self.x[bass.ds(T * P, P), :]).then_inc(self.x_back[o], 16)

    def add_res(self, dve, T, o, u):
        nc, later = self.nc, not (isinstance(T, int) and T < 2)
        dve.wait_ge(self.sums_out, T + 1)
        dve.wait_ge(self.res_back[o], u * 16 + 16)
        if later:
            dve.wait_ge(self.x2_ready if self.last else self.x1_ready, T - 1)
        nc.vector.scalar_tensor_tensor(self.layer_sum[:, o, :], self.sums[:, o, :], self.dis[:, bass.ds(T, 1)], self.res_tile[:, o, :],
                                       ALU.mult, ALU.add).then_inc(self.sum_ready, 1)

    def add_x(self, dve, T, o, u):
        nc, later = self.nc, not (isinstance(T, int) and T < 2)
        dve.wait_ge(self.sum_ready, T + 1)
        dve.wait_ge(self.x_back[o], u * 16 + 16)
        if later:
            dve.wait_ge(self.x2_stored[o], u * 16)
        nc.vector.scalar_tensor_tensor(self.x2[:, o, :], self.layer_sum[:, o, :], 0.0, self.x_tile[:, o, :], ALU.max, ALU.add).then_inc(self.x2_ready, 1)

    def clear_x(self, dve):
        nc, T = self.nc, self.tiles - 1
        dve.wait_ge(self.x2_ready, T - 1)
        nc.vector.memset(self.x_tile[:, T % 2, :], 0.0).then_inc(self.x_cleared, 1)

    def store_x2(self, eng, T, o):
        eng.wait_ge(self.x2_ready, T + 1)
        eng.dma_start(self.x2_table[bass.ds(T * P, P), :], self.x2[:, o, :]).then_inc(self.x2_stored[o], 16)

    def relu(self, act, T, o):
        nc, later = self.nc, not (isinstance(T, int) and T < 2)
        act.wait_ge(self.sum_ready, T + 1)
        if later:
            act.wait_ge(self.turned_ready, T - 1)
        nc.scalar.activation(self.x1[:, o, :], self.layer_sum[:, o, :], ACT.Relu).then_inc(self.x1_ready, 1)

    def turn(self, pe, T, o):
        nc = self.nc
        pe.wait_ge(self.x1_ready, T + 1)
        if not (isinstance(T, int) and T < 1):
            pe.wait_ge(self.turned_out, T)
        for k in range(self.dim // P):
            mm = nc.tensor.transpose(self.turn_bank[:, k * P:(k + 1) * P], self.x1[:, o, k * P:(k + 1) * P], self.ident[:, :])
        mm.then_inc(self.turned_ready, 1)

    def turned_copy(self, act, T, o):
        nc, later = self.nc, not (isinstance(T, int) and T < 2)
        act.wait_ge(self.turned_ready, T + 1)
        if later:
            act.wait_ge(self.products_ready, T - 1)
        nc.scalar.activation(self.x1_t[:, o, :], self.turn_bank[:, 0:self.dim], ACT.Copy).then_inc(self.turned_out, 1)

    def products(self, pe, T, o):
        nc, K2 = self.nc, self.dim // P
        pe.wait_ge(self.turned_out, T + 1)
        if not (isinstance(T, int) and T < 1):
            pe.wait_ge(self.res_out, T)
            pe.wait_ge(self.messages_ready, T)
        for k in range(K2):
            mm = nc.tensor.matmul(self.product_bank[:, :], self.x1_t[:, o, k * P:(k + 1) * P], self.both_w[:, self.l + 1, k, :], start=k == 0, stop=k == K2 - 1)
        mm.then_inc(self.products_ready, 1)

    def res_and_message(self, dve, T, o, u):
        nc, dim, later = self.nc, self.dim, not (isinstance(T, int) and T < 2)
        dve.wait_ge(self.products_ready, T + 1)
        if later:
            dve.wait_ge(self.res_stored[o], u * 16)
        nc.vector.tensor_tensor(self.res_next[:, o, :], self.product_bank[:, dim:2 * dim], self.bias_sum[:, self.l + 1, :], ALU.add).then_inc(self.res_out, 1)
        if later:
            dve.wait_ge(self.high_ready, T - 1)
            dve.wait_ge(self.rest_ready, T - 1)
        nc.vector.tensor_scalar(self.scaled[:, o, :], self.product_bank[:, 0:dim], self.dis[:, bass.ds(T, 1)], None, ALU.mult).then_inc(self.messages_ready, 1)

    def high_part(self, act, T, o, u):
        nc, dim = self.nc, self.dim
        act.wait_ge(self.messages_ready, T + 1)
        if not (isinstance(T, int) and T < 2):
            act.wait_ge(self.parts_stored[o], u * 16)
        nc.scalar.activation(self.parts_out[:, o, 0:dim], self.scaled[:, o, :], ACT.Copy).then_inc(self.high_ready, 1)

    def rest_of(self, dve, T, o):
        nc, dim = self.nc, self.dim
        dve.wait_ge(self.high_ready, T + 1)
        if not (isinstance(T, int) and T < 2):
            dve.wait_ge(self.low_ready, T - 1)
        nc.vector.tensor_tensor(self.rest[:, o, :], self.scaled[:, o, :], self.parts_out[:, o, 0:dim], ALU.subtract).then_inc(self.rest_ready, 1)

    def middle_part(self, act, T, o):
        nc, dim = self.nc, self.dim
        act.wait_ge(self.rest_ready, T + 1)
        nc.scalar.activation(self.parts_out[:, o, dim:2 * dim], self.rest[:, o, :], ACT.Copy).then_inc(self.middle_ready, 1)

    def low_part(self, dve, T, o):
        nc, dim = self.nc, self.dim
        dve.wait_ge(self.middle_ready, T + 1)
        nc.vector.tensor_tensor(self.parts_out[:, o, 2 * dim:3 * dim], self.rest[:, o, :], self.parts_out[:, o, dim:2 * dim], ALU.subtract).then_inc(self.low_ready, 1)

    def store_next(self, eng, T, o):
        eng.wait_ge(self.res_out, T + 1)
        eng.dma_start(self.res_table[self.l + 1][bass.ds(T * P, P), :], self.res_next[:, o, :]).then_inc(self.res_stored[o], 16)
        eng.wait_ge(self.low_ready, T + 1)
        eng.dma_start(self.parts_table[:, bass.ds(T, 1), :].rearrange("p t d -> p (t d)"), self.parts_out[:, o, :]).then_inc(self.parts_stored[o], 16)

    def wait_stored(self, eng):
        for o in range(2):
            stores = 16 * len(range(o, self.tiles, 2))
            for s in ((self.x2_stored[o],) if self.last else (self.res_stored[o], self.parts_stored[o])):
                eng.wait_ge(s, stores)


def gnn_moe_kernel(nc, x, src, dst, gnn_w, gnn_b, res_w, res_b, router_w1, router_b1, router_w2, router_b2,
                   expert_w1, expert_b1, expert_w2, expert_b2, expert_w3, expert_b3, out):
    nodes, dim = x.shape
    edges = src.shape[0]
    layers = gnn_w.shape[0]
    experts = expert_w1.shape[0]
    router_h = router_w1.shape[1]
    tiles = -(-nodes // P)
    padded = tiles * P
    last_rows = nodes - (tiles - 1) * P
    cols = -(-edges // P)
    last_cols = edges - (P - 1) * cols
    K2 = dim // P
    GROUP = 7
    groups = tiles // GROUP
    HALF = GROUP * P // 2
    pairs = -(-tiles // 2)
    slots = 64
    width = 2 * tiles
    HIST = 28
    hist_steps = -(-cols // HIST)
    assert tiles % GROUP == 0 and router_h == P and dim == 2 * P
    assert hist_steps % 2 == 0 and pairs % 2 == 1 and P * cols - edges >= slots

    ctx = ExitStack()
    with ctx:
        scopes = [ctx]

        def sb(name, shape, dt):
            return scopes[-1].enter_context(nc.sbuf_tensor(name, shape, dt))

        def open_scope():
            scopes.append(ExitStack())

        def close_scope():
            scopes.pop().close()

        def psum(name):
            return ctx.enter_context(nc.psum_tensor(name, [P, 512], F32))

        def sem(name):
            return ctx.enter_context(nc.semaphore(name))

        ident = sb("ident", [P, P], F32)
        ident_bf = sb("ident_bf", [P, P], BF16)
        ones = sb("ones", [P, P], F32)
        eps_col = sb("eps_col", [P, 1], F32)
        dis = sb("dis", [P, tiles], F32)
        flag = sb("flag", [P, 1], I32)
        both_w = sb("both_w", [P, layers, K2, 2 * dim], F32)
        router_w1_sb = sb("router_w1_sb", [P, K2, router_h], F32)
        router_b1_sb = sb("router_b1_sb", [P, 1], F32)
        router_w2_sb = sb("router_w2_sb", [P, experts], F32)
        router_b2_sb = sb("router_b2_sb", [P, experts], F32)
        w1_sb = sb("w1_sb", [P, experts, K2, dim], F32)
        b1_sb = sb("b1_sb", [P, experts, K2], F32)
        b2_sb = sb("b2_sb", [P, experts, K2], F32)
        bias_sum = sb("bias_sum", [P, layers, dim], F32)

        res_table = [nc.dram_tensor(f"res_table{l}", (padded, dim), F32).ap() for l in range(layers)]
        parts_table = nc.dram_tensor("parts_table", (P, tiles, 3 * dim), BF16).ap()
        x2_table = nc.dram_tensor("x2_table", (padded, dim), F32).ap()
        assert layers == 2
        hs_table = [x2_table, x2_table]
        agg_table = [res_table[1], res_table[0]]

        src_pad = nc.dram_tensor("src_pad", (P * cols,), I32).ap()
        dst_pad = nc.dram_tensor("dst_pad", (P * cols,), I32).ap()
        counts_table = nc.dram_tensor("counts_table", (pairs, P, tiles * 2 * P), BF16).ap()

        bank = [psum(f"bank{i}") for i in range(8)]

        def rows_of(table, n):
            return table.rearrange("(t p) d -> p t d", p=P)

        open_scope()
        parts = sb("parts", [P, tiles, 3 * dim], BF16)
        open_scope()
        keys_t = sb("keys_t", [P, pairs, 2, P], BF16)
        iota_lo = sb("iota_lo", [P, P, 2], BF16)
        iota_hi = sb("iota_hi", [P, width, 2], BF16)

        def onehot_rows(rows, keys, iota, n, values):
            k = keys.rearrange("p (i j) -> p i j", j=2).unsqueeze(2).to_broadcast([P, n // 2, values, 2])
            v = iota[:, 0:values, :].unsqueeze(1).to_broadcast([P, n // 2, values, 2])
            return nc.vector.tensor_tensor(rows, k, v, ALU.is_equal)
        open_scope()
        feat = sb("feat", [P, tiles, dim], F32)
        iota_slot = sb("iota_slot", [P, slots], F32)
        deg = sb("deg", [P, 2 * pairs], F32)
        upper = sb("upper", [P, P], F32)
        real = sb("real", [P, 1], F32)
        table_room = sb("table_room", [P, 1], F32)
        row_sum = sb("row_sum", [P, tiles], F32)
        row_mean = sb("row_mean", [P, tiles], F32)
        row_squares = sb("row_squares", [P, tiles], F32)
        rstd = sb("rstd", [P, tiles], F32)
        disorder = sb("disorder", [P, 3], F32)
        open_scope()
        res_bias = sb("res_bias", [P, dim], F32)
        src_sb = sb("src_sb", [P, cols], I32)
        dst_sb = sb("dst_sb", [P, cols + 1], I32)
        key_i = sb("key_i", [P, cols], I32)
        dst_lo = sb("dst_lo", [P, HIST * hist_steps], BF16)
        dst_hi = sb("dst_hi", [P, HIST * hist_steps], BF16)
        onehot_lo = sb("onehot_lo", [P, 2, HIST // 2, P, 2], BF16)
        onehot_hi = sb("onehot_hi", [P, 2, HIST // 2, tiles, 2], BF16)

        x_loaded = sem("x_loaded")
        dst_loaded = sem("dst_loaded")
        next_loaded = sem("next_loaded")
        src_loaded = sem("src_loaded")
        pad_stored = sem("pad_stored")
        dst_stored = sem("dst_stored")
        gnn_w_loaded = sem("gnn_w_loaded")
        edges_cleared = sem("edges_cleared")
        feat_cleared = sem("feat_cleared")
        iotas_made = sem("iotas_made")
        pool_link = sem("pool_link")
        prep_link = sem("prep_link")
        act_link = sem("act_link")
        table_room_set = sem("table_room_set")
        onehots_ready = sem("onehots_ready")
        hist_used = sem("hist_used")
        first_w_loaded = sem("first_w_loaded")
        FIRST_W = 16 * 7
        full = (tiles - 1) * P

        with nc.Block() as block:
            @block.sync
            def _(sp):
                sp.wait_ge(edges_cleared, 3)
                for table, tile, s in ((dst, dst_sb, dst_loaded), (src, src_sb, src_loaded)):
                    for a, b in ((0, 112), (112, P - 1)):
                        sp.dma_start(tile[a:b, 0:cols], table[a * cols:b * cols].rearrange("(p c) -> p c", c=cols)).then_inc(s, 16)
                    sp.dma_start(tile[P - 1:P, 0:last_cols], table[(P - 1) * cols:edges].rearrange("(p c) -> p c", p=1)).then_inc(s, 16)
                sp.dma_start(dst_sb[0:P - 1, cols:cols + 1], bass.AP(tensor=dst.tensor, offset=dst.offset + cols, ap=[[cols, P - 1], [1, 1]]), allow_slow_non_contiguous=True).then_inc(next_loaded, 16)
                sp.wait_ge(src_loaded, 16 * 3)
                sp.dma_start(src_pad.rearrange("(p c) -> p c", c=cols), src_sb[:, :]).then_inc(pad_stored, 16)
                sp.wait_ge(dst_loaded, 16 * 3)
                sp.dma_start(dst_pad.rearrange("(p c) -> p c", c=cols), dst_sb[:, 0:cols]).then_inc(dst_stored, 16)
                sp.wait_ge(pad_stored, 16)
                sp.wait_ge(dst_stored, 16)

            @block.gpsimd
            def _(pool):
                link = Link(pool, pool_link)
                nc.gpsimd.iota(iota_lo[:, :, :], [[1, P], [0, 2]], 0, 0, allow_small_or_imprecise_dtypes=True).then_inc(iotas_made, 1)
                nc.gpsimd.iota(iota_hi[:, :, :], [[1, width], [0, 2]], -P, 0, allow_small_or_imprecise_dtypes=True).then_inc(iotas_made, 1)
                nc.gpsimd.iota(iota_slot[:, :], [[1, slots]], 0, 0, allow_small_or_imprecise_dtypes=True).then_inc(iotas_made, 1)
                link(nc.gpsimd.memset(ident[:, :], 0.0))
                link(nc.gpsimd.affine_select(out=ident[:, :], in_=ident[:, :], compare_op=ALU.not_equal, fill=1.0,
                                             base=0, pattern=[[-1, P]], channel_multiplier=1))
                link(nc.gpsimd.tensor_copy(ident_bf[:, :], ident[:, :]))
                link(nc.gpsimd.memset(upper[:, :], 1.0))
                link(nc.gpsimd.affine_select(out=upper[:, :], in_=upper[:, :], compare_op=ALU.is_gt, fill=0.0,
                                             base=0, pattern=[[1, P]], channel_multiplier=-1))
                link(nc.gpsimd.memset(real[:, :], 1.0))
                link(nc.gpsimd.affine_select(out=real[:, :], in_=real[:, :], compare_op=ALU.is_gt, fill=0.0,
                                             base=last_rows, pattern=[[0, 1]], channel_multiplier=-1))
                link(nc.gpsimd.memset(ones[:, :], 1.0))
            @block.scalar
            def _(act):
                act.wait_ge(feat_cleared, 1)
                act.wait_ge(dst_loaded, 16 * 3)
                for t0 in range(0, tiles - 1, 8):
                    act.dma_start(feat[:, t0:t0 + 8, :], x[t0 * P:(t0 + 8) * P, :].rearrange("(t p) d -> p t d", p=P)).then_inc(x_loaded, 16)
                act.dma_start(feat[0:last_rows, tiles - 1, :], x[full:nodes, :]).then_inc(x_loaded, 16)
                for l in range(layers):
                    act.dma_start(both_w[:, l, :, 0:dim], gnn_w[l].rearrange("(k p) d -> p k d", p=P)).then_inc(gnn_w_loaded, 16)
                    act.dma_start(both_w[:, l, :, dim:2 * dim], res_w.rearrange("(k p) d -> p k d", p=P)).then_inc(gnn_w_loaded, 16)
                act.dma_start(bias_sum[:, :, :], gnn_b.partition_broadcast(P)).then_inc(gnn_w_loaded, 16)
                act.dma_start(res_bias[:, :], res_b.partition_broadcast(P)).then_inc(gnn_w_loaded, 16)
                link = Link(act, act_link)

                def row(t):
                    return feat[:, bass.ds(t, 1), :].rearrange("p a d -> p (a d)")

                def unused(t, i):
                    return parts[:, bass.ds(t, 1), i * dim:(i + 1) * dim].rearrange("p a d -> p (a d)")

                act.wait_ge(table_room_set, 1)
                link(nc.scalar.activation(row_mean[:, 0:1], table_room[:, 0:1], ACT.Copy))
                act.wait_ge(x_loaded, 16 * ((tiles - 1) // 8 + 1))
                with act.Fori(0, tiles) as t:
                    nc.scalar.activation(unused(t, 0), row(t), ACT.Copy, accum_out=row_sum[:, bass.ds(t, 1)]).then_inc(act_link, 1)
                link.count += tiles
                act.wait_ge(act_link, link.count)
                link(nc.scalar.activation(row_mean[:, :], row_sum[:, :], ACT.Copy, scale=-1.0 / dim))
                with act.Fori(0, tiles) as t:
                    nc.scalar.activation(row(t), row(t), ACT.Identity, bias=row_mean[:, bass.ds(t, 1)]).then_inc(act_link, 1)
                link.count += tiles
                act.wait_ge(act_link, link.count)
                with act.Fori(0, tiles) as t:
                    nc.scalar.activation(unused(t, 1), row(t), ACT.Square, accum_out=row_squares[:, bass.ds(t, 1)]).then_inc(act_link, 1)
                link.count += tiles
                act.wait_ge(act_link, link.count)

            @block.tensor
            def _(pe):
                def count(b, first, last):
                    for u in range(HIST):
                        mm = nc.tensor.matmul(bank[0][:, 0:tiles], onehot_lo[:, b, u // 2, :, u % 2], onehot_hi[:, b, u // 2, :, u % 2],
                                              start=first and u == 0, stop=last and u == HIST - 1)
                    mm.then_inc(hist_used, 1)

                for i in range(2):
                    pe.wait_ge(onehots_ready, i + 1)
                    count(i, i == 0, False)
                with pe.Fori(1, hist_steps // 2 - 1) as i:
                    for b in range(2):
                        pe.wait_ge(onehots_ready, 2 * i + b + 1)
                        count(b, False, False)
                for b in range(2):
                    pe.wait_ge(onehots_ready, hist_steps - 1 + b)
                    count(b, False, b == 1)

            @block.vector
            def _(dve):
                link = Link(dve, prep_link)
                pad = padded - 1
                last_quarter = slice(P - 32, P)
                nc.vector.memset(src_sb[last_quarter, :], pad).then_inc(edges_cleared, 1)
                nc.vector.memset(dst_sb[last_quarter, :], pad).then_inc(edges_cleared, 2)
                nc.vector.memset(feat[:, tiles - 1, :], 0.0).then_inc(feat_cleared, 1)
                nc.vector.memset(table_room[:, :], 0.0).then_inc(table_room_set, 1)
                link(nc.vector.memset(eps_col[:, :], EPS))
                nc.vector.memset(dst_hi[:, cols:], -1.0)
                link(nc.vector.memset(dst_lo[:, cols:], -1.0))
                dve.wait_ge(dst_loaded, 16 * 3)
                link(nc.vector.tensor_scalar(key_i[:, :], dst_sb[:, 0:cols], 7, None, ALU.logical_shift_right))
                link(nc.vector.tensor_copy(dst_hi[:, 0:cols], key_i[:, :]))
                link(nc.vector.tensor_scalar(key_i[:, :], dst_sb[:, 0:cols], P - 1, None, ALU.bitwise_and))
                link(nc.vector.tensor_copy(dst_lo[:, 0:cols], key_i[:, :]))
                dve.wait_ge(iotas_made, 3)

                def onehots(c, b):
                    onehot_rows(onehot_lo[:, b, :, :, :], dst_lo[:, bass.ds(c, HIST)], iota_lo, HIST, P)
                    onehot_rows(onehot_hi[:, b, :, :, :], dst_hi[:, bass.ds(c, HIST)], iota_lo, HIST, tiles).then_inc(onehots_ready, 1)

                for b in range(2):
                    onehots(b * HIST, b)
                with dve.Fori(1, hist_steps // 2) as i:
                    for b in range(2):
                        dve.wait_ge(hist_used, 2 * i - 1 + b)
                        onehots(i * (2 * HIST) + b * HIST, b)

                link(nc.vector.memset(disorder[:, :], 0.0))
                dve.wait_ge(next_loaded, 16)
                link(nc.vector.tensor_tensor(key_i[:, 0:cols - 1], dst_sb[:, 1:cols], dst_sb[:, 0:cols - 1], ALU.is_lt))
                link(nc.vector.tensor_reduce(disorder[:, 0:1], key_i[:, 0:cols - 1], AX, ALU.add))
                link(nc.vector.tensor_tensor(disorder[0:P - 1, 1:2], dst_sb[0:P - 1, cols:cols + 1], dst_sb[0:P - 1, cols - 1:cols], ALU.is_lt))
                dve.wait_ge(gnn_w_loaded, 16 * (2 * layers + 2))
                for l in range(layers):
                    link(nc.vector.tensor_tensor(bias_sum[:, l, :], bias_sum[:, l, :], res_bias[:, :], ALU.add))
        close_scope()

        total = sb("total", [P, 2 * pairs], F32)
        zeros = sb("zeros", [P, 2 * pairs], F32)
        start = sb("start", [P, 2 * pairs], F32)
        start_i = sb("start_i", [P, 2 * pairs], I32)
        over = sb("over", [P, 2 * pairs], F32)
        sources = sb("sources", [P, 2 * pairs, slots], I32)
        BATCH = 10
        batches = 2 * pairs // BATCH
        KEY_STEPS = 6
        FIRST_KEYS = 9
        src_hi = sb("src_hi", [P, BATCH, slots], I32)
        src_lo = sb("src_lo", [P, BATCH, slots], I32)
        inside = sb("inside", [P, BATCH, slots], F32)
        node_keys = sb("node_keys", [P, 2, 2, BATCH, slots], F32)
        scaled = sb("scaled", [P, 4, dim], F32)
        rest = sb("rest", [P, 2, dim], F32)
        res_tile = sb("res_tile", [P, 2, dim], F32)
        turned = sb("turned", [P, 2, K2 * P], F32)
        message_scale = sb("message_scale", [P, tiles], F32)
        deg_ready = sem("deg_ready")
        offsets_ready = sem("offsets_ready")
        csr_link = sem("csr_link")
        roots_ready = sem("roots_ready")
        inverses_ready = sem("inverses_ready")
        starts_ready = sem("starts_ready")
        fetched = [sem(f"fetched{n}") for n in range(batches)]
        keys_ready = sem("keys_ready")
        keys_turned = sem("keys_turned")
        keys_out = sem("keys_out")
        flag_summed = sem("flag_summed")
        flag_read = sem("flag_read")
        turned_ready = sem("turned_ready")
        turned_out = sem("turned_out")
        products_ready = sem("products_ready")
        res_ready = sem("res_ready")
        messages_ready = sem("messages_ready")
        high_ready = sem("high_ready")
        rest_ready = sem("rest_ready")
        middle_ready = sem("middle_ready")
        low_ready = sem("low_ready")
        res_stored = [sem(f"first_res_stored{b}") for b in range(2)]
        assert 2 * pairs % BATCH == 0 and BATCH % 2 == 0 and FIRST_KEYS + batches * KEY_STEPS + KEY_STEPS <= tiles

        def keys_due(t):
            n, k = divmod(t - FIRST_KEYS - KEY_STEPS, KEY_STEPS)
            return n * (BATCH // 2) + k if 0 <= n < batches and k < BATCH // 2 else None

        with nc.Block() as block:
            @block.tensor
            def _(pe):
                pe.wait_ge(deg_ready, 1)
                nc.tensor.matmul(bank[4][:, 0:2 * pairs], upper[:, :], deg[:, :], start=True, stop=True).then_inc(offsets_ready, 1)
                nc.tensor.matmul(bank[5][:, 0:2 * pairs], ones[:, :], deg[:, :], start=True, stop=True).then_inc(offsets_ready, 1)

                def turn(t):
                    if t >= 2:
                        pe.wait_ge(turned_out, t - 1)
                    for k in range(K2):
                        tr = nc.tensor.transpose(bank[2 + t % 2][:, k * P:(k + 1) * P], feat[:, t, k * P:(k + 1) * P], ident[:, :])
                    tr.then_inc(turned_ready, 1)

                def products(t):
                    pe.wait_ge(turned_out, t + 1)
                    if t >= 2:
                        pe.wait_ge(messages_ready, t - 1)
                        pe.wait_ge(res_ready, t - 1)
                    for k in range(K2):
                        mm = nc.tensor.matmul(bank[t % 2][:, :], turned[:, t % 2, k * P:(k + 1) * P], both_w[:, 0, k, :], start=k == 0, stop=k == K2 - 1)
                    mm.then_inc(products_ready, 1)

                def turn_keys(i):
                    n, j = divmod(2 * i, BATCH)
                    b = bank[4 + i % 4]
                    pe.wait_ge(keys_ready, n + 1)
                    if i >= 4:
                        pe.wait_ge(keys_out, i - 3)
                    for k in range(2):
                        tr = nc.tensor.transpose(b[:, k * P:(k + 1) * P], node_keys[:, n % 2, k, j:j + 2, :].rearrange("p t s -> p (t s)"), ident[:, :])
                    tr.then_inc(keys_turned, 1)

                turn(0)
                turn(1)
                for t in range(tiles):
                    products(t)
                    if t == 1:
                        pe.wait_ge(starts_ready, 2)
                        nc.tensor.matmul(bank[6][:, 0:3], ones[:, :], disorder[:, :], start=True, stop=True).then_inc(flag_summed, 1)
                    if t == 2:
                        pe.wait_ge(flag_read, 1)
                    if t + 2 < tiles:
                        turn(t + 2)
                    if keys_due(t) is not None:
                        turn_keys(keys_due(t))

            @block.gpsimd
            def _(pool):
                pool.wait_ge(starts_ready, 1)
                edge_list = src_pad.rearrange("(a n) -> a n", a=1)
                for t in range(tiles):
                    pool.indirect_dma_start(sources[:, t, :], None, edge_list, bass.IndirectOffsetOnAxis(ap=start_i[:, t:t + 1], axis=1)).then_inc(fetched[t // BATCH], 16)

            @block.scalar
            def _(act):
                act.wait_ge(inverses_ready, 1)
                nc.scalar.activation(dis[:, :], deg[:, 0:tiles], ACT.Sqrt, bias=1.0).then_inc(roots_ready, 1)
                nc.scalar.activation(rstd[:, :], row_squares[:, :], ACT.Sqrt, bias=eps_col[:, 0:1], scale=1.0 / dim).then_inc(roots_ready, 1)

                def turn_out(i):
                    act.wait_ge(keys_turned, i + 1)
                    nc.scalar.activation(keys_t[:, i, :, :].rearrange("p k n -> p (k n)"), bank[4 + i % 4][:, 0:2 * P], ACT.Copy).then_inc(keys_out, 1)

                def turned_copy(t):
                    act.wait_ge(turned_ready, t + 1)
                    if t >= 2:
                        act.wait_ge(products_ready, t - 1)
                    nc.scalar.activation(turned[:, t % 2, :], bank[2 + t % 2][:, 0:K2 * P], ACT.Copy).then_inc(turned_out, 1)

                turned_copy(0)
                act.wait_ge(inverses_ready, 4)
                for t in range(tiles):
                    if t + 1 < tiles:
                        turned_copy(t + 1)
                    act.wait_ge(products_ready, t + 1)
                    if t >= 4:
                        act.wait_ge(low_ready, t - 3)
                    nc.scalar.activation(scaled[:, t % 4, :], bank[t % 2][:, 0:dim], ACT.Copy, scale=message_scale[:, t:t + 1]).then_inc(messages_ready, 1)
                    if t >= 1:
                        act.wait_ge(rest_ready, t)
                        nc.scalar.activation(parts[:, t - 1, dim:2 * dim], rest[:, (t - 1) % 2, :], ACT.Copy).then_inc(middle_ready, 1)
                    act.wait_ge(messages_ready, t + 1)
                    nc.scalar.activation(parts[:, t, 0:dim], scaled[:, t % 4, :], ACT.Copy).then_inc(high_ready, 1)
                    if keys_due(t - 1) is not None:
                        turn_out(keys_due(t - 1))
                t = tiles
                act.wait_ge(rest_ready, t)
                nc.scalar.activation(parts[:, t - 1, dim:2 * dim], rest[:, (t - 1) % 2, :], ACT.Copy).then_inc(middle_ready, 1)

            @block.sync
            def _(sp):
                for t in range(tiles):
                    sp.wait_ge(res_ready, t + 1)
                    sp.dma_start(res_table[0][t * P:(t + 1) * P, :], res_tile[:, t % 2, :]).then_inc(res_stored[t % 2], 16)
                sp.dma_start(w1_sb[:, :, :, :].rearrange("p e k d -> p (e k) d"), expert_w1.rearrange("e (k p) d -> p (e k) d", p=P)).then_inc(first_w_loaded, 16)
                sp.dma_start(router_w1_sb[:, :, :], router_w1.rearrange("(k p) d -> p k d", p=P)).then_inc(first_w_loaded, 16)
                sp.dma_start(router_w2_sb[:, :], router_w2).then_inc(first_w_loaded, 16)
                sp.dma_start(router_b1_sb[:, :], router_b1.rearrange("(p a) -> p a", a=1)).then_inc(first_w_loaded, 16)
                sp.dma_start(router_b2_sb[:, :], router_b2.partition_broadcast(P)).then_inc(first_w_loaded, 16)
                for tile, b in ((b1_sb, expert_b1), (b2_sb, expert_b2)):
                    sp.dma_start(tile[:, :, :].rearrange("p e k -> p (e k)"), b.rearrange("e (k p) -> p (e k)", p=P), allow_slow_non_contiguous=True).then_inc(first_w_loaded, 16)
                for b in range(2):
                    sp.wait_ge(res_stored[b], 16 * len(range(b, tiles, 2)))

            @block.vector
            def _(dve):
                link = Link(dve, csr_link)
                nc.vector.memset(sources[:, tiles, :], 0)
                nc.vector.memset(zeros[:, :], 0.0)
                link(nc.vector.memset(deg[:, tiles:], 0.0))
                link(nc.vector.tensor_copy(deg[:, 0:tiles], bank[0][:, 0:tiles]))
                nc.vector.tensor_tensor(deg[:, tiles - 1:tiles], deg[:, tiles - 1:tiles], real[:, :], ALU.mult).then_inc(deg_ready, 1)
                dve.wait_ge(deg_ready, 1)
                dve.sem_inc(inverses_ready, 1)
                dve.wait_ge(offsets_ready, 2)
                link(nc.vector.tensor_copy(total[:, :], bank[5][:, 0:2 * pairs]))
                link(nc.vector.tensor_tensor_scan(start[:, :], total[:, :], zeros[:, :], 0.0, ALU.add, ALU.add))
                link(nc.vector.tensor_tensor(start[:, :], start[:, :], total[:, :], ALU.subtract))
                link(nc.vector.tensor_tensor(start[:, :], start[:, :], bank[4][:, 0:2 * pairs], ALU.add))
                nc.vector.tensor_copy(start_i[:, :], start[:, :]).then_inc(starts_ready, 1)
                link(nc.vector.tensor_scalar(over[:, :], deg[:, :], float(slots), None, ALU.is_gt))
                nc.vector.tensor_reduce(disorder[:, 2:3], over[:, :], AX, ALU.add).then_inc(starts_ready, 1)
                dve.wait_ge(roots_ready, 2)
                nc.vector.reciprocal(dis[:, :], dis[:, :]).then_inc(inverses_ready, 1)
                nc.vector.reciprocal(rstd[:, :], rstd[:, :]).then_inc(inverses_ready, 1)
                dve.wait_ge(inverses_ready, 3)
                nc.vector.tensor_tensor(message_scale[:, :], dis[:, :], rstd[:, :], ALU.mult).then_inc(inverses_ready, 1)
                dve.wait_ge(flag_summed, 1)
                nc.vector.tensor_reduce(over[:, 0:1], bank[6][:, 0:3], AX, ALU.add).then_inc(flag_read, 1)
                dve.wait_ge(flag_read, 1)
                link(nc.vector.tensor_scalar(over[:, 0:1], over[:, 0:1], 1.0, None, ALU.min))
                link(nc.vector.tensor_copy(flag[:, :], over[:, 0:1]))
                dve.wait_ge(iotas_made, 3)

                def residual(t):
                    dve.wait_ge(messages_ready, t + 1)
                    if t >= 2:
                        dve.wait_ge(res_stored[t % 2], 16 * (t // 2))
                    nc.vector.scalar_tensor_tensor(res_tile[:, t % 2, :], bank[t % 2][:, dim:2 * dim], rstd[:, t:t + 1], bias_sum[:, 0, :],
                                                   ALU.mult, ALU.add).then_inc(res_ready, 1)

                def rest_of(t):
                    dve.wait_ge(high_ready, t + 1)
                    if t >= 2:
                        dve.wait_ge(low_ready, t - 1)
                    nc.vector.tensor_tensor(rest[:, t % 2, :], scaled[:, t % 4, :], parts[:, t, 0:dim], ALU.subtract).then_inc(rest_ready, 1)

                def low_part(t):
                    dve.wait_ge(middle_ready, t + 1)
                    nc.vector.tensor_tensor(parts[:, t, 2 * dim:3 * dim], rest[:, t % 2, :], parts[:, t, dim:2 * dim], ALU.subtract).then_inc(low_ready, 1)

                def key_step(n, step):
                    ts = slice(n * BATCH, (n + 1) * BATCH)

                    def each_slot(v):
                        return v[:, ts].unsqueeze(2).to_broadcast([P, BATCH, slots])

                    if step == 0:
                        dve.wait_ge(fetched[n], 16 * (min((n + 1) * BATCH, tiles) - n * BATCH))
                        if n >= 1:
                            dve.wait_ge(keys_ready, n)
                        nc.vector.tensor_scalar(src_hi[:, :, :], sources[:, ts, :], 7, None, ALU.logical_shift_right)
                    if step == 1:
                        nc.vector.tensor_scalar(src_lo[:, :, :], sources[:, ts, :], P - 1, None, ALU.bitwise_and)
                    if step == 2:
                        link(nc.vector.tensor_tensor(inside[:, :, :], iota_slot[:, :].unsqueeze(1).to_broadcast([P, BATCH, slots]), each_slot(deg), ALU.is_lt))
                    if step == 3:
                        if n >= 2:
                            dve.wait_ge(keys_turned, (n - 1) * BATCH // 2)
                        link(nc.vector.scalar_tensor_tensor(node_keys[:, n % 2, 0, :, :], inside[:, :, :], -float(P), src_hi[:, :, :], ALU.mult, ALU.add))
                    if step == 4:
                        odd = node_keys[:, n % 2, 0, :, :].rearrange("p (t o) s -> p t o s", o=2)[:, :, 1, :]
                        link(nc.vector.tensor_scalar(odd, odd, float(tiles), None, ALU.add))
                    if step == 5:
                        nc.vector.tensor_copy(node_keys[:, n % 2, 1, :, :], src_lo[:, :, :]).then_inc(keys_ready, 1)

                for t in range(tiles):
                    residual(t)
                    if t >= 1:
                        low_part(t - 1)
                    rest_of(t)
                    if FIRST_KEYS <= t < FIRST_KEYS + batches * KEY_STEPS:
                        key_step(*divmod(t - FIRST_KEYS, KEY_STEPS))
                low_part(tiles - 1)
        close_scope()

        def gather_sum(l):
            index_ready = sem(f"index_ready{l}")
            rows_t_ready = sem(f"rows_t_ready{l}")
            same_ready = sem(f"same_ready{l}")
            count_ready = sem(f"count_ready{l}")
            target_ready = sem(f"target_ready{l}")
            hs_gathered = sem(f"hs_gathered{l}")
            agg_gathered = sem(f"agg_gathered{l}")
            summed = sem(f"summed{l}")
            added = sem(f"added{l}")
            scattered = sem(f"scattered{l}")
            passed = sem(f"passed{l}")
            edges_back = sem(f"edges_back{l}")
            open_scope()
            src_sb = sb(f"gs_src{l}", [P, cols], I32)
            dst_sb = sb(f"gs_dst_all{l}", [P, cols], I32)
            lower = sb(f"gs_lower{l}", [P, P], F32)
            index = sb(f"gs_index{l}", [P, 3], I32)
            gs_dst = sb(f"gs_dst{l}", [P, 1], F32)
            gs_count = sb(f"gs_count{l}", [P, 1], F32)
            gs_same = sb(f"gs_same{l}", [P, P], F32)
            gs_before = sb(f"gs_before{l}", [P, P], F32)
            gs_hs = sb(f"gs_hs{l}", [P, dim], F32)
            gs_agg = sb(f"gs_agg{l}", [P, dim], F32)
            lower_set = sem(f"lower_set{l}")
            with nc.Block() as block:
                @block.gpsimd
                def _(pool):
                    pool.dma_start(agg_table[l], hs_table[l]).then_inc(scattered, 16)
                    nc.gpsimd.memset(lower[:, :], 1.0).then_inc(lower_set, 1)
                    pool.wait_ge(lower_set, 1)
                    nc.gpsimd.affine_select(out=lower[:, :], in_=lower[:, :], compare_op=ALU.is_gt, fill=0.0,
                                            base=0, pattern=[[-1, P]], channel_multiplier=1).then_inc(lower_set, 1)
                    with pool.Fori(0, cols) as c:
                        pool.wait_ge(index_ready, 3 * c + 3)
                        pool.wait_ge(scattered, 16 * c + 16)
                        pool.sem_inc(passed, 1)
                        pool.indirect_dma_start(gs_hs[:, :], None, hs_table[l], bass.IndirectOffsetOnAxis(ap=index[:, 0:1], axis=0)).then_inc(hs_gathered, 16)
                        pool.indirect_dma_start(gs_agg[:, :], None, agg_table[l], bass.IndirectOffsetOnAxis(ap=index[:, 1:2], axis=0)).then_inc(agg_gathered, 16)
                        pool.wait_ge(target_ready, c + 1)
                        pool.wait_ge(added, c + 1)
                        pool.sem_inc(passed, 1)
                        pool.indirect_dma_start(agg_table[l], bass.IndirectOffsetOnAxis(ap=index[:, 2:3], axis=0), gs_agg[:, :], None,
                                                bounds_check=padded - 1, oob_is_err=False).then_inc(scattered, 16)
                    pool.wait_ge(scattered, 16 * (cols + 1))

                @block.tensor
                def _(pe):
                    with pe.Fori(0, cols) as c:
                        pe.wait_ge(index_ready, 3 * c + 3)
                        nc.tensor.transpose(bank[0][:, 0:P], gs_dst[:, 0:1].to_broadcast([P, P]), ident[:, :]).then_inc(rows_t_ready, 1)
                        pe.wait_ge(same_ready, c + 1)
                        pe.wait_ge(hs_gathered, 16 * c + 16)
                        nc.tensor.matmul(bank[1][:, 0:dim], gs_same[:, :], gs_hs[:, :], start=True, stop=True).then_inc(summed, 1)

                @block.sync
                def _(sp):
                    sp.dma_start(src_sb[:, :], src_pad.rearrange("(p c) -> p c", c=cols)).then_inc(edges_back, 16)
                    sp.dma_start(dst_sb[:, :], dst_pad.rearrange("(p c) -> p c", c=cols)).then_inc(edges_back, 16)

                @block.vector
                def _(dve):
                    dve.wait_ge(edges_back, 32)
                    dve.wait_ge(lower_set, 2)
                    with dve.Fori(0, cols) as c:
                        dve.wait_ge(scattered, 16 * c + 16)
                        nc.vector.tensor_copy(index[:, 0:1], src_sb[:, bass.ds(c, 1)]).then_inc(index_ready, 1)
                        nc.vector.tensor_copy(index[:, 1:2], dst_sb[:, bass.ds(c, 1)]).then_inc(index_ready, 1)
                        nc.vector.tensor_copy(gs_dst[:, :], dst_sb[:, bass.ds(c, 1)]).then_inc(index_ready, 1)
                        dve.wait_ge(rows_t_ready, c + 1)
                        nc.vector.tensor_scalar(gs_same[:, :], bank[0][:, 0:P], gs_dst[:, 0:1], None, ALU.is_equal).then_inc(same_ready, 1)
                        dve.wait_ge(same_ready, c + 1)
                        nc.vector.tensor_tensor(gs_before[:, :], gs_same[:, :], lower[:, :], ALU.mult).then_inc(count_ready, 1)
                        dve.wait_ge(count_ready, 3 * c + 1)
                        nc.vector.tensor_reduce(gs_count[:, :], gs_before[:, :], AX, ALU.add).then_inc(count_ready, 1)
                        dve.wait_ge(count_ready, 3 * c + 2)
                        nc.vector.scalar_tensor_tensor(gs_count[:, :], gs_count[:, :], float(FAR), gs_dst[:, :], ALU.mult, ALU.add).then_inc(count_ready, 1)
                        dve.wait_ge(count_ready, 3 * c + 3)
                        nc.vector.tensor_copy(index[:, 2:3], gs_count[:, :]).then_inc(target_ready, 1)
                        dve.wait_ge(summed, c + 1)
                        dve.wait_ge(agg_gathered, 16 * c + 16)
                        nc.vector.tensor_tensor(gs_agg[:, :], gs_agg[:, :], bank[1][:, 0:dim], ALU.add).then_inc(added, 1)

            close_scope()

        QUAD = 4
        quads = P // QUAD
        UNITS = 2 * (tiles + 1)
        LAST_UNITS = tiles + 1
        half_bank = 2

        def sum_units(pe, counts, b, i, lo, hi, sums_out, sums_ready, first, chunk_back=None, chunk_free=None):
            for n in range(lo, hi):
                o, s = divmod(n, tiles + 1)
                acc = bank[half_bank + o]
                if s == 0 and not first:
                    pe.wait_ge(sums_out, 2 * i + o - 1)
                if chunk_back is not None and o == 0 and s < tiles and s % CHUNK == 0:
                    pe.wait_ge(chunk_back[s // CHUNK], 32)
                if s < tiles:
                    lhs, rhs = counts[:, b, s, o * P:(o + 1) * P], parts[:, s, :]
                else:
                    lhs, rhs = ident_bf[:, :], parts[:, bass.ds(i * 2 + o, 1), :].rearrange("p a d -> p (a d)")
                nc.tensor.matmul(acc[:, 0:2 * dim], lhs, rhs[:, 0:2 * dim], start=s == 0, stop=False)
                mm = nc.tensor.matmul(acc[:, 0:dim], lhs, rhs[:, 2 * dim:3 * dim], start=False, stop=s == tiles)
                if s == tiles:
                    mm.then_inc(sums_ready, 1)
                elif chunk_free is not None and s % CHUNK == CHUNK - 1 and s < EARLY_CHUNKS * CHUNK:
                    mm.then_inc(chunk_free, 1)

        CHUNK = 7
        EARLY_CHUNKS = 4
        assert tiles % CHUNK == 0 and EARLY_CHUNKS * CHUNK <= tiles - 4
        chunk_free = sem("chunk_free")
        chunk_back = [sem(f"chunk_back{c}") for c in range(tiles // CHUNK)]

        def sums_middle(act, i, o, sums_ready, middle_out, middle, sums_out, first):
            act.wait_ge(sums_ready, 2 * i + o + 1)
            if not first:
                act.wait_ge(sums_out, 2 * i + o - 1)
            nc.scalar.activation(middle[:, o, :], bank[half_bank + o][:, dim:2 * dim], ACT.Copy).then_inc(middle_out, 1)

        def sums_high(dve, i, o, middle_out, middle, sums, sums_out, sum_ready, first):
            dve.wait_ge(middle_out, 2 * i + o + 1)
            if not first:
                dve.wait_ge(sum_ready, 2 * i + o - 1)
            nc.vector.tensor_tensor(sums[:, o, :], middle[:, o, :], bank[half_bank + o][:, 0:dim], ALU.add).then_inc(sums_out, 1)

        def count_and_sum(update):
            keys_copied = sem("keys_copied")
            onehots_made = sem("onehots_made")
            quad_ready = sem("quad_ready")
            quad_out = sem("quad_out")
            counts_stored = [sem(f"counts_stored{b}") for b in range(2)]
            STEP = 16
            steps = P // STEP
            per_step = STEP // QUAD
            open_scope()
            counts = sb("counts", [P, 2, tiles, 2 * P], BF16)
            keys = sb("pair_keys", [P, 2, 2, P], BF16)
            rows_lo = sb("rows_lo", [P, 2, STEP // 2, P, 2], BF16)
            rows_hi = sb("rows_hi", [P, 2, STEP // 2, width, 2], BF16)

            def there(T):
                return not isinstance(T, int) or T >= 0

            with nc.Block() as block:
                @block.tensor
                def _(pe):
                    def build(q, i, first):
                        r, u0 = divmod(q * QUAD, STEP)
                        if u0 == 0:
                            pe.wait_ge(onehots_made, i * steps + (r + 1))
                        if not (first and q < 4):
                            pe.wait_ge(quad_out, i * quads + (q - 3))
                        for u in range(QUAD):
                            at = (u0 + u) // 2
                            mm = nc.tensor.matmul(bank[4 + q % 4][:, u * width:(u + 1) * width], rows_lo[:, r % 2, at, :, u % 2],
                                                  rows_hi[:, r % 2, at, :, u % 2], start=True, stop=True)
                        mm.then_inc(quad_ready, 1)

                    def sum_pair(i, b, first, last=False):
                        pe.wait_ge(quad_out, i * quads + quads)
                        units = LAST_UNITS if last else UNITS
                        for q in range(quads):
                            if not last:
                                build(q, i + 1, False)
                            sum_units(pe, counts, b, i, q * units // quads, (q + 1) * units // quads, update.sums_out, update.sums_ready, first,
                                      chunk_free=chunk_free if last else None)
                            if q == 4 and there(i * 2 - 1):
                                update.turn(pe, i * 2 - 1, 1)
                            if q == 6 and there(i * 2 - 1):
                                update.products(pe, i * 2 - 1, 1)
                            if q == 20 and not last:
                                update.turn(pe, i * 2, 0)
                            if q == 22 and not last:
                                update.products(pe, i * 2, 0)

                    for q in range(quads):
                        build(q, 0, True)
                    sum_pair(0, 0, True)
                    sum_pair(1, 1, False)
                    with pe.Fori(1, pairs // 2) as j:
                        sum_pair(j * 2, 0, False)
                        sum_pair(j * 2 + 1, 1, False)
                    sum_pair(pairs - 1, 0, False, last=True)
                    update.turn(pe, tiles - 1, 0)
                    update.products(pe, tiles - 1, 0)

                @block.vector
                def _(dve):
                    def rows_of_step(r, i, b, first):
                        if not (first and r < 2):
                            dve.wait_ge(quad_ready, i * quads + (r - 1) * per_step)
                        nodes_of = slice(r * STEP, (r + 1) * STEP)
                        onehot_rows(rows_lo[:, r % 2, :, :, :], keys[:, b, 1, nodes_of], iota_lo, STEP, P)
                        onehot_rows(rows_hi[:, r % 2, :, :, :], keys[:, b, 0, nodes_of], iota_hi, STEP, width).then_inc(onehots_made, 1)

                    def sums(i, o):
                        sums_high(dve, i, o, update.middle_out, update.middle, update.sums, update.sums_out, update.sum_ready, isinstance(i, int) and i == 0)
                        update.add_res(dve, i * 2 + o, o, i)

                    def pair(i, b):
                        nc.vector.tensor_copy(keys[:, b, :, :].rearrange("p k n -> p (k n)"),
                                              keys_t[:, bass.ds(i, 1), :, :].rearrange("p a k n -> p (a k n)")).then_inc(keys_copied, 1)
                        dve.wait_ge(keys_copied, i + 1)
                        for r in range(steps):
                            rows_of_step(r, i, b, isinstance(i, int) and i == 0)
                            if there(i * 2 - 4):
                                if r == 0:
                                    update.rest_of(dve, i * 2 - 4, 0)
                                if r == 1:
                                    update.low_part(dve, i * 2 - 4, 0)
                            if there(i * 2 - 3):
                                if r == 1:
                                    sums(i - 2, 1)
                                if r == 3:
                                    update.res_and_message(dve, i * 2 - 3, 1, i - 2)
                                if r == 4:
                                    update.rest_of(dve, i * 2 - 3, 1)
                                if r == 5:
                                    update.low_part(dve, i * 2 - 3, 1)
                            if there(i * 2 - 2):
                                if r == 5:
                                    sums(i - 1, 0)
                                if r == 7:
                                    update.res_and_message(dve, i * 2 - 2, 0, i - 1)

                    for i in range(4):
                        pair(i, i % 2)
                    with dve.Fori(2, pairs // 2) as j:
                        pair(j * 2, 0)
                        pair(j * 2 + 1, 1)
                    pair(pairs - 1, 0)
                    update.rest_of(dve, tiles - 3, 0)
                    update.low_part(dve, tiles - 3, 0)
                    for T in (tiles - 2, tiles - 1):
                        sums(T // 2, T % 2)
                        update.res_and_message(dve, T, T % 2, T // 2)
                        update.rest_of(dve, T, T % 2)
                        update.low_part(dve, T, T % 2)

                @block.scalar
                def _(act):
                    def quad(q, i, b):
                        act.wait_ge(quad_ready, i * quads + (q + 1))
                        nc.scalar.activation(
                            counts[:, b, :, :].rearrange("p s (o n) -> p n o s", o=2)[:, q * QUAD:(q + 1) * QUAD, :, :],
                            bank[4 + q % 4][:, 0:QUAD * width].rearrange("p (n o s) -> p n o s", o=2, s=tiles), ACT.Copy).then_inc(quad_out, 1)

                    def middle_sums(i, o):
                        sums_middle(act, i, o, update.sums_ready, update.middle_out, update.middle, update.sums_out, isinstance(i, int) and i == 0)

                    def pair(i, j, b):
                        if not isinstance(i, int) or i >= 2:
                            act.wait_ge(counts_stored[b], j * 16)
                            act.wait_ge(update.sums_ready, 2 * i - 2)
                        for q in range(quads):
                            quad(q, i, b)
                            if q == 0 and there(i * 2 - 4):
                                update.middle_part(act, i * 2 - 4, 0)
                            if there(i * 2 - 3):
                                if q == 0:
                                    middle_sums(i - 2, 1)
                                if q == 3:
                                    update.relu(act, i * 2 - 3, 1)
                                if q == 5:
                                    update.turned_copy(act, i * 2 - 3, 1)
                                if q == 12:
                                    update.high_part(act, i * 2 - 3, 1, i - 2)
                                if q == 15:
                                    update.middle_part(act, i * 2 - 3, 1)
                            if there(i * 2 - 2):
                                if q == 16:
                                    middle_sums(i - 1, 0)
                                if q == 18:
                                    update.relu(act, i * 2 - 2, 0)
                                if q == 21:
                                    update.turned_copy(act, i * 2 - 2, 0)
                                if q == 28:
                                    update.high_part(act, i * 2 - 2, 0, i - 1)

                    for i in range(4):
                        pair(i, i // 2, i % 2)
                    with act.Fori(2, pairs // 2) as j:
                        pair(j * 2, j, 0)
                        pair(j * 2 + 1, j, 1)
                    pair(pairs - 1, pairs // 2, 0)
                    update.middle_part(act, tiles - 3, 0)
                    for T in (tiles - 2, tiles - 1):
                        middle_sums(T // 2, T % 2)
                        update.relu(act, T, T % 2)
                        update.turned_copy(act, T, T % 2)
                        update.high_part(act, T, T % 2, T // 2)
                        update.middle_part(act, T, T % 2)

                @block.sync
                def _(sp):
                    def store_counts(i, b):
                        sp.wait_ge(quad_out, i * quads + quads)
                        sp.dma_start(counts_table[bass.ds(i, 1), :, :].rearrange("a p n -> p (a n)"),
                                     counts[:, b, :, :].rearrange("p s n -> p (s n)")).then_inc(counts_stored[b], 16)

                    def pair(i, b):
                        update.load(sp, i * 2 + 1, 1, i)
                        if there(i * 2 - 2):
                            update.store_next(sp, i * 2 - 2, 0)
                            update.store_next(sp, i * 2 - 1, 1)
                        update.load(sp, i * 2 + 2, 0, i + 1)
                        store_counts(i + 1, 1 - b)

                    update.load(sp, 0, 0, 0)
                    store_counts(0, 0)
                    pair(0, 0)
                    pair(1, 1)
                    with sp.Fori(1, pairs // 2) as j:
                        pair(j * 2, 0)
                        pair(j * 2 + 1, 1)
                    update.store_next(sp, tiles - 3, 0)
                    for c in range(EARLY_CHUNKS):
                        at = slice(c * CHUNK, (c + 1) * CHUNK)
                        for o in range(2):
                            sp.wait_ge(update.parts_stored[o], 16 * len(range(o, at.stop, 2)))
                        sp.wait_ge(chunk_free, c + 1)
                        sp.dma_start(parts[:, at, :], parts_table[:, at, :]).then_inc(chunk_back[c], 16)
                        if c == 2:
                            update.store_next(sp, tiles - 2, 1)
                    update.store_next(sp, tiles - 1, 0)
                    for b in range(2):
                        sp.wait_ge(counts_stored[b], 16 * len(range(b, pairs, 2)))

                @block.gpsimd
                def _(pool):
                    update.wait_stored(pool)
            close_scope()

        def sum_by_counts(update, counts):
            counts_back = [sem(f"counts_back{b}") for b in range(2)]

            def by_pairs(eng, body):
                body(0, 0, 0, False)
                body(1, 0, 1, False)
                with eng.Fori(1, pairs // 2) as j:
                    body(j * 2, j, 0, False)
                    body(j * 2 + 1, j, 1, False)
                body(pairs - 1, pairs // 2, 0, True)

            with nc.Block() as block:
                @block.sync
                def _(sp):
                    def pair(i, j, b, last):
                        if isinstance(i, int) and i == 0:
                            for c in range(tiles // CHUNK):
                                at = slice(c * CHUNK, (c + 1) * CHUNK)
                                if c >= EARLY_CHUNKS:
                                    sp.dma_start(parts[:, at, :], parts_table[:, at, :]).then_inc(chunk_back[c], 16)
                                if c == 0:
                                    update.load(sp, 0, 0, 0)
                                    update.load(sp, 1, 1, 0)
                            return
                        if not (isinstance(i, int) and i < 2):
                            sp.wait_ge(update.sums_ready, 2 * i - 2)
                        sp.dma_start(counts[:, b, :, :].rearrange("p s n -> p (s n)"),
                                     counts_table[bass.ds(i, 1), :, :].rearrange("a p n -> p (a n)")).then_inc(counts_back[b], 16)
                        update.load(sp, i * 2, 0, i, last_tile=last)
                        if not last:
                            update.load(sp, i * 2 + 1, 1, i)
                    by_pairs(sp, pair)

                @block.tensor
                def _(pe):
                    def pair(i, j, b, last):
                        first = isinstance(i, int) and i == 0
                        if not first:
                            pe.wait_ge(counts_back[b], j * 16 + 16 * b)
                        sum_units(pe, counts, b, i, 0, LAST_UNITS if last else UNITS, update.sums_out, update.sums_ready, first,
                                  chunk_back if first else None)
                    by_pairs(pe, pair)

                @block.scalar
                def _(act):
                    for c in range(tiles // CHUNK):
                        at = slice(c * CHUNK, (c + 1) * CHUNK)
                        act.dma_start(counts[:, 0, at, :], counts_table[0].rearrange("p (s n) -> p s n", s=tiles)[:, at, :]).then_inc(chunk_back[c], 16)

                    def pair(i, j, b, last):
                        for o in range(1 if last else 2):
                            sums_middle(act, i, o, update.sums_ready, update.middle_out, update.middle, update.sums_out, isinstance(i, int) and i == 0)
                            update.store_x2(act, i * 2 + o, o)
                    by_pairs(act, pair)

                @block.gpsimd
                def _(pool):
                    update.wait_stored(pool)

                @block.vector
                def _(dve):
                    def pair(i, j, b, last):
                        if last:
                            update.clear_x(dve)
                        for o in range(1 if last else 2):
                            sums_high(dve, i, o, update.middle_out, update.middle, update.sums, update.sums_out, update.sum_ready, isinstance(i, int) and i == 0)
                            update.add_res(dve, i * 2 + o, o, i)
                            update.add_x(dve, i * 2 + o, o, i)
                    by_pairs(dve, pair)

        def messages_to_table(l):
            parts_back = sem(f"parts_back{l}")
            rest_added = sem(f"rest_added{l}")
            message_added = sem(f"message_added{l}")
            message_stored = sem(f"message_stored{l}")
            open_scope()
            message_rest = sb(f"message_rest{l}", [P, dim], F32)
            message = sb(f"message{l}", [P, dim], F32)
            with nc.Block() as block:
                @block.sync
                def _(sp):
                    if l > 0:
                        sp.dma_start(parts[:, :, :], parts_table[:, :, :]).then_inc(parts_back, 16)
                    with sp.Fori(0, tiles) as t:
                        sp.wait_ge(message_added, t + 1)
                        sp.dma_start(hs_table[l][bass.ds(t * P, P), :], message[:, :]).then_inc(message_stored, 16)
                    sp.wait_ge(message_stored, 16 * tiles)

                @block.gpsimd
                def _(pool):
                    pool.wait_ge(message_stored, 16 * tiles)

                @block.vector
                def _(dve):
                    def part(t, k):
                        return parts[:, bass.ds(t, 1), k * dim:(k + 1) * dim].rearrange("p a d -> p (a d)")

                    def add(t):
                        nc.vector.tensor_tensor(message_rest[:, :], part(t, 1), part(t, 2), ALU.add).then_inc(rest_added, 1)
                        dve.wait_ge(rest_added, t + 1)
                        nc.vector.tensor_tensor(message[:, :], part(t, 0), message_rest[:, :], ALU.add).then_inc(message_added, 1)

                    if l > 0:
                        dve.wait_ge(parts_back, 16)
                    add(0)
                    with dve.Fori(1, tiles) as t:
                        dve.wait_ge(message_stored, t * 16)
                        add(t)
            close_scope()

        def update_from_table(update):
            l = update.l
            agg_back = [sem(f"agg_back{l}_{o}") for o in range(2)]

            def over_tiles(eng, body):
                body(0, 0, 0, False)
                body(1, 0, 1, False)
                with eng.Fori(1, tiles // 2) as u:
                    body(u * 2, u, 0, False)
                    body(u * 2 + 1, u, 1, False)
                body(tiles - 1, tiles // 2, 0, True)

            with nc.Block() as block:
                @block.sync
                def _(sp):
                    def tile(T, u, o, last):
                        if not (isinstance(T, int) and T < 2):
                            sp.wait_ge(update.sum_ready, T - 1)
                        sp.dma_start(update.sums[:, o, :], agg_table[l][bass.ds(T * P, P), :]).then_inc(agg_back[o], 16)
                        update.load(sp, T, o, u, last_tile=last)
                    over_tiles(sp, tile)

                @block.vector
                def _(dve):
                    def tile(T, u, o, last):
                        if last and update.last:
                            update.clear_x(dve)
                        dve.wait_ge(agg_back[o], u * 16 + 16)
                        dve.sem_inc(update.sums_out, 1)
                        update.add_res(dve, T, o, u)
                        if update.last:
                            update.add_x(dve, T, o, u)
                        else:
                            update.res_and_message(dve, T, o, u)
                            update.rest_of(dve, T, o)
                            update.low_part(dve, T, o)
                    over_tiles(dve, tile)

                @block.scalar
                def _(act):
                    def tile(T, u, o, last):
                        if not update.last:
                            update.relu(act, T, o)
                            update.turned_copy(act, T, o)
                            update.high_part(act, T, o, u)
                            update.middle_part(act, T, o)
                    over_tiles(act, tile)

                @block.tensor
                def _(pe):
                    def tile(T, u, o, last):
                        if not update.last:
                            update.turn(pe, T, o)
                            update.products(pe, T, o)
                    over_tiles(pe, tile)

                @block.gpsimd
                def _(pool):
                    def tile(T, u, o, last):
                        if update.last:
                            update.store_x2(pool, T, o)
                        else:
                            update.store_next(pool, T, o)
                    over_tiles(pool, tile)
                    update.wait_stored(pool)

        many = nc.values_load(flag[0:1, 0:1], min_val=0, max_val=1)
        for l in range(layers):
            last = l == layers - 1
            if last:
                close_scope()
            open_scope()
            update = NodeUpdate(nc, l, last, sb, sem, (nodes, tiles, dim), (res_table, parts_table, x, x2_table),
                                dis, both_w, bias_sum, ident, bank[0], bank[1])
            with nc.If(many == 0):
                if l == 0:
                    count_and_sum(update)
                else:
                    open_scope()
                    sum_by_counts(update, sb("counts_again", [P, 2, tiles, 2 * P], BF16))
                    close_scope()
            with nc.Else():
                messages_to_table(l)
                gather_sum(l)
                update_from_table(update)
            close_scope()
        close_scope()

        features = sb("features", [P, tiles, dim], F32)
        w2_sb = sb("w2_sb", [P, experts, K2, dim], F32)
        w3_sb = sb("w3_sb", [P, experts, K2, dim], F32)
        b3_sb = sb("b3_sb", [P, experts, dim], F32)
        y = sb("y", [P, GROUP, dim], F32)
        y_t = sb("y_t", [P, 2, K2, GROUP * P], F32)
        router_t = sb("router_t", [P, GROUP * P], F32)
        h1_t = sb("h1_t", [P, 2, K2, GROUP * P], F32)
        h2_t = sb("h2_t", [P, 2, K2, GROUP * P], F32)
        acc = sb("acc", [P, GROUP, dim], F32)
        g_stats = sb("g_stats", [P, GROUP, 6], F32)
        g_a = sb("g_a", [P, GROUP], F32)
        g_d = sb("g_d", [P, GROUP], F32)
        g_s = sb("g_s", [P, GROUP], F32)
        g_mean = sb("g_mean", [P, GROUP], F32)
        g_rstd = sb("g_rstd", [P, GROUP], F32)
        rank = sb("rank", [P, experts], F32)
        top = sb("top", [P, 6, GROUP], F32)
        prob = sb("prob", [P, GROUP, experts], F32)
        pick = sb("pick", [P, 3, GROUP, experts], F32)
        gate = sb("gate", [P, GROUP, experts], F32)

        w2_loaded = sem("w2_loaded")
        w3_loaded = sem("w3_loaded")
        group_loaded = sem("group_loaded")
        features_back = sem("features_back")
        first_group_loaded = sem("first_group_loaded")
        ffn_link = sem("ffn_link")
        ffn_var = sem("ffn_var")
        ffn_std = sem("ffn_std")
        y_ready = sem("y_ready")
        item_ready = sem("item_ready")
        act_out = sem("act_out")
        dve_out = sem("dve_out")
        logits_ready = sem("logits_ready")
        logits_used = sem("logits_used")
        shifted = sem("shifted")
        exped = sem("exped")
        gap_ready = sem("gap_ready")
        gap_exped = sem("gap_exped")
        outs_ready = sem("outs_ready")
        outs_used = sem("outs_used")
        acc_stored = sem("acc_stored")
        acc_free = sem("acc_free")
        acc_ready = sem("acc_ready")
        rank_made = sem("rank_made")

        RING = 3
        ring, out_bank, logit_bank = bank[0:3], bank[3:7], bank[7]
        def layer_items(kind, e):
            return [(kind, e, m, n) for m in range(K2) for n in range(2)]

        turn_items = [("turn", k, n) for k in range(K2) for n in range(2)]
        route_items = [("route", 0, n) for n in range(2)]
        prep_items = turn_items + route_items + layer_items("h1", 0)
        PREP = len(prep_items)

        def of_next(it):
            return it in prep_items

        def spread(few, many):
            return [it for k, m in enumerate(many) for it in [m] + few[k:k + 1]]

        def group_items(last):
            stages = []
            for e in range(experts):
                first_layer = layer_items("h1", e + 1) if e + 1 < experts else [] if last else layer_items("h1", 0)
                if e == 3 and not last:
                    first_layer = spread(turn_items, first_layer)
                if e == 4 and not last:
                    first_layer = spread(route_items, first_layer)
                stages.append(layer_items("h2", e) + first_layer)
            return stages

        ITEMS = sum(len(stage) for stage in group_items(False))
        FREE = 2
        assert ITEMS % (2 * RING) == 0 and PREP % 2 == 0 and groups % 2 == 1
        OUTS = experts * 4

        def numbered(last):
            k = 0
            for e, stage in enumerate(group_items(last)):
                for it in stage:
                    yield e, k, it
                    k += 1

        def wait_emptied(eng, g, k):
            eng.wait_ge((act_out, dve_out)[k % 2], g * (ITEMS // 2) + (FREE + (PREP + k) // 2 + 1))

        def wait_all_emptied(pe, g, k):
            wait_emptied(pe, g, k)
            wait_emptied(pe, g, k - 1)

        def cols_of(n):
            return slice(n * HALF, (n + 1) * HALF)

        def over_groups(eng, body):
            with eng.Fori(0, groups // 2) as j:
                body(j * 2, 0, False)
                body(j * 2 + 1, 1, False)
            body(groups - 1, 0, True)

        BEFORE = 0

        with nc.Block() as block:
            @block.tensor
            def _(pe):
                def item(g, b, k, it):
                    dstb = ring[(PREP + k) % RING]
                    wait_emptied(pe, g, k - RING)
                    if it[0] == "turn":
                        _, kf, n = it
                        ts = range(4) if n == 0 else range(4, GROUP)
                        for j, t in enumerate(ts):
                            mm = nc.tensor.transpose(dstb[:, j * P:(j + 1) * P], y[:, t, kf * P:(kf + 1) * P], ident[:, :])
                    elif it[0] == "route":
                        for kf in range(K2):
                            mm = nc.tensor.matmul(dstb[:, 0:HALF], router_w1_sb[:, kf, :], y_t[:, b, kf, cols_of(it[2])], start=kf == 0, stop=kf == K2 - 1)
                    else:
                        kind, e, m, n = it
                        w, source = (w1_sb, y_t[:, b, :, :]) if kind == "h1" else (w2_sb, h1_t[:, e % 2, :, :])
                        for kf in range(K2):
                            mm = nc.tensor.matmul(dstb[:, 0:HALF], w[:, e, kf, m * P:(m + 1) * P], source[:, kf, cols_of(n)], start=kf == 0, stop=kf == K2 - 1)
                    mm.then_inc(item_ready, 1)

                def outs(g, e):
                    for q in range(4):
                        pe.wait_ge(outs_used, g * OUTS + (e * 4 + q + 1))
                        for t in range(2 * q, min(2 * q + 2, GROUP)):
                            o = out_bank[q][:, (t % 2) * dim:(t % 2 + 1) * dim]
                            for kf in range(K2):
                                mm = nc.tensor.matmul(o, h2_t[:, e % 2, kf, t * P:(t + 1) * P], w3_sb[:, e, kf, :], start=kf == 0, stop=kf == K2 - 1)
                        mm.then_inc(outs_ready, 1)

                def logits(n):
                    pe.wait_ge(logits_used, n + 1)
                    for t in range(GROUP):
                        o = logit_bank[:, t * experts:(t + 1) * experts]
                        mm = nc.tensor.matmul(o, router_t[:, t * P:(t + 1) * P], router_w2_sb[:, :], start=True, stop=True)
                    mm.then_inc(logits_ready, 1)

                def group(g, b, last):
                    last_of = {(it[0], it[1]): k for e, k, it in numbered(last)}
                    stages = list(numbered(last))
                    for e in range(experts):
                        for _e, k, it in [s for s in stages if s[0] == e]:
                            if it == ("h2", 0, 0, 0):
                                pe.wait_ge(w2_loaded, 16)
                            if it[2:] == (0, 0) and it[0] == "h2":
                                wait_all_emptied(pe, g, last_of["h1", e] if e else -1)
                            if it == ("turn", 0, 0):
                                pe.wait_ge(y_ready, g + 2)
                            if it == ("route", 0, 0):
                                wait_all_emptied(pe, g, last_of["turn", K2 - 1])
                            item(g, 1 - b if of_next(it) else b, k, it)
                        if e == 0:
                            pe.wait_ge(w3_loaded, 32)
                        wait_all_emptied(pe, g, last_of["h2", e])
                        outs(g, e)
                        if e == 4 and not last:
                            wait_all_emptied(pe, g, last_of["route", 0])
                            logits(g + 1)

                pe.wait_ge(first_w_loaded, FIRST_W)
                pe.wait_ge(y_ready, 1)
                for k, it in enumerate(prep_items):
                    if k == len(turn_items):
                        wait_all_emptied(pe, BEFORE, k - 1 - PREP)
                    item(BEFORE, 0, k - PREP, it)
                wait_all_emptied(pe, BEFORE, len(turn_items + route_items) - 1 - PREP)
                logits(0)
                over_groups(pe, group)

            def empty(eng, g, b, k, it):
                frm_bank = ring[(PREP + k) % RING]
                eng.wait_ge(item_ready, g * ITEMS + (PREP + k + 1))
                if it[0] == "turn":
                    n = 4 * P if it[2] == 0 else (GROUP - 4) * P
                    to, bias, frm = y_t[:, b, it[1], it[2] * 4 * P:it[2] * 4 * P + n], None, frm_bank[:, 0:n]
                elif it[0] == "route":
                    to, bias, frm = router_t[:, cols_of(it[2])], router_b1_sb[:, 0:1], frm_bank[:, 0:HALF]
                else:
                    kind, e, m, n = it
                    h, bb = (h1_t, b1_sb) if kind == "h1" else (h2_t, b2_sb)
                    to, bias, frm = h[:, e % 2, m, cols_of(n)], bb[:, e, m:m + 1], frm_bank[:, 0:HALF]
                if k % 2 == 0:
                    if bias is None:
                        ins = nc.scalar.activation(to, frm, ACT.Copy)
                    else:
                        ins = nc.scalar.activation(to, frm, ACT.Relu, bias=bias)
                    ins.then_inc(act_out, 1)
                else:
                    if bias is None:
                        ins = nc.vector.tensor_copy(to, frm)
                    else:
                        ins = nc.vector.tensor_scalar(to, frm, bias, 0.0, ALU.add, ALU.max)
                    ins.then_inc(dve_out, 1)

            @block.scalar
            def _(act):
                def deviation(n):
                    act.wait_ge(ffn_var, n + 1)
                    nc.scalar.activation(g_rstd[:, :], g_s[:, :], ACT.Sqrt, bias=eps_col[:, 0:1], scale=1.0 / dim).then_inc(ffn_std, 1)

                def group(g, b, last):
                    for e, k, it in numbered(last):
                        if k % 2 == 0:
                            empty(act, g, 1 - b if of_next(it) else b, k, it)
                        if k == 2:
                            act.wait_ge(shifted, g + 1)
                            nc.scalar.activation(prob[:, :, :], prob[:, :, :], ACT.Exp).then_inc(exped, 1)
                        if k == 6:
                            act.wait_ge(gap_ready, g + 1)
                            nc.scalar.activation(top[:, 4, :], top[:, 4, :], ACT.Exp).then_inc(gap_exped, 1)
                        if k == 14 and not last:
                            deviation(g + 1)

                act.sem_inc(act_out, FREE)
                act.wait_ge(first_w_loaded, FIRST_W)
                deviation(0)
                for k in range(0, PREP, 2):
                    empty(act, BEFORE, 0, k - PREP, prep_items[k])
                over_groups(act, group)

            @block.vector
            def _(dve):
                link = Link(dve, ffn_link)

                def row_stats(n, ts):
                    for t in ts:
                        nc.vector.bn_stats(g_stats[:, t, :], features[:, bass.ds(n * GROUP + t, 1), :].rearrange("p a d -> p (a d)")).then_inc(ffn_link, 1)
                        link.count += 1

                def variance():
                    link.wait()
                    st = g_stats[:, :, :]
                    link(nc.vector.tensor_tensor(g_a[:, :], st[:, :, 1], st[:, :, 4], ALU.add))
                    link(nc.vector.tensor_tensor(g_d[:, :], st[:, :, 1], st[:, :, 4], ALU.subtract))
                    link(nc.vector.tensor_tensor(g_s[:, :], st[:, :, 2], st[:, :, 5], ALU.add))
                    link(nc.vector.tensor_tensor(g_d[:, :], g_d[:, :], g_d[:, :], ALU.mult))
                    link(nc.vector.tensor_scalar(g_mean[:, :], g_a[:, :], 0.5, None, ALU.mult))
                    nc.vector.scalar_tensor_tensor(g_s[:, :], g_d[:, :], dim / 4.0, g_s[:, :], ALU.mult, ALU.add).then_inc(ffn_var, 1)

                def inverse(n):
                    dve.wait_ge(ffn_std, n + 1)
                    link(nc.vector.reciprocal(g_rstd[:, :], g_rstd[:, :]))

                def normal_rows(n, ts):
                    for t in ts:
                        ins = nc.vector.tensor_scalar(y[:, t, :], features[:, bass.ds(n * GROUP + t, 1), :].rearrange("p a d -> p (a d)"),
                                                      g_mean[:, t:t + 1], g_rstd[:, t:t + 1], ALU.subtract, ALU.mult)
                    if GROUP - 1 in ts:
                        ins.then_inc(y_ready, 1)

                def wide(v):
                    return v.unsqueeze(2).to_broadcast([P, GROUP, experts])

                ranks = rank[:, :].unsqueeze(1).to_broadcast([P, GROUP, experts])

                def largest(i):
                    link(nc.vector.tensor_reduce(top[:, 1 + i, :], prob[:, :, :], AX, ALU.max))
                    link(nc.vector.tensor_tensor(pick[:, 2, :, :], prob[:, :, :], wide(top[:, 1 + i, :]), ALU.is_equal))
                    link(nc.vector.tensor_tensor(pick[:, 2, :, :], pick[:, 2, :, :], ranks, ALU.mult))
                    link(nc.vector.tensor_reduce(top[:, 3, :], pick[:, 2, :, :], AX, ALU.max))
                    link(nc.vector.tensor_tensor(pick[:, i, :, :], ranks, wide(top[:, 3, :]), ALU.is_equal))

                def shift_logits(g):
                    logits = logit_bank[:, 0:GROUP * experts].rearrange("p (t e) -> p t e", e=experts)
                    dve.wait_ge(logits_ready, g + 1)
                    link(nc.vector.tensor_tensor(prob[:, :, :], logits, router_b2_sb[:, :].unsqueeze(1).to_broadcast([P, GROUP, experts]), ALU.add))
                    dve.sem_inc(logits_used, 1)
                    link(nc.vector.tensor_reduce(top[:, 0, :], prob[:, :, :], AX, ALU.max))
                    nc.vector.tensor_tensor(prob[:, :, :], prob[:, :, :], wide(top[:, 0, :]), ALU.subtract).then_inc(shifted, 1)

                def first_choice(g):
                    dve.wait_ge(exped, g + 1)
                    link(nc.vector.tensor_reduce(top[:, 0, :], prob[:, :, :], AX, ALU.add))
                    link(nc.vector.reciprocal(top[:, 0, :], top[:, 0, :]))
                    link(nc.vector.tensor_tensor(prob[:, :, :], prob[:, :, :], wide(top[:, 0, :]), ALU.mult))
                    largest(0)

                def second_choice():
                    link(nc.vector.scalar_tensor_tensor(prob[:, :, :], pick[:, 0, :, :], -4.0, prob[:, :, :], ALU.mult, ALU.add))
                    largest(1)
                    nc.vector.tensor_tensor(top[:, 4, :], top[:, 2, :], top[:, 1, :], ALU.subtract).then_inc(gap_ready, 1)

                def gates(g):
                    dve.wait_ge(gap_exped, g + 1)
                    link(nc.vector.tensor_scalar(top[:, 0, :], top[:, 4, :], 1.0, None, ALU.add))
                    link(nc.vector.reciprocal(top[:, 0, :], top[:, 0, :]))
                    link(nc.vector.tensor_tensor(top[:, 5, :], top[:, 4, :], top[:, 0, :], ALU.mult))
                    link(nc.vector.tensor_tensor(pick[:, 0, :, :], pick[:, 0, :, :], wide(top[:, 0, :]), ALU.mult))
                    link(nc.vector.tensor_tensor(pick[:, 1, :, :], pick[:, 1, :, :], wide(top[:, 5, :]), ALU.mult))
                    link(nc.vector.tensor_tensor(gate[:, :, :], pick[:, 0, :, :], pick[:, 1, :, :], ALU.add))

                def accumulate(g, e):
                    if e == 0:
                        dve.wait_ge(w3_loaded, 32)
                        dve.wait_ge(acc_free, g + 1)
                    for t in range(GROUP):
                        before = acc[:, t, :] if e else features[:, bass.ds(g * GROUP + t, 1), :].rearrange("p a d -> p (a d)")
                        ins = nc.vector.scalar_tensor_tensor(acc[:, t, :], b3_sb[:, e, :], gate[:, t, e:e + 1], before, ALU.mult, ALU.add)
                    link(ins)
                    for q in range(4):
                        dve.wait_ge(outs_ready, g * OUTS + (e * 4 + q + 1))
                        for t in range(2 * q, min(2 * q + 2, GROUP)):
                            o = out_bank[q][:, (t % 2) * dim:(t % 2 + 1) * dim]
                            ins = nc.vector.scalar_tensor_tensor(acc[:, t, :], o, gate[:, t, e:e + 1], acc[:, t, :], ALU.mult, ALU.add)
                        link(ins)
                        dve.sem_inc(outs_used, 1)

                def group(g, b, last):
                    stages = list(numbered(last))
                    for e in range(experts):
                        for _e, k, it in [s for s in stages if s[0] == e]:
                            if k % 2 == 1:
                                empty(dve, g, 1 - b if of_next(it) else b, k, it)
                            if k == 1:
                                shift_logits(g)
                            if k == 3:
                                first_choice(g)
                            if k == 5:
                                second_choice()
                            if k == 7:
                                gates(g)
                            if not last:
                                if k == 9:
                                    dve.wait_ge(features_back, g + 1)
                                    row_stats(g + 1, range(0, 4))
                                if k == 11:
                                    row_stats(g + 1, range(4, GROUP))
                                if k == 13:
                                    variance()
                                if k == 15:
                                    inverse(g + 1)
                                    normal_rows(g + 1, range(0, 4))
                                if k == 17:
                                    normal_rows(g + 1, range(4, GROUP))
                        accumulate(g, e)
                    dve.sem_inc(acc_ready, 1)

                for j in range(experts):
                    nc.vector.memset(rank[:, j:j + 1], float(experts - j)).then_inc(rank_made, 1)
                dve.wait_ge(rank_made, experts)
                dve.wait_ge(first_w_loaded, FIRST_W)
                dve.sem_inc(dve_out, FREE)
                dve.sem_inc(outs_used, 4)
                dve.sem_inc(acc_free, 1)
                dve.sem_inc(logits_used, 1)
                dve.wait_ge(first_group_loaded, 16)
                row_stats(0, range(GROUP))
                variance()
                inverse(0)
                normal_rows(0, range(GROUP))
                for k in range(1, PREP, 2):
                    empty(dve, BEFORE, 0, k - PREP, prep_items[k])
                with dve.Fori(0, groups // 2) as j:
                    link.loop(j, 2 * LINKS_PER_GROUP)
                    group(j * 2, 0, False)
                    group(j * 2 + 1, 1, False)
                link.end(groups // 2)
                group(groups - 1, 0, True)

            @block.gpsimd
            def _(pool):
                with pool.Fori(1, groups) as g:
                    pool.dma_start(features[:, bass.ds(g * GROUP, GROUP), :], x2_table[bass.ds(g * (GROUP * P), GROUP * P), :].rearrange("(t p) d -> p t d", p=P)).then_inc(group_loaded, 16)
                    pool.wait_ge(group_loaded, g * 16)
                    pool.sem_inc(features_back, 1)

            @block.sync
            def _(sp):
                sp.dma_start(features[:, 0:GROUP, :], x2_table[0:GROUP * P, :].rearrange("(t p) d -> p t d", p=P)).then_inc(first_group_loaded, 16)
                sp.dma_start(w2_sb[:, :, :, :].rearrange("p e k d -> p (e k) d"), expert_w2.rearrange("e (k p) d -> p (e k) d", p=P)).then_inc(w2_loaded, 16)
                sp.dma_start(w3_sb[:, :, :, :].rearrange("p e k d -> p (e k) d"), expert_w3.rearrange("e (k p) d -> p (e k) d", p=P)).then_inc(w3_loaded, 16)
                sp.dma_start(b3_sb[:, :, :], expert_b3.partition_broadcast(P)).then_inc(w3_loaded, 16)
                with sp.Fori(0, groups - 1) as g:
                    sp.wait_ge(acc_ready, g + 1)
                    sp.dma_start(out[bass.ds(g * (GROUP * P), GROUP * P), :].rearrange("(t p) d -> p t d", p=P), acc[:, :, :]).then_inc(acc_stored, 16)
                    sp.wait_ge(acc_stored, 16 * g + 16)
                    sp.sem_inc(acc_free, 1)
                g = groups - 1
                sp.wait_ge(acc_ready, groups)
                sp.dma_start(out[g * GROUP * P:full, :].rearrange("(t p) d -> p t d", p=P), acc[:, 0:GROUP - 1, :]).then_inc(acc_stored, 16)
                sp.dma_start(out[full:nodes, :], acc[0:last_rows, GROUP - 1, :]).then_inc(acc_stored, 16)
                sp.wait_ge(acc_stored, 16 * (groups + 1))


LINKS_PER_GROUP = (2 + 3 + 11 + 6) + (7 + 5 + 1) + 30

_INS = ['x', 'src', 'dst', 'L0_gnn_W', 'L0_gnn_b', 'L0_gnn_resW', 'L0_gnn_resb', 'L0_ffn_router_w1', 'L0_ffn_router_b1',
        'L0_ffn_router_w2', 'L0_ffn_router_b2', 'L0_ffn_expert_w1', 'L0_ffn_expert_b1', 'L0_ffn_expert_w2', 'L0_ffn_expert_b2',
        'L0_ffn_expert_w3', 'L0_ffn_expert_b3']


def kernel(**inputs):
    import numpy as _np
    import concourse.bacc as _bacc
    from concourse import mybir as _mybir
    from concourse.bass_utils import run_bass_kernel_spmd as _run

    nc = _bacc.Bacc("TRN2", target_bir_lowering=False, num_devices=1)
    arrays, args = {}, []
    for name in _INS:
        a = _np.ascontiguousarray(inputs[name])
        arrays[f"in_{name}_dram"] = a
        args.append(nc.dram_tensor(f"in_{name}_dram", a.shape, _mybir.dt.from_np(a.dtype), kind="ExternalInput").ap())
    shape = inputs['x'].shape
    args.append(nc.dram_tensor("out_dram", shape, _mybir.dt.float32, kind="ExternalOutput").ap())
    gnn_moe_kernel(nc, *args)
    r = _run(nc, [arrays], core_ids=[0])
    return r.results[0]["out_dram"]
```
